# Optimizing a Trainium2 kernel written in Bass

```python
import numpy as np
import jax
import jax.numpy as jnp

def _softmax(x, axis=-1):
    return jax.nn.softmax(x, axis=axis)

def _gelu(x):
    return jax.nn.gelu(x, approximate=True)

def _silu(x):
    return jax.nn.silu(x)

def _sigmoid(x):
    return jax.nn.sigmoid(x)

def _layernorm(x, axis=-1, eps=1e-05):
    m = jnp.mean(x, axis=axis, keepdims=True)
    v = jnp.var(x, axis=axis, keepdims=True)
    return (x - m) / jnp.sqrt(v + eps)

def _scatter_add(tgt, idx, src, axis=0):
    return tgt.at[idx].add(src)

def _segment_sum(src, seg, n):
    return jax.ops.segment_sum(src, seg, n)
kernel_name = 'mk_decoder_preln_d2_seqx_r2_374cda'

def setup_inputs(seed: int=0):
    np.random.seed(seed)
    _w = jnp.asarray

    def _rec_inputs():
        import jax
        import jax.numpy as jnp
        _rk = jax.random.key(seed)
        x = 7.22e-05 + 1 * jax.random.normal(jax.random.fold_in(_rk, 1), (16, 256, 512), jnp.float32)
        _lenS = 256 - jax.random.randint(jax.random.fold_in(_rk, 7), (16,), 0, max(1, 256 // 4) + 1, jnp.int32)
        _lenS2 = 256 - jax.random.randint(jax.random.fold_in(_rk, 8), (16,), 0, max(1, 256 // 4) + 1, jnp.int32)
        _ctx_1024P = jax.random.normal(jax.random.fold_in(_rk, 11), (16, 16, 512), jnp.float32)
        _ctx_1024c = jax.random.dirichlet(jax.random.fold_in(_rk, 511), 0.3 * jnp.ones((16,), jnp.float32), (16, 256))
        _ctx_1024t = jnp.einsum('bsk,bkd->bsd', _ctx_1024c, _ctx_1024P)
        _ctx_1024t = _ctx_1024t * jax.lax.rsqrt(jnp.mean(jnp.square(_ctx_1024t)) + 1e-12) * 0.953939
        ctx_1024 = 4.13588e-05 + 0.999923 * (_ctx_1024t + 0.3 * jax.random.normal(jax.random.fold_in(_rk, 611), (16, 256, 512), jnp.float32))
        return (x, ctx_1024)
    x, ctx_1024 = _rec_inputs()

    def _L0_attn_setup():
        import jax, jax.numpy as jnp
        import numpy as np
        D_MODEL = 512
        N_HEADS = 16
        D_HEAD = 64
        ROTARY_DIM = 64
        ROTARY_BASE = 10000.0
        ATTN_SCALE = 8.0

        def _rope_sin_cos(n_pos, rotary_dim):
            pos = jnp.arange(n_pos, dtype=jnp.float32)
            dim = jnp.arange(rotary_dim // 2, dtype=jnp.float32)
            freq = ROTARY_BASE ** (dim / (rotary_dim / 2))
            freq = jnp.concatenate([freq, freq])
            angles = pos[:, None] / freq[None, :]
            return (jnp.sin(angles), jnp.cos(angles))

        def _apply_rotary(x, sin, cos):
            n = x.shape[-1] // 2
            x_flip = jnp.concatenate([-x[..., n:], x[..., :n]], axis=-1)
            return x * cos[None, :, None, :] + x_flip * sin[None, :, None, :]
        key = jax.random.key(seed)
        ks = jax.random.split(key, 9)
        std = 0.02
        x = jax.random.normal(ks[0], (2, 1024, D_MODEL), dtype=jnp.float32)
        W_Q = jax.random.normal(ks[1], (N_HEADS, D_MODEL, D_HEAD), dtype=jnp.float32) * std
        W_K = jax.random.normal(ks[2], (N_HEADS, D_MODEL, D_HEAD), dtype=jnp.float32) * std
        W_V = jax.random.normal(ks[3], (N_HEADS, D_MODEL, D_HEAD), dtype=jnp.float32) * std
        W_O = jax.random.normal(ks[4], (N_HEADS, D_HEAD, D_MODEL), dtype=jnp.float32) * std
        b_Q = jnp.zeros((N_HEADS, D_HEAD), dtype=jnp.float32)
        b_K = jnp.zeros((N_HEADS, D_HEAD), dtype=jnp.float32)
        b_V = jnp.zeros((N_HEADS, D_HEAD), dtype=jnp.float32)
        b_O = jnp.zeros((D_MODEL,), dtype=jnp.float32)
        return {'x': x, 'W_Q': W_Q, 'b_Q': b_Q, 'W_K': W_K, 'b_K': b_K, 'W_V': W_V, 'b_V': b_V, 'W_O': W_O, 'b_O': b_O}
    _L0_attn_all = _L0_attn_setup()
    _L0_attn_in = {k: v for k, v in _L0_attn_all.items() if k in ('W_Q', 'b_Q', 'W_K', 'b_K', 'W_V', 'b_V', 'W_O', 'b_O')}
    del _L0_attn_all

    def _L0_xattn_setup():
        import jax, jax.numpy as jnp
        import numpy as np
        N_HEADS = 16
        D_MODEL = 512
        D_K = D_MODEL // N_HEADS
        NEG_INF = -1000000000.0

        def _split_heads(x):
            B, S, _ = x.shape
            return x.reshape(B, S, N_HEADS, D_K).transpose(0, 2, 1, 3)
        key = jax.random.key(seed)
        ks = jax.random.split(key, 7)
        B, S, D = (4, 1024, D_MODEL)
        scale = 1.0 / np.sqrt(D)
        return {'query': jax.random.normal(ks[0], (B, S, D), dtype=jnp.float32), 'key': jax.random.normal(ks[1], (B, S, D), dtype=jnp.float32), 'value': jax.random.normal(ks[2], (B, S, D), dtype=jnp.float32), 'Wq': jax.random.normal(ks[3], (D, D), dtype=jnp.float32) * scale, 'Wk': jax.random.normal(ks[4], (D, D), dtype=jnp.float32) * scale, 'Wv': jax.random.normal(ks[5], (D, D), dtype=jnp.float32) * scale, 'Wo': jax.random.normal(ks[6], (D, D), dtype=jnp.float32) * scale}
    _L0_xattn_all = _L0_xattn_setup()
    _L0_xattn_in = {k: v for k, v in _L0_xattn_all.items() if k in ('Wq', 'Wk', 'Wv', 'Wo')}
    del _L0_xattn_all

    def _L0_ffn_setup():
        import jax, jax.numpy as jnp
        import numpy as np
        B, S, D, E, H, K = (64, 1024, 512, 32, 2048, 8)
        key = jax.random.key(seed)
        k0, k1, k2, k3 = jax.random.split(key, 4)
        x = jax.random.normal(k0, (B, S, D), jnp.float32)
        gate_w = jax.random.normal(k1, (E, D), jnp.float32) * (1.0 / np.sqrt(D))
        gate_b = jnp.zeros((E,), jnp.float32)
        w1 = jax.random.normal(k2, (E, D + 1, H), jnp.float32) * (1.0 / np.sqrt(D + 1))
        w2 = jax.random.normal(k3, (E, H + 1, D), jnp.float32) * (1.0 / np.sqrt(H + 1))
        return {'x': x, 'gate_w': gate_w, 'gate_b': gate_b, 'w1': w1, 'w2': w2}
    _L0_ffn_all = _L0_ffn_setup()
    _L0_ffn_in = {k: v for k, v in _L0_ffn_all.items() if k in ('gate_w', 'gate_b', 'w1', 'w2')}
    del _L0_ffn_all

    def _L1_attn_setup():
        import jax, jax.numpy as jnp
        import numpy as np
        key = jax.random.key(seed)
        ks = jax.random.split(key, 7)
        B, S, D = (4, 4096, 512)
        sc = 1.0 / np.sqrt(D)
        return {'x': jax.random.normal(ks[0], (B, S, D), dtype=jnp.float32), 'Wq': jax.random.normal(ks[1], (D, D), dtype=jnp.float32) * sc, 'bq': jnp.zeros((D,), dtype=jnp.float32), 'Wk': jax.random.normal(ks[2], (D, D), dtype=jnp.float32) * sc, 'bk': jnp.zeros((D,), dtype=jnp.float32), 'Wv': jax.random.normal(ks[3], (D, D), dtype=jnp.float32) * sc, 'bv': jnp.zeros((D,), dtype=jnp.float32)}
    _L1_attn_all = _L1_attn_setup()
    _L1_attn_in = {k: v for k, v in _L1_attn_all.items() if k in ('Wq', 'bq', 'Wk', 'bk', 'Wv', 'bv')}
    del _L1_attn_all

    def _L1_xattn_setup():
        import jax, jax.numpy as jnp
        import numpy as np
        D_MODEL = 512
        NUM_HEADS = 16
        D_K = D_MODEL // NUM_HEADS
        key = jax.random.key(seed)
        ks = jax.random.split(key, 8)
        B, S, D = (4, 1024, D_MODEL)
        scale = 1.0 / np.sqrt(D)
        return {'query': jax.random.normal(ks[0], (B, S, D), dtype=jnp.float32), 'key': jax.random.normal(ks[1], (B, S, D), dtype=jnp.float32), 'value': jax.random.normal(ks[2], (B, S, D), dtype=jnp.float32), 'Wq': jax.random.normal(ks[3], (D, D), dtype=jnp.float32) * scale, 'bq': jnp.zeros((D,), dtype=jnp.float32), 'Wk': jax.random.normal(ks[4], (D, D), dtype=jnp.float32) * scale, 'bk': jnp.zeros((D,), dtype=jnp.float32), 'Wv': jax.random.normal(ks[5], (D, D), dtype=jnp.float32) * scale, 'bv': jnp.zeros((D,), dtype=jnp.float32), 'Wo': jax.random.normal(ks[6], (D, D), dtype=jnp.float32) * scale, 'bo': jnp.zeros((D,), dtype=jnp.float32)}
    _L1_xattn_all = _L1_xattn_setup()
    _L1_xattn_in = {k: v for k, v in _L1_xattn_all.items() if k in ('Wq', 'bq', 'Wk', 'bk', 'Wv', 'bv', 'Wo', 'bo')}
    del _L1_xattn_all

    def _L1_ffn_setup():
        import jax, jax.numpy as jnp
        import numpy as np
        FP8_MAX = 448.0
        SCALE = 1.0
        _FP8_DTYPE = getattr(jnp, 'float8_e4m3fn', jnp.float16)

        def quantize_e4m3(t, scale):
            return jnp.clip(t / scale, -FP8_MAX, FP8_MAX).astype(_FP8_DTYPE)
        key = jax.random.key(seed)
        kx, kw = jax.random.split(key)
        B, N, C, F = (8, 2048, 512, 512)
        x = jax.random.normal(kx, (B, N, C), dtype=jnp.float32)
        weight = jax.random.normal(kw, (F, C), dtype=jnp.float32) * 0.02
        bias = jnp.zeros((F,), dtype=jnp.float32)
        return {'x': x, 'weight': weight, 'bias': bias}
    _L1_ffn_all = _L1_ffn_setup()
    _L1_ffn_in = {k: v for k, v in _L1_ffn_all.items() if k in ('weight', 'bias')}
    del _L1_ffn_all
    return {'x': x, 'ctx_1024': ctx_1024, 'L0_attn_W_Q': _L0_attn_in['W_Q'], 'L0_attn_b_Q': _L0_attn_in['b_Q'], 'L0_attn_W_K': _L0_attn_in['W_K'], 'L0_attn_b_K': _L0_attn_in['b_K'], 'L0_attn_W_V': _L0_attn_in['W_V'], 'L0_attn_b_V': _L0_attn_in['b_V'], 'L0_attn_W_O': _L0_attn_in['W_O'], 'L0_attn_b_O': _L0_attn_in['b_O'], 'L0_xattn_Wq': _L0_xattn_in['Wq'], 'L0_xattn_Wk': _L0_xattn_in['Wk'], 'L0_xattn_Wv': _L0_xattn_in['Wv'], 'L0_xattn_Wo': _L0_xattn_in['Wo'], 'L0_ffn_gate_w': _L0_ffn_in['gate_w'], 'L0_ffn_gate_b': _L0_ffn_in['gate_b'], 'L0_ffn_w1': _L0_ffn_in['w1'], 'L0_ffn_w2': _L0_ffn_in['w2'], 'L1_attn_Wq': _L1_attn_in['Wq'], 'L1_attn_bq': _L1_attn_in['bq'], 'L1_attn_Wk': _L1_attn_in['Wk'], 'L1_attn_bk': _L1_attn_in['bk'], 'L1_attn_Wv': _L1_attn_in['Wv'], 'L1_attn_bv': _L1_attn_in['bv'], 'L1_xattn_Wq': _L1_xattn_in['Wq'], 'L1_xattn_bq': _L1_xattn_in['bq'], 'L1_xattn_Wk': _L1_xattn_in['Wk'], 'L1_xattn_bk': _L1_xattn_in['bk'], 'L1_xattn_Wv': _L1_xattn_in['Wv'], 'L1_xattn_bv': _L1_xattn_in['bv'], 'L1_xattn_Wo': _L1_xattn_in['Wo'], 'L1_xattn_bo': _L1_xattn_in['bo'], 'L1_ffn_weight': _L1_ffn_in['weight'], 'L1_ffn_bias': _L1_ffn_in['bias']}

def reference(x, ctx_1024, L0_attn_W_Q, L0_attn_b_Q, L0_attn_W_K, L0_attn_b_K, L0_attn_W_V, L0_attn_b_V, L0_attn_W_O, L0_attn_b_O, L0_xattn_Wq, L0_xattn_Wk, L0_xattn_Wv, L0_xattn_Wo, L0_ffn_gate_w, L0_ffn_gate_b, L0_ffn_w1, L0_ffn_w2, L1_attn_Wq, L1_attn_bq, L1_attn_Wk, L1_attn_bk, L1_attn_Wv, L1_attn_bv, L1_xattn_Wq, L1_xattn_bq, L1_xattn_Wk, L1_xattn_bk, L1_xattn_Wv, L1_xattn_bv, L1_xattn_Wo, L1_xattn_bo, L1_ffn_weight, L1_ffn_bias):
    import jax
    import jax.numpy as jnp

    def _L0_attn_ref(x, W_Q, b_Q, W_K, b_K, W_V, b_V, W_O, b_O):
        import jax, jax.numpy as jnp
        import numpy as np
        D_MODEL = 512
        N_HEADS = 16
        D_HEAD = 64
        ROTARY_DIM = 64
        ROTARY_BASE = 10000.0
        ATTN_SCALE = 8.0

        def _rope_sin_cos(n_pos, rotary_dim):
            pos = jnp.arange(n_pos, dtype=jnp.float32)
            dim = jnp.arange(rotary_dim // 2, dtype=jnp.float32)
            freq = ROTARY_BASE ** (dim / (rotary_dim / 2))
            freq = jnp.concatenate([freq, freq])
            angles = pos[:, None] / freq[None, :]
            return (jnp.sin(angles), jnp.cos(angles))

        def _apply_rotary(x, sin, cos):
            n = x.shape[-1] // 2
            x_flip = jnp.concatenate([-x[..., n:], x[..., :n]], axis=-1)
            return x * cos[None, :, None, :] + x_flip * sin[None, :, None, :]
        B, S, _ = x.shape
        q = jnp.einsum('bsd,hdk->bshk', x, W_Q) + b_Q
        k = jnp.einsum('bsd,hdk->bshk', x, W_K) + b_K
        v = jnp.einsum('bsd,hdk->bshk', x, W_V) + b_V
        sin, cos = _rope_sin_cos(S, ROTARY_DIM)
        q = _apply_rotary(q, sin, cos)
        k = _apply_rotary(k, sin, cos)
        scores = jnp.einsum('bqhd,bkhd->bhqk', q, k) / ATTN_SCALE
        causal = jnp.tril(jnp.ones((S, S), dtype=bool))
        scores = jnp.where(causal[None, None], scores, -jnp.inf)
        pattern = jax.nn.softmax(scores, axis=-1)
        pattern = jnp.where(jnp.isnan(pattern), jnp.zeros_like(pattern), pattern)
        z = jnp.einsum('bhqk,bkhd->bqhd', pattern, v)
        out = jnp.einsum('bqhd,hdm->bqm', z, W_O) + b_O
        return out

    def _L0_xattn_ref(query, key, value, Wq, Wk, Wv, Wo):
        import jax, jax.numpy as jnp
        import numpy as np
        N_HEADS = 16
        D_MODEL = 512
        D_K = D_MODEL // N_HEADS
        NEG_INF = -1000000000.0

        def _split_heads(x):
            B, S, _ = x.shape
            return x.reshape(B, S, N_HEADS, D_K).transpose(0, 2, 1, 3)
        B, S, D = query.shape
        Q = _split_heads(query @ Wq.T)
        K = _split_heads(key @ Wk.T)
        V = _split_heads(value @ Wv.T)
        scores = jnp.einsum('bhqd,bhkd->bhqk', Q, K) / jnp.sqrt(jnp.float32(D_K))
        causal = jnp.where(jnp.tril(jnp.ones((S, S), dtype=bool)), 0.0, NEG_INF).astype(scores.dtype)
        scores = scores + causal[None, None, :, :]
        attn = jax.nn.softmax(scores, axis=-1)
        heads = jnp.einsum('bhqk,bhkd->bhqd', attn, V)
        concat = heads.transpose(0, 2, 1, 3).reshape(B, S, D)
        out = concat @ Wo.T
        return out

    def _L0_ffn_ref(x, gate_w, gate_b, w1, w2):
        import jax, jax.numpy as jnp
        import numpy as np
        B, S, D, E, H, K = (64, 1024, 512, 32, 2048, 8)
        b, s, d = x.shape
        logits = jnp.einsum('bsd,ed->bse', x, gate_w) + gate_b
        probs = jax.nn.softmax(logits, axis=-2)
        vals_t, idx_t = jax.lax.top_k(probs.transpose(0, 2, 1), K)
        vals = vals_t.transpose(0, 2, 1)
        idx = idx_t.transpose(0, 2, 1)
        flat_idx = idx.reshape(b, K * E)
        tok = jnp.take_along_axis(x, flat_idx[:, :, None], axis=1)
        tok = tok.reshape(b, K, E, d)
        merged = jnp.einsum('bked,bke->bed', tok, vals)
        ones = jnp.ones(merged.shape[:-1] + (1,), merged.dtype)
        h = jnp.einsum('bei,eih->beh', jnp.concatenate([merged, ones], -1), w1)
        h = jax.nn.gelu(h, approximate=False)
        o = jnp.einsum('bej,ejo->beo', jnp.concatenate([h, ones], -1), w2)
        out_tok = jnp.einsum('beo,bke->bkeo', o, vals).reshape(b, K * E, d)
        out = jnp.zeros_like(x).at[jnp.arange(b)[:, None], flat_idx].add(out_tok)
        return out

    def _L1_attn_ref(x, Wq, bq, Wk, bk, Wv, bv):
        import jax, jax.numpy as jnp
        import numpy as np
        q = jnp.einsum('bsd,ed->bse', x, Wq) + bq
        k = jnp.einsum('bsd,ed->bse', x, Wk) + bk
        v = jnp.einsum('bsd,ed->bse', x, Wv) + bv
        q = q / jnp.linalg.norm(q, axis=-1, keepdims=True)
        k = k / jnp.linalg.norm(k, axis=-1, keepdims=True)
        kv = jnp.sum(k * v, axis=-2, keepdims=True)
        return q * kv

    def _L1_xattn_ref(query, key, value, Wq, bq, Wk, bk, Wv, bv, Wo, bo):
        import jax, jax.numpy as jnp
        import numpy as np
        D_MODEL = 512
        NUM_HEADS = 16
        D_K = D_MODEL // NUM_HEADS
        B, S, D = query.shape
        H, dk = (NUM_HEADS, D_K)

        def proj(x, W, b):
            y = jnp.einsum('bsd,ed->bse', x, W) + b
            return y.reshape(B, -1, H, dk).transpose(0, 2, 1, 3)
        Q = proj(query, Wq, bq)
        K = proj(key, Wk, bk)
        V = proj(value, Wv, bv)
        scores = jnp.einsum('bhqd,bhkd->bhqk', Q, K) / np.sqrt(dk).astype(jnp.float32)
        attn = jax.nn.softmax(scores, axis=-1)
        out = jnp.einsum('bhqk,bhkd->bhqd', attn, V)
        out = out.transpose(0, 2, 1, 3).reshape(B, -1, D)
        return jnp.einsum('bsd,ed->bse', out, Wo) + bo

    def _L1_ffn_ref(x, weight, bias):
        import jax, jax.numpy as jnp
        import numpy as np
        FP8_MAX = 448.0
        SCALE = 1.0
        _FP8_DTYPE = getattr(jnp, 'float8_e4m3fn', jnp.float16)

        def quantize_e4m3(t, scale):
            return jnp.clip(t / scale, -FP8_MAX, FP8_MAX).astype(_FP8_DTYPE)
        B, N, C = x.shape
        x2d = x.reshape(B * N, C)
        x_mat = quantize_e4m3(x2d, SCALE).astype(jnp.float16)
        w_mat = quantize_e4m3(weight, SCALE).astype(jnp.float16)
        out2d = (x_mat @ w_mat.T).astype(jnp.float32) * (SCALE * SCALE)
        out2d = out2d + bias
        return out2d.reshape(B, N, -1)
    x = x + _L0_attn_ref(_layernorm(x, axis=-1), L0_attn_W_Q, L0_attn_b_Q, L0_attn_W_K, L0_attn_b_K, L0_attn_W_V, L0_attn_b_V, L0_attn_W_O, L0_attn_b_O)
    x = x + _L0_xattn_ref(_layernorm(x, axis=-1), ctx_1024, ctx_1024, L0_xattn_Wq, L0_xattn_Wk, L0_xattn_Wv, L0_xattn_Wo)
    x = x + _L0_ffn_ref(_layernorm(x, axis=-1), L0_ffn_gate_w, L0_ffn_gate_b, L0_ffn_w1, L0_ffn_w2)
    x = x + _L1_attn_ref(_layernorm(x, axis=-1), L1_attn_Wq, L1_attn_bq, L1_attn_Wk, L1_attn_bk, L1_attn_Wv, L1_attn_bv)
    x = x + _L1_xattn_ref(_layernorm(x, axis=-1), ctx_1024, ctx_1024, L1_xattn_Wq, L1_xattn_bq, L1_xattn_Wk, L1_xattn_bk, L1_xattn_Wv, L1_xattn_bv, L1_xattn_Wo, L1_xattn_bo)
    x = x + _L1_ffn_ref(_layernorm(x, axis=-1), L1_ffn_weight, L1_ffn_bias)
    return x

_drawn_inputs = setup_inputs


def setup_inputs(seed=0):
    import zlib

    import numpy as np

    out = dict(_drawn_inputs(seed))
    spreads = {'L0_attn_b_Q': (0.0, 0.8),
     'L0_attn_b_K': (0.0, 0.8),
     'L0_attn_b_V': (0.0, 0.1),
     'L0_attn_b_O': (0.0, 0.1),
     'L0_ffn_gate_b': (0.0, 0.8),
     'L1_attn_bq': (0.0, 0.8),
     'L1_attn_bk': (0.0, 0.492),
     'L1_attn_bv': (0.0, 0.464),
     'L1_xattn_bq': (0.0, 0.521),
     'L1_xattn_bk': (0.0, 0.8),
     'L1_xattn_bv': (0.0, 0.1),
     'L1_xattn_bo': (0.0, 0.1),
     'L1_ffn_bias': (0.0, 0.1)}
    factors = {'L0_attn_W_Q': 8.0, 'L0_attn_W_K': 7.874}
    for name, (base, spread) in spreads.items():
        noise = np.random.default_rng([zlib.crc32(name.encode()), seed]).standard_normal(out[name].shape)
        drawn = base * np.exp(spread * noise) if base else spread * noise
        out[name] = jnp.asarray(drawn.astype(out[name].dtype))
    for name, factor in factors.items():
        out[name] = (out[name] * factor).astype(out[name].dtype)
    return out
```

```python
from contextlib import ExitStack

import numpy as np

import concourse.bass as bass
from concourse import mybir

F32 = mybir.dt.float32
F32R = mybir.dt.float32r
BF16 = mybir.dt.bfloat16
F16 = mybir.dt.float16
FP8 = mybir.dt.float8e4
ALU = mybir.AluOpType
ACT = mybir.ActivationFunctionType
AX = mybir.AxisListType

P = 128
D = 512
KD = D // P
S = 256
T = S // P
H = 16
EPS = 1e-5
ROPE_BASE = 10000.0


class Phase:

    def __init__(self, nc, name):
        self.nc, self.name, self.ctx, self.sems = nc, name, ExitStack(), []

    def __enter__(self):
        self.ctx.__enter__()
        self.ctx.callback(self.clear)
        return self

    def __exit__(self, *a):
        return self.ctx.__exit__(*a)

    def clear(self):
        self.nc.clear_and_free_semaphores(self.sems)
        self.nc.all_engine_barrier()

    def sb(self, name, shape, dt=F32):
        return self.ctx.enter_context(self.nc.sbuf_tensor(f"{self.name}_{name}", shape, dt))

    def bank(self, name, dt=F32):
        return self.ctx.enter_context(self.nc.psum_tensor(f"{self.name}_{name}", [P, 2048 // (2 if dt == BF16 else 4)], dt))

    def sem(self, name):
        self.sems.append(self.nc.alloc_semaphore(name=f"{self.name}_{name}"))
        return self.sems[-1]


def over_batches(eng, n, body):
    if n > 1:
        with eng.Fori(0, n - 1) as b:
            body(b, False)
    body(n - 1, True)


def split_products(pe, out, pairs):
    for i, ((ah, al), (bh, bl)) in enumerate(pairs):
        first, last = i == 0, i == len(pairs) - 1
        pe.matmul(out, ah, bh, start=first, stop=False)
        pe.matmul(out, ah, bl, start=False, stop=False)
        mm = pe.matmul(out, al, bh, start=False, stop=last)
    return mm


def attention_phase(nc, name, n_batch, x_in, x_out, consts, wq, wk, wv, wo,
                    d_head, causal, rotary, ctx=None, bq=None, bk=None, bv=None, bo=None, rope=None):
    HD = H * d_head
    CH = HD // 512
    HPT = P // d_head
    NT = H // HPT
    SCALE = 1.0 / float(np.sqrt(d_head))
    KQ = [P * (t + 1) if causal else S for t in range(T)]
    SOFF = [sum(KQ[:t]) for t in range(T)]
    SW = sum(KQ)
    QK = [P * k if causal else 0 for k in range(T)]
    TOFF = [sum(S - QK[j] for j in range(k)) for k in range(T)]
    NP, NPT = 3, 3
    N_LN = KD // 2
    N_IN = N_LN * (1 if rotary else 2)
    N_PROJ = (3 * CH * T + NT) if rotary else (NT + T)
    N_USE = N_PROJ + N_IN + T
    N_W = 0 if rotary else 4 * KD
    BASE = N_W + N_IN

    with Phase(nc, name) as ph:
        A = [ph.bank(f"A{i}") for i in range(2)]
        SC = [ph.bank(f"S{i}") for i in range(2)]
        TP = [ph.bank(f"T{i}") for i in range(2)]
        Z = [ph.bank(f"Z{i}") for i in range(2)]

        ident = ph.sb("ident", [P, P])
        ident_b = ph.sb("ident_b", [P, P], BF16)
        mask_b = ph.sb("mask_b", [P, P], BF16)
        x_t = ph.sb("x_t", [P, T, D])
        res = ph.sb("res", [P, T, D])
        stats = ph.sb("stats", [P, T, 6])
        mv = ph.sb("mv", [P, T, 2])
        rstd = ph.sb("rstd", [P, T])
        wait_slot = ph.sb("wait_slot", [P, 1])
        minus_half = ph.sb("minus_half", [P, T])
        xT = [ph.sb(f"xT{i}", [P, KD, S], F32R) for i in "hl"]
        V = ph.sb("V", [P, T, HD])
        n_qt = 3 if rotary else NT
        n_kt = n_qt * HPT
        QT = ph.sb("QT", [P, n_qt, S])
        KT = ph.sb("KT", [P, n_kt, S])
        neg_max = ph.sb("neg_max", [P, H, T])
        sums = ph.sb("sums", [P, H, T])
        rsum = ph.sb("rsum", [P, H, T])
        prob = ph.sb("prob", [P, NP, SW])
        probT = ph.sb("probT", [P, NPT, SW])
        wvs = [ph.sb(f"wv{i}", [P, KD, HD], F32R) for i in "hl"]
        wqs = [ph.sb(f"wq{i}", [P, KD, HD], F32R) for i in "hl"]
        wks = [ph.sb(f"wk{i}", [P, KD, HD], F32R) for i in "hl"]
        if rotary:
            q_t = ph.sb("q_t", [P, T, HD])
            k_t = ph.sb("k_t", [P, T, HD])
            turn = ph.sb("turn", [P, 2, 2, 512])
            cos = ph.sb("cos", [P, T, d_head])
            sin = ph.sb("sin", [P, T, d_head])
            rb = ph.sb("rb", [P, 2, T, HD])
            wo_f = ph.sb("wo_f", [P, NT, D])
            zT = ph.sb("zT", [P, NT, S])
            stage = [q_t, k_t, V]
        else:
            c_t = ph.sb("c_t", [P, T, D])
            cT = [ph.sb(f"cT{i}", [P, KD, S], F32R) for i in "hl"]
            wos = [ph.sb(f"wo{i}", [P, KD, D], F32R) for i in "hl"]
            zTs = [ph.sb(f"zT{i}", [P, NT, S], F32R) for i in "hl"]
            w_stage = ph.sb("w_stage", [P, 4, KD, D])
        if bq is not None and not rotary:
            bq_c = ph.sb("bq_c", [P, NT])
            bk_c = ph.sb("bk_c", [P, NT])
        if bv is not None:
            bv_c = ph.sb("bv_c", [P, NT])
        if bo is not None:
            bo_r = ph.sb("bo_r", [P, D])

        const_in = ph.sem("const_in")
        w_in = [ph.sem(f"w_in{i}") for i in range(3)]
        wo_in = ph.sem("wo_in")
        w_hi = ph.sem("w_hi")
        w_lo = ph.sem("w_lo")
        x_ok = ph.sem("x_ok")
        c_ok = ph.sem("c_ok")
        res_in = ph.sem("res_in")
        res_b = ph.sem("res_b")
        stored = ph.sem("stored")
        ln = ph.sem("ln")
        ln_pow = ph.sem("ln_pow")
        a_full = ph.sem("a_full")
        a_hi = ph.sem("a_hi")
        a_free = ph.sem("a_free")
        rot = ph.sem("rot")
        zeroed = ph.sem("zeroed")
        s_full = ph.sem("s_full")
        max_ok = ph.sem("max_ok")
        exp_ok = ph.sem("exp_ok")
        rsum_ok = ph.sem("rsum_ok")
        norm_ok = ph.sem("norm_ok")
        t_full = ph.sem("t_full")
        pt_even = ph.sem("pt_even")
        pt_odd = ph.sem("pt_odd")
        pv_ok = ph.sem("pv_ok")
        pool_const = ph.sem("pool_const")
        z_hi = ph.sem("z_hi")
        z_ok = ph.sem("z_ok")

        N_CONST = 3 + (2 if rotary else 0) + sum(v is not None for v in (bv, bo)) \
            + (0 if bq is None else 4 if rotary else 2)
        N_STAGE = 3 * 2 if rotary else 4

        U_IN = N_PROJ

        def use(b, i, last=False):
            return BASE + b * N_USE + i

        block = ph.ctx.enter_context(nc.Block())

        @block.sync
        def _(sp):
            sp.sem_inc(stored, 16)
            sp.dma_start(ident[:, :], consts["ident"]).then_inc(const_in, 16)
            sp.dma_start(ident_b[:, :], consts["ident_b"]).then_inc(const_in, 16)
            sp.dma_start(mask_b[:, :], consts["mask_b"]).then_inc(const_in, 16)
            if rotary:
                sp.dma_start(cos[:, :, :], rope[0]).then_inc(const_in, 16)
                sp.dma_start(sin[:, :, :], rope[1]).then_inc(const_in, 16)
                for j, b_ in enumerate((bq, bk)):
                    for t in range(T):
                        sp.dma_start(rb[:, j, t, :], b_.rearrange("h k -> (h k)").partition_broadcast(P)).then_inc(const_in, 16)
            elif bq is not None:
                sp.dma_start(bq_c[:, :], bq.rearrange("(t p) -> p t", p=P), allow_slow_non_contiguous=True).then_inc(const_in, 16)
                sp.dma_start(bk_c[:, :], bk.rearrange("(t p) -> p t", p=P), allow_slow_non_contiguous=True).then_inc(const_in, 16)
            if bv is not None:
                bv_flat = bv.rearrange("h k -> (h k)") if rotary else bv
                sp.dma_start(bv_c[:, :], bv_flat.rearrange("(t p) -> p t", p=P), allow_slow_non_contiguous=True).then_inc(const_in, 16)
            if bo is not None:
                sp.dma_start(bo_r[:, :], bo.partition_broadcast(P)).then_inc(const_in, 16)
            sp.dma_start(x_t[:, :, :], x_in[0].rearrange("(t p) d -> p t d", p=P)).then_inc(x_ok, 16)
            if rotary:
                for i in range(N_STAGE):
                    w = (wq, wk, wv)[i // 2]
                    if i >= 3:
                        sp.wait_ge(w_lo, i - 2)
                    hh = i % 2
                    buf = stage[i % 3]
                    for k in range(KD):
                        sp.dma_start(
                            buf[:, :, :].rearrange("p t n -> p (t n)")[:, k * 512:(k + 1) * 512].rearrange("p (h e) -> p h e", e=d_head),
                            w[hh * H // 2:(hh + 1) * H // 2, k * P:(k + 1) * P, :].rearrange("h p e -> p h e"),
                        ).then_inc(w_in[i % 3], 16)
                sp.dma_start(wo_f[:, :, :], wo.rearrange("h e m -> (h e) m").rearrange("(k p) m -> p k m", p=P)).then_inc(wo_in, 16)
            else:
                sp.dma_start(c_t[:, :, :], ctx[0].rearrange("(t p) d -> p t d", p=P)).then_inc(c_ok, 16)
                for i, w in enumerate((wq, wk, wv, wo)):
                    sp.dma_start(w_stage[:, i, :, :], w.rearrange("(j p) d -> p j d", p=P)).then_inc(w_in[0], 16)

            def body(b, last):
                if not last:
                    sp.wait_ge(a_full, use(b, 0))
                    sp.dma_start(x_t[:, :, :], x_in[b + 1].rearrange("(t p) d -> p t d", p=P)).then_inc(x_ok, 16)
                    if not rotary:
                        sp.dma_start(c_t[:, :, :], ctx[b + 1].rearrange("(t p) d -> p t d", p=P)).then_inc(c_ok, 16)
                sp.wait_ge(stored, 16 + b * 16)
                sp.dma_start(res[:, :, :], x_in[b].rearrange("(t p) d -> p t d", p=P)).then_inc(res_in, 16)
                sp.wait_ge(a_free, use(b, N_USE - (N_IN if last else 0)))
                sp.dma_start(x_out[b].rearrange("(t p) d -> p t d", p=P), res[:, :, :]).then_inc(stored, 16)
            over_batches(sp, n_batch, body)
            sp.wait_ge(stored, 16 + 16 * n_batch)

        @block.gpsimd
        def _(pool):
            def rstds(n):
                pool.wait_ge(ln, 7 * n + 5)
                pool.tensor_tensor(rstd[:, :], rstd[:, :], minus_half[:, :], ALU.pow).then_inc(ln_pow, 1)

            pool.sem_inc(rot, 1)
            pool.memset(minus_half[:, :], -0.5).then_inc(pool_const, 1)
            pool.wait_ge(pool_const, 1)
            rstds(0)
            pool.wait_ge(const_in, 16 * N_CONST)
            if rotary:
                pool.wait_ge(zeroed, 1 + 4 * T * CH)

            def body(b, last):
                if rotary:
                    for i in range(2 * CH * T):
                        which, c, t = (i // T) % 2, i // (2 * T), i % T
                        dst = (q_t, k_t)[which][:, t, c * 512:(c + 1) * 512]
                        pool.wait_ge(a_free, use(b, i + 1))
                        pool.tensor_tensor(turn[:, i % 2, 0, :], turn[:, i % 2, 0, :], turn[:, i % 2, 1, :], ALU.add).then_inc(rot, 1)
                        pool.wait_ge(rot, 1 + b * 4 * CH * T + 2 * i + 1)
                        pool.tensor_tensor(dst, turn[:, i % 2, 0, :], rb[:, which, t, c * 512:(c + 1) * 512], ALU.add).then_inc(rot, 1)
                if bo is not None:
                    pool.wait_ge(res_in, b * 16 + 16)
                    for t in range(T):
                        pool.tensor_tensor(res[:, t, :], res[:, t, :], bo_r[:, :], ALU.add).then_inc(res_b, 1)
                for h in range(H):
                    if h == H - 9 and not last:
                        rstds(b + 1)
                    pool.wait_ge(rsum_ok, b * H + h + 1)
                    for t in range(T):
                        pr = prob[:, h % NP, SOFF[t]:SOFF[t] + KQ[t]]
                        ins = pool.tensor_tensor(pr, pr, rsum[:, h, t:t + 1].to_broadcast([P, KQ[t]]), ALU.mult)
                    ins.then_inc(norm_ok, 1)
            over_batches(pool, n_batch, body)

        @block.tensor
        def _(pe):
            for count in (s_full, t_full, pv_ok):
                pe.sem_inc(count, 1)
            pe.wait_ge(const_in, 16 * N_CONST)

            def bank_for(u):
                if not isinstance(u, int) or u >= 2:
                    pe.wait_ge(a_free, u - 1)

            def ln_transposes(n, u, src):
                for j in range(N_LN):
                    bank_for(u + j)
                    for kk in range(2):
                        for t in range(T):
                            k = 2 * j + kk
                            mm = pe.transpose(A[j % 2][:, (kk * T + t) * P:(kk * T + t + 1) * P], src[:, t, k * P:(k + 1) * P], ident[:, :])
                    mm.then_inc(a_full, 1)

            if not rotary:
                pe.wait_ge(w_in[0], 16 * 4)
                for i in range(4):
                    for k in range(KD):
                        u = i * KD + k
                        bank_for(u)
                        for j in range(4):
                            mm = pe.transpose(A[u % 2][:, j * P:(j + 1) * P], w_stage[:, i, j, k * P:(k + 1) * P], ident[:, :])
                        mm.then_inc(a_full, 1)
            pe.wait_ge(ln, 7)
            ln_transposes(0, N_W, x_t)
            if not rotary:
                pe.wait_ge(c_ok, 16)
                ln_transposes(0, N_W + N_LN, c_t)
            if rotary:
                pe.wait_ge(w_lo, N_STAGE)
                pe.wait_ge(wo_in, 16)
            pe.wait_ge(zeroed, 1)

            def proj_tokens(b, i, src, w, t, c):
                bank_for(use(b, i))
                split_products(pe, A[i % 2][:, :], [
                    ((src[0][:, k, t * P:(t + 1) * P], src[1][:, k, t * P:(t + 1) * P]),
                     (w[0][:, k, c * 512:(c + 1) * 512], w[1][:, k, c * 512:(c + 1) * 512])) for k in range(KD)
                ]).then_inc(a_full, 1)

            def qk_transposes(b, hp):
                i = 3 * CH * T + hp
                pe.wait_ge(rot, 1 + b * 4 * CH * T + 4 * T * (hp // (NT // CH) + 1))
                bank_for(use(b, i))
                for j, src in enumerate((q_t, k_t)):
                    for t in range(T):
                        mm = pe.transpose(A[i % 2][:, (j * T + t) * P:(j * T + t + 1) * P], src[:, t, hp * P:(hp + 1) * P], ident[:, :])
                mm.then_inc(a_full, 1)

            def scores(b, h):
                g = h // HPT
                pe.wait_ge(a_free, use(b, (3 * CH * T if rotary else 0) + g + 1))
                pe.wait_ge(exp_ok, 1 + b * H + max(h - 1, 0))
                for t in range(T):
                    out = SC[h % 2][:, SOFF[t]:SOFF[t] + KQ[t]]
                    mm = pe.matmul(out, QT[:, g % n_qt, t * P:(t + 1) * P], KT[:, h % n_kt, 0:KQ[t]], start=True, stop=True, skip_group_check=causal)
                    if causal:
                        mm = pe.matmul(SC[h % 2][:, SOFF[t] + t * P:SOFF[t] + (t + 1) * P], ident_b[:, :], mask_b[:, :],
                                       start=False, stop=True, skip_group_check=True)
                mm.then_inc(s_full, 1)

            def prob_transposes(b, h):
                pe.wait_ge(norm_ok, b * H + h + 1)
                pe.wait_ge((pt_even, pt_odd)[h % 2], 1 + b * (H // 2) + h // 2)
                for k in range(T):
                    for t in range(T):
                        if k * P < KQ[t]:
                            o = TOFF[k] + t * P - QK[k]
                            mm = pe.transpose(TP[h % 2][:, o:o + P], prob[:, h % NP, SOFF[t] + k * P:SOFF[t] + (k + 1) * P], ident[:, :])
                mm.then_inc(t_full, 1)

            def times_v(b, h):
                g, j = h // HPT, h % HPT
                pe.wait_ge((pt_even, pt_odd)[h % 2], 1 + b * (H // 2) + h // 2 + 1)
                if j == 0:
                    pe.wait_ge(z_ok, 1 + b * NT + max(g - 1, 0))
                for k in range(T):
                    mm = pe.matmul(Z[g % 2][j * d_head:(j + 1) * d_head, QK[k]:S], V[:, k, h * d_head:(h + 1) * d_head],
                                   probT[:, h % NPT, TOFF[k]:TOFF[k] + S - QK[k]], start=(k == 0), stop=(k == T - 1),
                                   tile_position=(0, j * d_head))
                mm.then_inc(pv_ok, 1)

            def body(b, last):
                pe.wait_ge(a_free, use(b, 0))
                if rotary:
                    for i in range(2 * CH * T):
                        proj_tokens(b, i, xT, (wqs, wks)[(i // T) % 2], i % T, i // (2 * T))
                    for i in range(CH * T):
                        proj_tokens(b, 2 * CH * T + i, xT, wvs, i % T, i // T)
                    qk_transposes(b, 0)
                    qk_transposes(b, 1)
                else:
                    for i in range(NT):
                        bank_for(use(b, i))
                        for j, (w, src) in enumerate(((wqs, xT), (wks, cT))):
                            mm = split_products(pe, A[i % 2][:, j * S:(j + 1) * S], [
                                ((w[0][:, k, i * P:(i + 1) * P], w[1][:, k, i * P:(i + 1) * P]),
                                 (src[0][:, k, :], src[1][:, k, :])) for k in range(KD)])
                        mm.then_inc(a_full, 1)
                    for t in range(T):
                        proj_tokens(b, NT + t, cT, wvs, t, 0)
                for i in range(H + 4):
                    if i < H:
                        scores(b, i)
                    if rotary and i % 2 == 0 and i // 2 + 2 < NT:
                        qk_transposes(b, i // 2 + 2)
                    if i == H - 2 and not last:
                        pe.wait_ge(ln, (b + 1) * 7 + 7)
                        ln_transposes(b + 1, use(b, U_IN), x_t)
                        if not rotary:
                            pe.wait_ge(c_ok, (b + 1) * 16 + 16)
                            ln_transposes(b + 1, use(b, U_IN + N_LN), c_t)
                    if 2 <= i < H + 2:
                        prob_transposes(b, i - 2)
                    if i >= 4:
                        times_v(b, i - 4)
                pe.wait_ge(z_ok, 1 + (b + 1) * NT)
                for t in range(T):
                    i = U_IN + (0 if last else N_IN) + t
                    bank_for(use(b, i))
                    if rotary:
                        for k in range(NT):
                            mm = pe.matmul(A[i % 2][:, :], zT[:, k, t * P:(t + 1) * P], wo_f[:, k, :], start=(k == 0), stop=(k == NT - 1))
                        mm.then_inc(a_full, 1)
                    else:
                        split_products(pe, A[i % 2][:, :], [
                            ((zTs[0][:, k, t * P:(t + 1) * P], zTs[1][:, k, t * P:(t + 1) * P]),
                             (wos[0][:, k, :], wos[1][:, k, :])) for k in range(KD)]).then_inc(a_full, 1)
            over_batches(pe, n_batch, body)

        N_HI = N_IN + NT

        def hi_at(b, i):
            return N_W + N_IN + b * N_HI + i

        @block.scalar
        def _(act):
            for count in (exp_ok, pt_odd):
                act.sem_inc(count, 1)
            if rotary:
                for i in range(N_STAGE):
                    w = (wqs, wks, wvs)[i // 2]
                    act.wait_ge(w_in[i % 3], 16 * KD * (i // 3 + 1))
                    act.activation(w[0][:, :, (i % 2) * 512:(i % 2 + 1) * 512],
                                   stage[i % 3][:, :, :].rearrange("p t n -> p (t n)").rearrange("p (k n) -> p k n", k=KD), ACT.Copy).then_inc(w_hi, 1)
            else:
                for u in range(N_W):
                    act.wait_ge(a_full, u + 1)
                    act.activation((wqs, wks, wvs, wos)[u // KD][0][:, u % KD, :], A[u % 2][:, :], ACT.Copy).then_inc(a_hi, 1)

            def take_hi(u, dst):
                for j in range(N_LN):
                    act.wait_ge(a_full, u + j + 1)
                    act.activation(dst[0][:, 2 * j:2 * j + 2, :].rearrange("p k n -> p (k n)"), A[j % 2][:, :], ACT.Copy).then_inc(a_hi, 1)

            if not rotary and bq is not None:
                act.wait_ge(zeroed, 2)
            act.wait_ge(const_in, 16 * N_CONST)
            take_hi(N_W, xT)
            if not rotary:
                take_hi(N_W + N_LN, cT)

            def queries(b, g):
                i = (3 * CH * T if rotary else 0) + g
                act.wait_ge(a_full, use(b, i + 1))
                act.wait_ge(s_full, 1 + b * H + HPT * max(g + 1 - n_qt, 0))
                if rotary or bq is None:
                    act.activation(QT[:, g % n_qt, :], A[i % 2][:, 0:S], ACT.Copy, scale=SCALE).then_inc(a_hi, 1)
                else:
                    act.activation(QT[:, g % n_qt, :], A[i % 2][:, 0:S], ACT.Identity, bias=bq_c[:, g:g + 1], scale=SCALE).then_inc(a_hi, 1)

            def exps(b, h):
                act.wait_ge(max_ok, b * H + h + 1)
                act.wait_ge(t_full, 1 + b * H + max(h - NP + 1, 0))
                for t in range(T):
                    ins = act.activation(prob[:, h % NP, SOFF[t]:SOFF[t] + KQ[t]], SC[h % 2][:, SOFF[t]:SOFF[t] + KQ[t]], ACT.Exp,
                                         bias=neg_max[:, h, t:t + 1], scale=1.0, accum_out=sums[:, h, t:t + 1])
                ins.then_inc(exp_ok, 1)

            def probs_odd(b, h):
                act.wait_ge(t_full, 1 + b * H + h + 1)
                act.wait_ge(pv_ok, 1 + b * H + max(h - NPT + 1, 0))
                act.activation(probT[:, h % NPT, :], TP[1][:, 0:SW], ACT.Copy).then_inc(pt_odd, 1)

            def body(b, last):
                for g in range(2 if rotary else NT):
                    queries(b, g)
                for i in range(H + 5):
                    if i < H:
                        exps(b, i)
                    if rotary and i % 2 == 0 and i // 2 + 2 < NT:
                        queries(b, i // 2 + 2)
                    if i == H - 2 and not last:
                        take_hi(use(b, U_IN), xT)
                        if not rotary:
                            take_hi(use(b, U_IN + N_LN), cT)
                    if 3 <= i < H + 3 and (i - 3) % 2:
                        probs_odd(b, i - 3)
                    if not rotary and i >= 5 and (i - 5) % HPT == HPT - 1:
                        g = (i - 5) // HPT
                        act.wait_ge(pv_ok, 1 + b * H + HPT * (g + 1))
                        if bv is None:
                            act.activation(zTs[0][:, g, :], Z[g % 2][:, 0:S], ACT.Copy).then_inc(z_hi, 1)
                        else:
                            act.activation(zTs[0][:, g, :], Z[g % 2][:, 0:S], ACT.Identity, bias=bv_c[:, g:g + 1]).then_inc(z_hi, 1)
            over_batches(act, n_batch, body)

        @block.vector
        def _(dve):
            for count in (pt_even, z_ok):
                dve.sem_inc(count, 1)
            dve.memset(KT[:, :, :], 0.0).then_inc(zeroed, 1)
            dve.wait_ge(const_in, 16 * N_CONST)
            if bq is not None and not rotary:
                dve.wait_ge(zeroed, 1)
                dve.tensor_scalar(bq_c[:, :], bq_c[:, :], SCALE, None, ALU.mult).then_inc(zeroed, 1)
            if rotary:
                n = 0
                for j in range(2):
                    for t in range(T):
                        for c in range(CH):
                            bias = rb[:, j, t, c * 512:(c + 1) * 512].rearrange("p (h a e) -> p h a e", a=2, e=d_head // 2)
                            tmp = turn[:, 0, 0, :].rearrange("p (h a e) -> p h a e", a=2, e=d_head // 2)
                            tmp2 = turn[:, 0, 1, :].rearrange("p (h a e) -> p h a e", a=2, e=d_head // 2)
                            rot_tables(dve, bias, tmp, tmp2, cos[:, t, :], sin[:, t, :], 512 // d_head, d_head)[1].then_inc(zeroed, 1)
                            n += 1
                            dve.wait_ge(zeroed, 1 + n)
                            dve.tensor_tensor(rb[:, j, t, c * 512:(c + 1) * 512], turn[:, 0, 0, :], turn[:, 0, 1, :], ALU.add).then_inc(zeroed, 1)
                            n += 1
                            dve.wait_ge(zeroed, 1 + n)
                for i in range(N_STAGE):
                    w = (wqs, wks, wvs)[i // 2]
                    cs = slice((i % 2) * 512, (i % 2 + 1) * 512)
                    dve.wait_ge(w_hi, i + 1)
                    dve.tensor_tensor(w[1][:, :, cs], stage[i % 3][:, :, :].rearrange("p t n -> p (t n)").rearrange("p (k n) -> p k n", k=KD),
                                      w[0][:, :, cs], ALU.subtract).then_inc(w_lo, 1)
            else:
                for u in range(N_W):
                    dve.wait_ge(a_hi, u + 1)
                    w = (wqs, wks, wvs, wos)[u // KD]
                    dve.tensor_tensor(w[1][:, u % KD, :], A[u % 2][:, :], w[0][:, u % KD, :], ALU.subtract).then_inc(a_free, 1)

            def norm_stats(n):
                dve.wait_ge(x_ok, 16 * n + 16)
                for t in range(T):
                    dve.bn_stats(stats[:, t, :], x_t[:, t, :]).then_inc(ln, 1)
                dve.wait_ge(ln, 7 * n + 2)
                dve.memset(wait_slot[:, :], 0.0)
                for t in range(T):
                    dve.bn_aggr(mv[:, t, :], stats[:, t, :]).then_inc(ln, 1)
                dve.wait_ge(ln, 7 * n + 4)
                dve.tensor_scalar(rstd[:, :], mv[:, :, 1], EPS, None, ALU.add).then_inc(ln, 1)

            def apply_norm(n):
                dve.wait_ge(ln_pow, n + 1)
                for t in range(T):
                    dve.tensor_scalar(x_t[:, t, :], x_t[:, t, :], mv[:, t, 0:1], rstd[:, t:t + 1], ALU.subtract, ALU.mult).then_inc(ln, 1)

            def take_lo(hi, dst):
                for j in range(N_LN):
                    dve.wait_ge(a_hi, hi + j + 1)
                    dve.tensor_tensor(dst[1][:, 2 * j:2 * j + 2, :].rearrange("p k n -> p (k n)"), A[j % 2][:, :],
                                      dst[0][:, 2 * j:2 * j + 2, :].rearrange("p k n -> p (k n)"), ALU.subtract).then_inc(a_free, 1)

            norm_stats(0)
            apply_norm(0)
            take_lo(N_W, xT)
            if not rotary:
                take_lo(N_W + N_LN, cT)

            def keys(b, g):
                i = (3 * CH * T if rotary else 0) + g
                dve.wait_ge(a_hi, hi_at(b, g + 1))
                if rotary:
                    dve.wait_ge(s_full, 1 + b * H + max(HPT * (g + 1) - n_kt, 0))
                for j in range(HPT):
                    rows = slice(j * d_head, (j + 1) * d_head)
                    if rotary or bk is None:
                        ins = dve.tensor_copy(KT[rows, (g * HPT + j) % n_kt, :], A[i % 2][rows, S:2 * S])
                    else:
                        ins = dve.tensor_scalar(KT[rows, g * HPT + j, :], A[i % 2][rows, S:2 * S], bk_c[rows, g:g + 1], None, ALU.add)
                ins.then_inc(a_free, 1)

            def maxima(b, h):
                dve.wait_ge(s_full, 1 + b * H + h + 1)
                for t in range(T):
                    ins = dve.tensor_reduce(neg_max[:, h, t:t + 1], SC[h % 2][:, SOFF[t]:SOFF[t] + KQ[t]], AX.X, ALU.max, negate=True)
                ins.then_inc(max_ok, 1)

            def body(b, last):
                if rotary:
                    for i in range(2 * CH * T):
                        t = i % T
                        dve.wait_ge(a_full, use(b, i + 1))
                        dve.wait_ge(rot, 1 + b * 4 * CH * T + max(2 * (i - 1), 0))
                        src = A[i % 2][:, :].rearrange("p (h a e) -> p h a e", a=2, e=d_head // 2)
                        to = [turn[:, i % 2, s, :].rearrange("p (h a e) -> p h a e", a=2, e=d_head // 2) for s in range(2)]
                        rot_tables(dve, src, to[0], to[1], cos[:, t, :], sin[:, t, :], 512 // d_head, d_head)[1].then_inc(a_free, 1)
                    v_first, v_n = 2 * CH * T, CH * T
                else:
                    for g in range(NT):
                        keys(b, g)
                    v_first, v_n = NT, T
                for j in range(v_n):
                    i = v_first + j
                    t, c = j % T, j // T
                    dve.wait_ge(a_full, use(b, i + 1))
                    dve.tensor_copy(V[:, t, c * 512:(c + 1) * 512], A[i % 2][:, :]).then_inc(a_free, 1)
                if rotary:
                    keys(b, 0)
                    keys(b, 1)
                for i in range(H + 5):
                    if i < H:
                        maxima(b, i)
                    if rotary and i % 2 == 0 and i // 2 + 2 < NT:
                        keys(b, i // 2 + 2)
                    if i == H - 8 and not last:
                        norm_stats(b + 1)
                    if i == H - 6 and not last:
                        apply_norm(b + 1)
                    if i == H - 2 and not last:
                        take_lo(hi_at(b, NT), xT)
                        if not rotary:
                            take_lo(hi_at(b, NT + N_LN), cT)
                    if 1 <= i < H + 1:
                        h = i - 1
                        dve.wait_ge(exp_ok, 1 + b * H + h + 1)
                        dve.reciprocal(rsum[:, h, :], sums[:, h, :]).then_inc(rsum_ok, 1)
                    if 3 <= i < H + 3 and (i - 3) % 2 == 0:
                        h = i - 3
                        dve.wait_ge(t_full, 1 + b * H + h + 1)
                        dve.wait_ge(pv_ok, 1 + b * H + max(h - NPT + 1, 0))
                        dve.tensor_copy(probT[:, h % NPT, :], TP[0][:, 0:SW]).then_inc(pt_even, 1)
                    if i >= 5 and (i - 5) % HPT == HPT - 1:
                        g = (i - 5) // HPT
                        if rotary:
                            dve.wait_ge(pv_ok, 1 + b * H + HPT * (g + 1))
                            dve.tensor_scalar(zT[:, g, :], Z[g % 2][:, 0:S], bv_c[:, g:g + 1], None, ALU.add).then_inc(z_ok, 1)
                        else:
                            dve.wait_ge(z_hi, b * NT + g + 1)
                            if bv is None:
                                dve.tensor_tensor(zTs[1][:, g, :], Z[g % 2][:, 0:S], zTs[0][:, g, :], ALU.subtract).then_inc(z_ok, 1)
                            else:
                                dve.scalar_tensor_tensor(zTs[1][:, g, :], Z[g % 2][:, 0:S], bv_c[:, g:g + 1], zTs[0][:, g, :],
                                                         ALU.add, ALU.subtract).then_inc(z_ok, 1)
                dve.wait_ge(res_in, b * 16 + 16)
                if bo is not None:
                    dve.wait_ge(res_b, (b + 1) * T)
                for t in range(T):
                    i = U_IN + (0 if last else N_IN) + t
                    dve.wait_ge(a_full, use(b, i + 1))
                    dve.tensor_tensor(res[:, t, :], A[i % 2][:, :], res[:, t, :], ALU.add).then_inc(a_free, 1)
            over_batches(dve, n_batch, body)


def rot_tables(dve, src, to_cos, to_sin, cos, sin, heads, d_head):
    half = d_head // 2
    c = cos.rearrange("p (o a e) -> p o a e", o=1, a=2).to_broadcast([P, heads, 2, half])
    s = sin.rearrange("p (o a e) -> p o a e", o=1, a=2).to_broadcast([P, heads, 2, half])
    return (dve.tensor_tensor(to_cos, src, c, ALU.mult),
            dve.tensor_tensor(to_sin, src[:, :, ::-1, :], s, ALU.mult))


def expert_phase(nc, n_batch, x_in, x_norm, consts, gate_w, gate_b, w1, w2, logits_d, sel_d, selT_d, out_d):
    E = gate_w.shape[0]
    HID = w1.shape[2]
    Q = HID // 512
    G = P // E
    NG = n_batch // G
    K8 = 8
    with Phase(nc, "moe") as ph:
        ident = ph.sb("ident", [P, P])
        merged = ph.sb("merged", [P, E, KD, n_batch])
        const_in = ph.sem("const_in")

        with Phase(nc, "route") as r:
            xT_bank = [r.bank(f"X{i}") for i in range(2)]
            L = r.bank("L")
            gate = r.sb("gate", [E, D])
            gateT = r.sb("gateT", [P, KD, E])
            gb = r.sb("gb", [E, 1])
            x_t = r.sb("x_t", [P, 2, T, D])
            xT = r.sb("xT", [P, KD, S])
            lg = r.sb("lg", [E, 2, S])
            stats = r.sb("stats", [P, T, 6])
            mv = r.sb("mv", [P, T, 2])
            rstd = r.sb("rstd", [P, T])
            minus_half = r.sb("minus_half", [P, T])
            wait_slot = r.sb("wait_slot", [P, 1])
            x_ok = [r.sem(f"x_ok{i}") for i in range(2)]
            ln = r.sem("ln")
            ln_pow = r.sem("ln_pow")
            pool_const = r.sem("pool_const")
            stored = [r.sem(f"stored{i}") for i in range(2)]
            g_full = r.sem("g_full")
            g_ok = r.sem("g_ok")
            t_full = r.sem("t_full")
            t_ok = r.sem("t_ok")
            l_full = r.sem("l_full")
            l_ok = r.sem("l_ok")
            block = r.ctx.enter_context(nc.Block())

            @block.sync
            def _(sp):
                sp.dma_start(ident[:, :], consts["ident"]).then_inc(const_in, 16)
                sp.dma_start(gate[:, :], gate_w).then_inc(const_in, 16)
                sp.dma_start(gb[:, :], gate_b.rearrange("(e o) -> e o", o=1)).then_inc(const_in, 16)
                for s in range(2):
                    sp.sem_inc(stored[s], 16)
                with sp.Fori(0, n_batch // 2) as i:
                    for s in range(2):
                        b = 2 * i + s
                        sp.wait_ge(stored[s], 16 + 32 * i)
                        sp.dma_start(x_t[:, s, :, :], x_in[b].rearrange("(t p) d -> p t d", p=P)).then_inc(x_ok[s], 16)
                for s in range(2):
                    sp.wait_ge(stored[s], 16 + 16 * n_batch)

            @block.gpsimd
            def _(pool):
                pool.memset(minus_half[:, :], -0.5).then_inc(pool_const, 1)
                pool.wait_ge(pool_const, 1)
                with pool.Fori(0, n_batch) as b:
                    pool.wait_ge(ln, 7 * b + 5)
                    pool.tensor_tensor(rstd[:, :], rstd[:, :], minus_half[:, :], ALU.pow).then_inc(ln_pow, 1)

            @block.vector
            def _(dve):
                dve.sem_inc(l_ok, 1)
                dve.wait_ge(g_full, 1)
                dve.tensor_copy(gateT[:, :, :].rearrange("p k e -> p (k e)"), L[:, 0:KD * E]).then_inc(g_ok, 1)
                with dve.Fori(0, n_batch // 2) as i:
                    for s in range(2):
                        n = 2 * i + s
                        dve.wait_ge(x_ok[s], 16 * i + 16)
                        for t in range(T):
                            dve.bn_stats(stats[:, t, :], x_t[:, s, t, :]).then_inc(ln, 1)
                        dve.wait_ge(ln, 7 * n + 2)
                        dve.memset(wait_slot[:, :], 0.0)
                        for t in range(T):
                            dve.bn_aggr(mv[:, t, :], stats[:, t, :]).then_inc(ln, 1)
                        dve.wait_ge(ln, 7 * n + 4)
                        dve.tensor_scalar(rstd[:, :], mv[:, :, 1], EPS, None, ALU.add).then_inc(ln, 1)
                        dve.wait_ge(ln_pow, n + 1)
                        for t in range(T):
                            dve.tensor_scalar(x_t[:, s, t, :], x_t[:, s, t, :], mv[:, t, 0:1], rstd[:, t:t + 1], ALU.subtract, ALU.mult).then_inc(ln, 1)
                        dve.wait_ge(l_full, n + 1)
                        dve.wait_ge(stored[s], 16 + 32 * i)
                        dve.tensor_scalar(lg[:, s, :], L[0:E, 0:S], gb[:, 0:1], None, ALU.add).then_inc(l_ok, 1)

            @block.tensor
            def _(pe):
                pe.wait_ge(const_in, 48)
                pe.sem_inc(t_full, 1)
                for k in range(KD):
                    mm = pe.transpose(L[:, k * E:(k + 1) * E], gate[:, k * P:(k + 1) * P], ident[0:E, 0:E])
                mm.then_inc(g_full, 1)
                pe.wait_ge(g_ok, 1)
                with pe.Fori(0, n_batch // 2) as i:
                    for s in range(2):
                        n = 2 * i + s
                        pe.wait_ge(ln, 7 * n + 7)
                        pe.wait_ge(t_ok, 1 + 2 * n)
                        for j in range(2):
                            for kk in range(2):
                                for t in range(T):
                                    k = 2 * j + kk
                                    mm = pe.transpose(xT_bank[j][:, (kk * T + t) * P:(kk * T + t + 1) * P], x_t[:, s, t, k * P:(k + 1) * P], ident[:, :])
                            mm.then_inc(t_full, 1)
                        pe.wait_ge(t_ok, 1 + 2 * n + 2)
                        pe.wait_ge(l_ok, 1 + n)
                        for k in range(KD):
                            mm = pe.matmul(L[0:E, 0:S], gateT[:, k, :], xT[:, k, :], start=(k == 0), stop=(k == KD - 1))
                        mm.then_inc(l_full, 1)

            @block.scalar
            def _(act):
                act.sem_inc(t_ok, 1)
                with act.Fori(0, n_batch // 2) as i:
                    for s in range(2):
                        n = 2 * i + s
                        act.wait_ge(ln, 7 * n + 7)
                        act.dma_start(x_norm[n].rearrange("(t p) d -> p t d", p=P), x_t[:, s, :, :]).then_inc(stored[s], 16)
                        for j in range(2):
                            act.wait_ge(t_full, 1 + 2 * n + j + 1)
                            act.activation(xT[:, 2 * j:2 * j + 2, :].rearrange("p k n -> p (k n)"), xT_bank[j][:, :], ACT.Copy).then_inc(t_ok, 1)
                        act.wait_ge(l_ok, 1 + n + 1)
                        act.dma_start(logits_d[n], lg[:, s, :]).then_inc(stored[s], 16)

        with Phase(nc, "top") as r:
            TB = [r.bank(f"T{i}") for i in range(2)]
            pr = r.sb("pr", [P, NG, S])
            rest = r.sb("rest", [P, NG, S])
            nm = r.sb("nm", [P, NG])
            sm = r.sb("sm", [P, NG])
            top = r.sb("top", [P, NG, K8])
            selT = r.sb("selT", [P, T, NG, P])
            landed, mx, ex, step, full, got, done = (r.sem(n) for n in ("landed", "mx", "ex", "step", "full", "got", "done"))
            block = r.ctx.enter_context(nc.Block())
            NDONE = 1 + NG * G * T

            @block.sync
            def _(sp):
                sp.dma_start(pr[:, :, :], logits_d.rearrange("(g b) e s -> (b e) g s", b=G)).then_inc(landed, 16)
                sp.wait_ge(step, 5 * NG)
                sp.dma_start(sel_d.rearrange("(g b) e s -> (b e) g s", b=G), pr[:, :, :]).then_inc(done, 16)
                for g in range(NG):
                    sp.wait_ge(got, g + 1)
                    for b in range(G):
                        for t in range(T):
                            sp.dma_start(selT_d[g * G + b, t], selT[:, t, g, b * E:(b + 1) * E]).then_inc(done, 16)
                sp.wait_ge(done, 16 * NDONE)

            @block.vector
            def _(dve):
                dve.wait_ge(landed, 16)
                for g in range(NG):
                    dve.tensor_reduce(nm[:, g:g + 1], pr[:, g, :], AX.X, ALU.max, negate=True).then_inc(mx, 1)
                for g in range(NG):
                    dve.wait_ge(ex, g + 1)
                    dve.reciprocal(sm[:, g:g + 1], sm[:, g:g + 1]).then_inc(step, 1)
                    dve.wait_ge(step, 5 * g + 1)
                    dve.tensor_scalar(pr[:, g, :], pr[:, g, :], sm[:, g:g + 1], None, ALU.mult).then_inc(step, 1)
                    dve.wait_ge(step, 5 * g + 2)
                    dve.max(top[:, g, :], pr[:, g, :]).then_inc(step, 1)
                    dve.wait_ge(step, 5 * g + 3)
                    dve.match_replace(rest[:, g, :], top[:, g, :], pr[:, g, :], 0.0).then_inc(step, 1)
                    dve.wait_ge(step, 5 * g + 4)
                    dve.tensor_tensor(pr[:, g, :], pr[:, g, :], rest[:, g, :], ALU.subtract).then_inc(step, 1)
                for g in range(NG):
                    dve.wait_ge(full, g + 1)
                    dve.tensor_copy(selT[:, :, g, :], TB[g % 2][:, 0:T * P].rearrange("p (t e) -> p t e", t=T)).then_inc(got, 1)

            @block.scalar
            def _(act):
                for g in range(NG):
                    act.wait_ge(mx, g + 1)
                    act.activation(pr[:, g, :], pr[:, g, :], ACT.Exp, bias=nm[:, g:g + 1], accum_out=sm[:, g:g + 1]).then_inc(ex, 1)

            @block.tensor
            def _(pe):
                for g in range(NG):
                    pe.wait_ge(step, 5 * g + 5)
                    if g >= 2:
                        pe.wait_ge(got, g - 1)
                    for t in range(T):
                        mm = pe.transpose(TB[g % 2][:, t * P:(t + 1) * P], pr[:, g, t * P:(t + 1) * P], ident[:, :])
                    mm.then_inc(full, 1)

        with Phase(nc, "merge") as r:
            M = [r.bank(f"M{i}") for i in range(2)]
            xn = r.sb("xn", [P, 2, T, D])
            sel = r.sb("sel", [P, 2, T, E])
            landed = [r.sem(f"landed{i}") for i in range(2)]
            full, got = r.sem("full"), r.sem("got")
            block = r.ctx.enter_context(nc.Block())

            @block.sync
            def _(sp):
                with sp.Fori(0, n_batch // 2) as i:
                    for s in range(2):
                        b = 2 * i + s
                        sp.wait_ge(full, 2 * i + s + 1)
                        sp.dma_start(xn[:, s, :, :], x_norm[b].rearrange("(t p) d -> p t d", p=P)).then_inc(landed[s], 16)
                        sp.dma_start(sel[:, s, :, :], selT_d[b].rearrange("t p e -> p t e")).then_inc(landed[s], 16)

            @block.tensor
            def _(pe):
                pe.sem_inc(full, 2)
                with pe.Fori(0, n_batch // 2) as i:
                    for s in range(2):
                        pe.wait_ge(landed[s], 32 * i + 32)
                        pe.wait_ge(got, 2 * i + s + 1)
                        for k in range(KD):
                            for t in range(T):
                                mm = pe.matmul(M[s][:, k * E:(k + 1) * E], xn[:, s, t, k::KD], sel[:, s, t, :], start=(t == 0), stop=(t == T - 1))
                        mm.then_inc(full, 1)

            @block.vector
            def _(dve):
                dve.sem_inc(got, 2)
                with dve.Fori(0, n_batch // 2) as i:
                    for s in range(2):
                        dve.wait_ge(full, 2 + 2 * i + s + 1)
                        dve.tensor_copy(merged[:, :, :, bass.ds(2 * i + s, 1)].rearrange("p e k o -> p k e o"),
                                        M[s][:, 0:KD * E].rearrange("p (k e o) -> p k e o", k=KD, o=1)).then_inc(got, 1)

        with Phase(nc, "experts") as r:
            HP = [r.bank(f"H{i}") for i in range(2)]
            TP = [r.bank(f"T{i}") for i in range(2)]
            OP = [r.bank(f"O{i}") for i in range(2)]
            w1_s = [r.sb(f"w1_{i}", [P, KD, HID]) for i in range(2)]
            w2_s = [r.sb(f"w2_{i}", [P, Q, HID // (P * Q), D]) for i in range(2)]
            NQ = HID // (P * Q)
            b1_s = [r.sb(f"b1_{i}", [1, HID]) for i in range(2)]
            tok = r.sb("tok", [P, 2, KD, 32])
            ones = r.sb("ones", [1, 32])
            hid = r.sb("hid", [P, 2, 512])
            hidT = r.sb("hidT", [P, 2, NQ, P])
            o_sb = r.sb("o_sb", [P, 2, D])
            w1_in = [r.sem(f"w1_in{i}") for i in range(2)]
            w2_in = [r.sem(f"w2_in{i}") for i in range(2)]
            stored = [r.sem(f"stored{i}") for i in range(2)]
            zeroed, tok_ok, h_full, act_ok, ht_full, ht_ok, o_full, o_ok = (
                r.sem(n) for n in ("zeroed", "tok_ok", "h_full", "act_ok", "ht_full", "ht_ok", "o_full", "o_ok"))
            block = r.ctx.enter_context(nc.Block())

            @block.sync
            def _(sp):
                with sp.Fori(0, E // 2) as i:
                    for s in range(2):
                        e = 2 * i + s
                        sp.wait_ge(h_full, e + 1)
                        sp.dma_start(w1_s[s][:, :, :], w1[e, 0:D].rearrange("(p k) j -> p k j", k=KD)).then_inc(w1_in[s], 16)
                        sp.dma_start(b1_s[s][:, :], w1[e, D:D + 1]).then_inc(w1_in[s], 16)
                        sp.wait_ge(o_full, e + 1)
                        sp.dma_start(w2_s[s][:, :, :, :], w2[e, 0:HID].rearrange("(n p q) m -> p n q m", n=Q, q=NQ)).then_inc(w2_in[s], 16)

            @block.gpsimd
            def _(pool):
                pool.memset(tok[:, :, :, :], 0.0).then_inc(zeroed, 1)
                pool.memset(ones[:, :], 1.0).then_inc(zeroed, 1)

            @block.tensor
            def _(pe):
                pe.sem_inc(h_full, 2)
                pe.sem_inc(o_full, 2)
                pe.sem_inc(ht_full, 2)
                pe.wait_ge(zeroed, 2)

                def hidden(e, i, s):
                    pe.wait_ge(w1_in[s], 32 * i + 32)
                    pe.wait_ge(tok_ok, e + 1)
                    pe.wait_ge(act_ok, e + 1)
                    for k in range(KD):
                        for n in range(Q):
                            pe.matmul(HP[s][32 * n:32 * n + 32, :], tok[:, s, k, :], w1_s[s][:, k, n * 512:(n + 1) * 512],
                                      start=(k == 0), stop=False, tile_position=(0, 32 * n))
                    for n in range(Q):
                        mm = pe.matmul(HP[s][32 * n:32 * n + 32, :], ones[:, :], b1_s[s][:, n * 512:(n + 1) * 512],
                                       start=False, stop=True, tile_position=(0, 32 * n))
                    mm.then_inc(h_full, 1)

                def output(e, i, s):
                    pe.wait_ge(act_ok, e + 3)
                    pe.wait_ge(ht_ok, e + 1)
                    for q in range(NQ):
                        mm = pe.transpose(TP[s][:, q * P:(q + 1) * P], hid[:, s, q::NQ], ident[:, :])
                    mm.then_inc(ht_full, 1)
                    pe.wait_ge(w2_in[s], 16 * i + 16)
                    pe.wait_ge(ht_ok, e + 3)
                    pe.wait_ge(o_ok, e + 1)
                    for q in range(NQ):
                        for n in range(Q):
                            mm = pe.matmul(OP[s][32 * n:32 * n + 32, :], hidT[:, s, q, 32 * n:32 * n + 32], w2_s[s][:, n, q, :],
                                           start=(q == 0), stop=(q == NQ - 1), tile_position=(0, 32 * n))
                    mm.then_inc(o_full, 1)

                with pe.Fori(0, E // 2) as i:
                    for s in range(2):
                        hidden(2 * i + s, i, s)
                        output(2 * i + s, i, s)

            @block.scalar
            def _(act):
                act.sem_inc(act_ok, 2)
                for s in range(2):
                    act.sem_inc(stored[s], 16)
                with act.Fori(0, E // 2) as i:
                    for s in range(2):
                        e = 2 * i + s
                        act.wait_ge(h_full, 2 + e + 1)
                        act.wait_ge(ht_full, e + 1)
                        act.activation(hid[:, s, :], HP[s][:, :], ACT.Gelu).then_inc(act_ok, 1)
                        act.wait_ge(o_ok, 2 + e + 1)
                        for n in range(Q):
                            act.dma_start(out_d[:, n, bass.ds(e, 1), :].rearrange("b o d -> b (o d)"),
                                          o_sb[32 * n:32 * n + n_batch, s, :]).then_inc(stored[s], 16)
                for s in range(2):
                    act.wait_ge(stored[s], 16 + 16 * Q * E // 2)

            @block.vector
            def _(dve):
                for count in (ht_ok, o_ok):
                    dve.sem_inc(count, 2)
                dve.wait_ge(zeroed, 2)

                def tokens(e, s):
                    dve.tensor_copy(tok[:, s, :, 0:n_batch], merged[:, bass.ds(e, 1), :, :].rearrange("p o k b -> p (o k) b")).then_inc(tok_ok, 1)

                with dve.Fori(0, E // 2) as i:
                    for s in range(2):
                        e = 2 * i + s
                        dve.wait_ge(h_full, e + 1)
                        tokens(e, s)
                        dve.wait_ge(ht_full, 2 + e + 1)
                        dve.tensor_copy(hidT[:, s, :, :].rearrange("p q n -> p (q n)"), TP[s][:, :]).then_inc(ht_ok, 1)
                        dve.wait_ge(o_full, 2 + e + 1)
                        dve.wait_ge(stored[s], 16 + 16 * Q * i)
                        dve.tensor_copy(o_sb[:, s, :], OP[s][:, :]).then_inc(o_ok, 1)


def over_pairs(eng, n, body):
    if n > 2:
        with eng.Fori(0, n // 2 - 1) as i:
            for s in range(2):
                body(2 * i + s, i, s, False)
    for s in range(2):
        body(n - 2 + s, n // 2 - 1, s, s == 1)


def norm_attention_phase(nc, n_batch, x_in, x_out, consts, sel_d, out_d, w2, wq, bq, wk, bk, wv, bv):
    E, Q = out_d.shape[2], out_d.shape[1]
    HID = w2.shape[1] - 1
    NU = 3 * T
    ORDER = [("k", 0), ("v", 0), ("k", 1), ("v", 1), ("q", 0), ("q", 1)]
    NL = 9
    with Phase(nc, "norm") as ph:
        A = [ph.bank(f"A{i}") for i in range(2)]
        B = [ph.bank(f"B{i}") for i in range(2)]
        C = [ph.bank(f"C{i}") for i in range(3)]
        KV = ph.bank("KV")
        ident = ph.sb("ident", [P, P])
        w_stage = ph.sb("w_stage", [P, 3, KD, D])
        w = {n: [ph.sb(f"w{n}{i}", [P, KD, D], F32R) for i in "hl"] for n in "qkv"}
        bias = {n: ph.sb(f"b{n}", [P, D]) for n in "qkv"}
        b2 = ph.sb("b2", [E, D])
        x_ld = ph.sb("x_ld", [P, T, D])
        x3 = ph.sb("x3", [P, 2, T, D])
        xn = ph.sb("xn", [P, T, D])
        sel4 = ph.sb("sel4", [P, S])
        ob = ph.sb("ob", [P, D])
        stats = ph.sb("stats", [P, T, 6])
        mv = ph.sb("mv", [P, T, 2])
        rstd = ph.sb("rstd", [P, T])
        minus_half = ph.sb("minus_half", [P, T])
        wait_slot = ph.sb("wait_slot", [P, 1])
        xT = [ph.sb(f"xT{i}", [P, KD, S], F32R) for i in "hl"]
        t_sb = {n: ph.sb(f"{n}_sb", [P, T, D]) for n in "qkv"}
        prod = ph.sb("prod", [P, T, D])
        squares = ph.sb("squares", [P, D])
        ssq = ph.sb("ssq", [P, 2 * T])
        rn = ph.sb("rn", [P, 2 * T])
        names = ("const_in w_in w_full w_hi w_lo f_in ob_ok sc_full ln ln_pow xT_full hi_ok lo_ok p_full c_ok "
                 "sq_ok prod_ok rn_ok kv_full fin pool_const")
        (const_in, w_in, w_full, w_hi, w_lo, f_in, ob_ok, sc_full, ln, ln_pow, xT_full, hi_ok, lo_ok, p_full, c_ok,
         sq_ok, prod_ok, rn_ok, kv_full, fin, pool_const) = (ph.sem(n) for n in names.split())
        stored = [ph.sem(f"stored{i}") for i in range(2)]
        NW = 3 * KD
        block = ph.ctx.enter_context(nc.Block())

        @block.sync
        def _(sp):
            sp.dma_start(ident[:, :], consts["ident"]).then_inc(const_in, 16)
            for i, src in enumerate((wq, wk, wv)):
                sp.dma_start(w_stage[:, i, :, :], src.rearrange("(j p) d -> p j d", p=P)).then_inc(w_in, 16)
            for n, src in zip("qkv", (bq, bk, bv)):
                sp.dma_start(bias[n][:, :], src.partition_broadcast(P)).then_inc(const_in, 16)
            sp.dma_start(b2[:, :], w2[:, HID, :]).then_inc(const_in, 16)

            def load(n):
                sp.dma_start(x_ld[:, :, :], x_in[n].rearrange("(t p) d -> p t d", p=P)).then_inc(f_in, 16)
                sp.dma_start(ob[:, :], out_d[n].rearrange("n e d -> (n e) d")).then_inc(f_in, 16)
                for j in range(Q):
                    sp.dma_start(sel4[j * E:(j + 1) * E, :], sel_d[n]).then_inc(f_in, 16)

            load(0)

            def body(n, i, s, last):
                if not last:
                    sp.wait_ge(ln, NL * n + 2)
                    load(n + 1)
                sp.wait_ge(fin, 4 * n + 4)
                sp.dma_start(x_out[n].rearrange("(t p) d -> p t d", p=P), x3[:, s, :, :]).then_inc(stored[s], 16)
            over_pairs(sp, n_batch, body)
            for s in range(2):
                sp.wait_ge(stored[s], 16 + 8 * n_batch)

        @block.gpsimd
        def _(pool):
            pool.memset(minus_half[:, :], -0.5).then_inc(pool_const, 1)
            pool.wait_ge(pool_const, 1)

            def rstds(n):
                pool.wait_ge(ln, NL * n + 7)
                pool.tensor_tensor(rstd[:, :], rstd[:, :], minus_half[:, :], ALU.pow).then_inc(ln_pow, 1)

            rstds(0)

            def body(n, i, s, last):
                for t in range(T):
                    pool.wait_ge(c_ok, 3 + NU * n + 2 * t + 2)
                    pool.tensor_tensor(prod[:, t, :], t_sb["k"][:, t, :], t_sb["v"][:, t, :], ALU.mult).then_inc(prod_ok, 1)
                for j in range(2):
                    pool.wait_ge(sq_ok, 1 + 4 * n + 2 * j + 2)
                    pool.tensor_tensor(rn[:, 2 * j:2 * j + 2], ssq[:, 2 * j:2 * j + 2], minus_half[:, :], ALU.pow).then_inc(rn_ok, 1)
                if not last:
                    rstds(n + 1)
            over_pairs(pool, n_batch, body)

        @block.tensor
        def _(pe):
            pe.wait_ge(const_in, 16 * 5)
            pe.wait_ge(w_in, 48)
            for i in range(3):
                for k in range(KD):
                    u = i * KD + k
                    if u >= 2:
                        pe.wait_ge(w_lo, u - 1)
                    for j in range(4):
                        mm = pe.transpose(B[u % 2][:, j * P:(j + 1) * P], w_stage[:, i, j, k * P:(k + 1) * P], ident[:, :])
                    mm.then_inc(w_full, 1)
            pe.wait_ge(w_lo, NW)

            def spread(n):
                pe.wait_ge(ob_ok, n + 1)
                for t in range(T):
                    mm = pe.matmul(A[t][:, :], sel4[:, t * P:(t + 1) * P], ob[:, :], start=True, stop=True)
                mm.then_inc(sc_full, 1)

            def transposes(n):
                pe.wait_ge(ln, NL * n + NL)
                for j in range(2):
                    for kk in range(2):
                        for t in range(T):
                            k = 2 * j + kk
                            mm = pe.transpose(B[j][:, (kk * T + t) * P:(kk * T + t + 1) * P], xn[:, t, k * P:(k + 1) * P], ident[:, :])
                    mm.then_inc(xT_full, 1)

            spread(0)
            transposes(0)

            def body(n, i, s, last):
                pe.wait_ge(lo_ok, 2 * n + 2)
                for u, (which, t) in enumerate(ORDER):
                    pe.wait_ge(c_ok, NU * n + u + 1)
                    split_products(pe, C[u % 3][:, :], [
                        ((xT[0][:, k, t * P:(t + 1) * P], xT[1][:, k, t * P:(t + 1) * P]),
                         (w[which][0][:, k, :], w[which][1][:, k, :])) for k in range(KD)]).then_inc(p_full, 1)
                if not last:
                    spread(n + 1)
                pe.wait_ge(prod_ok, 2 * n + 2)
                pe.wait_ge(rn_ok, 2 * n + 1)
                for t in range(T):
                    mm = pe.matmul(KV[:, :], rn[:, t:t + 1].to_broadcast([P, P]), prod[:, t, :], start=(t == 0), stop=(t == T - 1))
                mm.then_inc(kv_full, 1)
                if not last:
                    transposes(n + 1)
            over_pairs(pe, n_batch, body)

        @block.scalar
        def _(act):
            act.sem_inc(sq_ok, 1)
            for u in range(NW):
                act.wait_ge(w_full, u + 1)
                act.activation(w["qkv"[u // KD]][0][:, u % KD, :], B[u % 2][:, :], ACT.Copy).then_inc(w_hi, 1)

            def take_hi(n):
                for j in range(2):
                    act.wait_ge(xT_full, 2 * n + j + 1)
                    act.activation(xT[0][:, 2 * j:2 * j + 2, :].rearrange("p k n -> p (k n)"), B[j][:, :], ACT.Copy).then_inc(hi_ok, 1)

            take_hi(0)

            def body(n, i, s, last):
                for j, (which, t, u) in enumerate((("k", 0, 0), ("k", 1, 2), ("q", 0, 4), ("q", 1, 5))):
                    act.wait_ge(c_ok, 3 + NU * n + u + 1)
                    act.wait_ge(sq_ok, 1 + 4 * n + j)
                    act.activation(squares[:, :], t_sb[which][:, t, :], ACT.Square, accum_out=ssq[:, j:j + 1]).then_inc(sq_ok, 1)
                if not last:
                    take_hi(n + 1)
            over_pairs(act, n_batch, body)

        @block.vector
        def _(dve):
            dve.sem_inc(c_ok, 3)
            for s in range(2):
                dve.sem_inc(stored[s], 16)
            for u in range(NW):
                parts = w["qkv"[u // KD]]
                dve.wait_ge(w_hi, u + 1)
                dve.tensor_tensor(parts[1][:, u % KD, :], B[u % 2][:, :], parts[0][:, u % KD, :], ALU.subtract).then_inc(w_lo, 1)
            dve.wait_ge(const_in, 16 * 5)

            def residual_and_stats(n, i, s):
                dve.wait_ge(f_in, 16 * (2 + Q) * (n + 1))
                dve.tensor_tensor(ob[0:E, :], ob[0:E, :], b2[:, :], ALU.add).then_inc(ob_ok, 1)
                dve.wait_ge(sc_full, n + 1)
                dve.wait_ge(stored[s], 16 + 16 * i)
                for t in range(T):
                    dve.tensor_tensor(x3[:, s, t, :], A[t][:, :], x_ld[:, t, :], ALU.add).then_inc(ln, 1)
                dve.wait_ge(ln, NL * n + 2)
                for t in range(T):
                    dve.bn_stats(stats[:, t, :], x3[:, s, t, :]).then_inc(ln, 1)
                dve.wait_ge(ln, NL * n + 4)
                dve.memset(wait_slot[:, :], 0.0)
                for t in range(T):
                    dve.bn_aggr(mv[:, t, :], stats[:, t, :]).then_inc(ln, 1)
                dve.wait_ge(ln, NL * n + 6)
                dve.tensor_scalar(rstd[:, :], mv[:, :, 1], EPS, None, ALU.add).then_inc(ln, 1)

            def apply_norm(n, s):
                dve.wait_ge(ln_pow, n + 1)
                for t in range(T):
                    dve.tensor_scalar(xn[:, t, :], x3[:, s, t, :], mv[:, t, 0:1], rstd[:, t:t + 1], ALU.subtract, ALU.mult).then_inc(ln, 1)

            def take_lo(n):
                for j in range(2):
                    dve.wait_ge(hi_ok, 2 * n + j + 1)
                    dve.tensor_tensor(xT[1][:, 2 * j:2 * j + 2, :].rearrange("p k n -> p (k n)"), B[j][:, :],
                                      xT[0][:, 2 * j:2 * j + 2, :].rearrange("p k n -> p (k n)"), ALU.subtract).then_inc(lo_ok, 1)

            residual_and_stats(0, 0, 0)
            apply_norm(0, 0)
            take_lo(0)

            def body(n, i, s, last):
                for u, (which, t) in enumerate(ORDER):
                    dve.wait_ge(p_full, NU * n + u + 1)
                    dve.tensor_tensor(t_sb[which][:, t, :], C[u % 3][:, :], bias[which][:, :], ALU.add).then_inc(c_ok, 1)
                if not last:
                    residual_and_stats(n + 1, i + s, 1 - s)
                dve.wait_ge(kv_full, n + 1)
                dve.wait_ge(rn_ok, 2 * n + 2)
                for t in range(T):
                    dve.tensor_tensor(t_sb["q"][:, t, :], KV[:, :], t_sb["q"][:, t, :], ALU.mult).then_inc(fin, 1)
                dve.wait_ge(fin, 4 * n + 2)
                for t in range(T):
                    dve.scalar_tensor_tensor(x3[:, s, t, :], t_sb["q"][:, t, :], rn[:, T + t:T + t + 1], x3[:, s, t, :], ALU.mult, ALU.add).then_inc(fin, 1)
                if not last:
                    apply_norm(n + 1, 1 - s)
                    take_lo(n + 1)
            over_pairs(dve, n_batch, body)


def fp8_linear_phase(nc, n_batch, x_in, x_out, consts, weight, bias):
    NL = 9
    with Phase(nc, "fp8") as ph:
        B = [ph.bank(f"B{i}", BF16) for i in range(2)]
        O = [ph.bank(f"O{i}") for i in range(4)]
        ident_b = ph.sb("ident_b", [P, P], BF16)
        w_f = ph.sb("w_f", [P, KD, D])
        small = ph.sb("small", [P, KD, D])
        large = ph.sb("large", [P, KD, D])
        w8 = ph.sb("w8", [P, KD, D], FP8)
        wb = ph.sb("wb", [P, KD, D], BF16)
        wT = ph.sb("wT", [P, KD, D], BF16)
        bias_r = ph.sb("bias_r", [P, D])
        x_t = ph.sb("x_t", [P, 2, T, D])
        x8 = ph.sb("x8", [P, 2, T, D], FP8)
        xb = ph.sb("xb", [P, 2, T, D], BF16)
        xT = ph.sb("xT", [P, 2, KD, S], BF16)
        y16 = ph.sb("y16", [P, 2, T, D], F16)
        stats = ph.sb("stats", [P, T, 6])
        mv = ph.sb("mv", [P, T, 2])
        rstd = ph.sb("rstd", [P, T])
        minus_half = ph.sb("minus_half", [P, T])
        wait_slot = ph.sb("wait_slot", [P, 1])
        (const_in, w_step, wT_full, wT_ok, ln, ln_pow, xT_full, xT_ok, o_full, y_ok, fin, pool_const) = (
            ph.sem(n) for n in "const_in w_step wT_full wT_ok ln ln_pow xT_full xT_ok o_full y_ok fin pool_const".split())
        x_ok = [ph.sem(f"x_ok{i}") for i in range(2)]
        stored = [ph.sem(f"stored{i}") for i in range(2)]
        block = ph.ctx.enter_context(nc.Block())

        @block.sync
        def _(sp):
            sp.dma_start(ident_b[:, :], consts["ident_b"]).then_inc(const_in, 16)
            sp.dma_start(w_f[:, :, :], weight.rearrange("(j p) d -> p j d", p=P)).then_inc(const_in, 16)
            sp.dma_start(bias_r[:, :], bias.partition_broadcast(P)).then_inc(const_in, 16)
            for s in range(2):
                sp.sem_inc(stored[s], 16)
            with sp.Fori(0, n_batch // 2) as i:
                for s in range(2):
                    sp.wait_ge(stored[s], 16 + 16 * i)
                    sp.dma_start(x_t[:, s, :, :], x_in[2 * i + s].rearrange("(t p) d -> p t d", p=P)).then_inc(x_ok[s], 16)
            for s in range(2):
                sp.wait_ge(stored[s], 16 + 8 * n_batch)

        @block.gpsimd
        def _(pool):
            pool.sem_inc(fin, 4)
            pool.memset(minus_half[:, :], -0.5).then_inc(pool_const, 1)
            pool.wait_ge(pool_const, 1)
            pool.wait_ge(const_in, 48)

            def rstds(n):
                pool.wait_ge(ln, NL * n + 5)
                pool.tensor_tensor(rstd[:, :], rstd[:, :], minus_half[:, :], ALU.pow).then_inc(ln_pow, 1)

            rstds(0)

            def body(n, i, s, last):
                if not last:
                    rstds(n + 1)
                for t in range(T):
                    pool.wait_ge(y_ok, 2 * T + T * n + t + 1)
                    pool.tensor_tensor(x_t[:, s, t, :], x_t[:, s, t, :], y16[:, s, t, :], ALU.add).then_inc(fin, 1)
            over_pairs(pool, n_batch, body)

        @block.tensor
        def _(pe):
            pe.wait_ge(const_in, 48)
            pe.wait_ge(w_step, 9)
            for k in range(KD):
                if k >= 2:
                    pe.wait_ge(wT_ok, k - 1)
                for j in range(4):
                    mm = pe.transpose(B[k % 2][:, j * P:(j + 1) * P], wb[:, j, k * P:(k + 1) * P], ident_b[:, :])
                mm.then_inc(wT_full, 1)
            pe.wait_ge(wT_ok, KD)
            pe.sem_inc(xT_full, 2)
            with pe.Fori(0, n_batch // 2) as i:
                for s in range(2):
                    n = 2 * i + s
                    pe.wait_ge(ln, NL * n + 9)
                    pe.wait_ge(xT_ok, n + 1)
                    for k in range(KD):
                        for t in range(T):
                            mm = pe.transpose(B[s][:, (k * T + t) * P:(k * T + t + 1) * P], xb[:, s, t, k * P:(k + 1) * P], ident_b[:, :])
                    mm.then_inc(xT_full, 1)
                    pe.wait_ge(xT_ok, n + 3)
                    pe.wait_ge(y_ok, T * n + T)
                    for t in range(T):
                        for k in range(KD):
                            mm = pe.matmul(O[2 * s + t][:, :], xT[:, s, k, t * P:(t + 1) * P], wT[:, k, :], start=(k == 0), stop=(k == KD - 1))
                    mm.then_inc(o_full, 1)

        @block.scalar
        def _(act):
            act.sem_inc(xT_ok, 2)
            for k in range(KD):
                act.wait_ge(wT_full, k + 1)
                act.activation(wT[:, k, :], B[k % 2][:, 0:D], ACT.Copy).then_inc(wT_ok, 1)
            with act.Fori(0, n_batch // 2) as i:
                for s in range(2):
                    n = 2 * i + s
                    act.wait_ge(xT_full, 2 + n + 1)
                    act.activation(xT[:, s, :, :].rearrange("p k n -> p (k n)"), B[s][:, :], ACT.Copy).then_inc(xT_ok, 1)
                    act.wait_ge(fin, 4 + T * n + T)
                    act.dma_start(x_out[n].rearrange("(t p) d -> p t d", p=P), x_t[:, s, :, :]).then_inc(stored[s], 16)

        @block.vector
        def _(dve):
            dve.wait_ge(const_in, 48)
            steps = [
                lambda: dve.tensor_scalar(small[:, :, :], w_f[:, :, :], 240.0, -240.0, ALU.min, ALU.max),
                lambda: dve.tensor_copy(w8[:, :, :], small[:, :, :], saturate=False),
                lambda: dve.tensor_copy(small[:, :, :], w8[:, :, :]),
                lambda: dve.tensor_scalar(large[:, :, :], w_f[:, :, :], 448.0, -448.0, ALU.min, ALU.max),
            ]
            n = 0
            for step in steps:
                n += 1
                step().then_inc(w_step, 1)
                dve.wait_ge(w_step, n)
            dve.tensor_scalar(w8[:, :, :], large[:, :, :], 0.5, None, ALU.mult, saturate=False).then_inc(w_step, 1)
            dve.wait_ge(w_step, 5)
            dve.scalar_tensor_tensor(large[:, :, :], w8[:, :, :], 2.0, small[:, :, :], ALU.mult, ALU.subtract).then_inc(w_step, 1)
            dve.tensor_tensor(w_f[:, :, :], w_f[:, :, :], w_f[:, :, :], ALU.mult).then_inc(w_step, 1)
            dve.wait_ge(w_step, 7)
            dve.tensor_scalar(w_f[:, :, :], w_f[:, :, :], 256.0, None, ALU.is_ge).then_inc(w_step, 1)
            dve.wait_ge(w_step, 8)
            dve.tensor_tensor(large[:, :, :], large[:, :, :], w_f[:, :, :], ALU.mult).then_inc(pool_const, 1)
            dve.wait_ge(pool_const, 2)
            dve.tensor_tensor(wb[:, :, :], large[:, :, :], small[:, :, :], ALU.add).then_inc(w_step, 1)
            dve.sem_inc(y_ok, 2 * T)

            def norm(n, i, s):
                dve.wait_ge(x_ok[s], 16 * i + 16)
                for t in range(T):
                    dve.bn_stats(stats[:, t, :], x_t[:, s, t, :]).then_inc(ln, 1)
                dve.wait_ge(ln, NL * n + 2)
                dve.memset(wait_slot[:, :], 0.0)
                for t in range(T):
                    dve.bn_aggr(mv[:, t, :], stats[:, t, :]).then_inc(ln, 1)
                dve.wait_ge(ln, NL * n + 4)
                dve.tensor_scalar(rstd[:, :], mv[:, :, 1], EPS, None, ALU.add).then_inc(ln, 1)
                dve.wait_ge(ln_pow, n + 1)
                dve.memset(wait_slot[:, :], 0.0)
                for t in range(T):
                    dve.tensor_scalar(x8[:, s, t, :], x_t[:, s, t, :], mv[:, t, 0:1], rstd[:, t:t + 1], ALU.subtract, ALU.mult, saturate=False).then_inc(ln, 1)
                dve.wait_ge(ln, NL * n + 7)
                dve.memset(wait_slot[:, :], 0.0)
                for t in range(T):
                    dve.tensor_copy(xb[:, s, t, :], x8[:, s, t, :]).then_inc(ln, 1)

            norm(0, 0, 0)

            def body(n, i, s, last):
                if not last:
                    norm(n + 1, i + s, 1 - s)
                for t in range(T):
                    dve.tensor_tensor(x_t[:, s, t, :], x_t[:, s, t, :], bias_r[:, :], ALU.add)
                dve.wait_ge(o_full, n + 1)
                dve.wait_ge(fin, T * n + T)
                for t in range(T):
                    dve.tensor_copy(y16[:, s, t, :], O[2 * s + t][:, :]).then_inc(y_ok, 1)
            over_pairs(dve, n_batch, body)


def constants():
    bf16 = np.dtype("bfloat16")
    pos = np.arange(S, dtype=np.float32)
    half = 32
    freq = np.power(np.float32(ROPE_BASE), np.arange(half, dtype=np.float32) / np.float32(half)).astype(np.float32)
    angles = pos[:, None] / np.concatenate([freq, freq])[None, :]
    sign = np.concatenate([-np.ones(half), np.ones(half)]).astype(np.float32)

    def rows(a):
        return np.ascontiguousarray(a.reshape(T, P, -1).transpose(1, 0, 2))
    return {
        "ident": np.eye(P, dtype=np.float32),
        "ident_b": np.eye(P).astype(bf16),
        "mask_b": np.triu(np.full((P, P), -1e9), 1).astype(bf16),
        "cos": rows(np.cos(angles).astype(np.float32)),
        "sin": rows((np.sin(angles) * sign).astype(np.float32)),
    }


def decoder(nc, a, c, out, n_batch):
    def scratch(name, shape):
        return nc.dram_tensor(name, shape, F32, kind="Internal").ap()
    def self0(x, y):
        attention_phase(nc, "self0", n_batch, x, y, c, a["L0_attn_W_Q"], a["L0_attn_W_K"], a["L0_attn_W_V"], a["L0_attn_W_O"],
                        64, True, True, bq=a["L0_attn_b_Q"], bk=a["L0_attn_b_K"], bv=a["L0_attn_b_V"], bo=a["L0_attn_b_O"],
                        rope=(c["cos"], c["sin"]))

    def cross0(x, y):
        attention_phase(nc, "cross0", n_batch, x, y, c, a["L0_xattn_Wq"], a["L0_xattn_Wk"], a["L0_xattn_Wv"], a["L0_xattn_Wo"],
                        32, True, False, ctx=a["ctx_1024"])

    def cross1(x, y):
        attention_phase(nc, "cross1", n_batch, x, y, c, a["L1_xattn_Wq"], a["L1_xattn_Wk"], a["L1_xattn_Wv"], a["L1_xattn_Wo"],
                        32, False, False, ctx=a["ctx_1024"], bq=a["L1_xattn_bq"], bk=a["L1_xattn_bk"], bv=a["L1_xattn_bv"],
                        bo=a["L1_xattn_bo"])

    E, HID = a["L0_ffn_w1"].shape[0], a["L0_ffn_w1"].shape[2]
    logits_d, sel_d = scratch("logits", (n_batch, E, S)), scratch("sel", (n_batch, E, S))
    selT_d = scratch("selT", (n_batch, T, P, E))
    out_d = scratch("experts_out", (n_batch, HID // 512, E, D))
    x_norm = scratch("x_norm", (n_batch, S, D))

    def experts(x):
        expert_phase(nc, n_batch, x, x_norm, c, a["L0_ffn_gate_w"], a["L0_ffn_gate_b"], a["L0_ffn_w1"], a["L0_ffn_w2"],
                     logits_d, sel_d, selT_d, out_d)

    def norm1(x, y):
        norm_attention_phase(nc, n_batch, x, y, c, sel_d, out_d, a["L0_ffn_w2"], a["L1_attn_Wq"], a["L1_attn_bq"],
                             a["L1_attn_Wk"], a["L1_attn_bk"], a["L1_attn_Wv"], a["L1_attn_bv"])

    def fp8(x, y):
        fp8_linear_phase(nc, n_batch, x, y, c, a["L1_ffn_weight"], a["L1_ffn_bias"])

    x1, x2, x4, x5 = (scratch(f"x{i}", (n_batch, S, D)) for i in (1, 2, 4, 5))
    self0(a["x"], x1)
    cross0(x1, x2)
    experts(x2)
    norm1(x2, x4)
    cross1(x4, x5)
    fp8(x5, out)

def kernel(**inputs):
    import concourse.bacc as bacc
    from concourse.bass_utils import run_bass_kernel_spmd

    nc = bacc.Bacc("TRN2", target_bir_lowering=False, num_devices=1)
    arrays, a, c = {}, {}, {}
    for group, made in ((a, inputs), (c, constants())):
        for name, value in made.items():
            value = np.ascontiguousarray(value)
            arrays[f"in_{name}"] = value
            group[name] = nc.dram_tensor(f"in_{name}", value.shape, mybir.dt.from_np(value.dtype), kind="ExternalInput").ap()
    n_batch = a["x"].shape[0]
    out = nc.dram_tensor("out_x", (n_batch, S, D), F32, kind="ExternalOutput").ap()
    decoder(nc, a, c, out, n_batch)
    r = run_bass_kernel_spmd(nc, [arrays], core_ids=[0])
    return r.results[0]["out_x"]
```

```python
from contextlib import ExitStack

import numpy as np

import concourse.bass as bass
from concourse import mybir

F32 = mybir.dt.float32
F32R = mybir.dt.float32r
BF16 = mybir.dt.bfloat16
F16 = mybir.dt.float16
FP8 = mybir.dt.float8e4
ALU = mybir.AluOpType
ACT = mybir.ActivationFunctionType
AX = mybir.AxisListType

P = 128
D = 512
KD = D // P
S = 256
T = S // P
H = 16
EPS = 1e-5
ROPE_BASE = 10000.0


class Phase:

    def __init__(self, nc, name):
        self.nc, self.name, self.ctx, self.sems = nc, name, ExitStack(), []

    def __enter__(self):
        self.ctx.__enter__()
        self.ctx.callback(self.clear)
        return self

    def __exit__(self, *a):
        return self.ctx.__exit__(*a)

    def clear(self):
        self.nc.clear_and_free_semaphores(self.sems)
        self.nc.all_engine_barrier()

    def sb(self, name, shape, dt=F32):
        return self.ctx.enter_context(self.nc.sbuf_tensor(f"{self.name}_{name}", shape, dt))

    def bank(self, name, dt=F32):
        return self.ctx.enter_context(self.nc.psum_tensor(f"{self.name}_{name}", [P, 2048 // (2 if dt == BF16 else 4)], dt))

    def sem(self, name):
        self.sems.append(self.nc.alloc_semaphore(name=f"{self.name}_{name}"))
        return self.sems[-1]


def over_batches(eng, n, body):
    if n > 1:
        with eng.Fori(0, n - 1) as b:
            body(b, False)
    body(n - 1, True)


def split_products(pe, out, pairs):
    for i, ((ah, al), (bh, bl)) in enumerate(pairs):
        first, last = i == 0, i == len(pairs) - 1
        pe.matmul(out, ah, bh, start=first, stop=False)
        pe.matmul(out, ah, bl, start=False, stop=False)
        mm = pe.matmul(out, al, bh, start=False, stop=last)
    return mm


def after(eng, sem, value):
    if not isinstance(value, int) or value > 0:
        eng.wait_ge(sem, value)


def over_rotated(eng, n, body, tail):
    body(0, True, False)
    if n > 2:
        with eng.Fori(1, n - 1) as b:
            body(b, False, False)
    body(n - 1, False, True)
    tail(n)


class Uses:

    def __init__(self, plan, before, n_batch):
        self.keys = [k for step in plan for k in step]
        self.before, self.n, self.n_batch = before, len(self.keys), n_batch
        self.n_out = sum(k[0] == "O" for k in self.keys)
        assert self.n % 2 == 0 and self.n_out % 2 == 0

    def here(self, b, first, last):
        if isinstance(b, int) and b == self.n_batch:
            return [k for k in self.keys if k[0] == "O"]
        return [k for k in self.keys if not (first and k[0] == "O") and not (last and k[0] == "+")]

    def start(self, b):
        if isinstance(b, int) and b == 0:
            return self.before
        if isinstance(b, int) and b == self.n_batch:
            return self.start(b - 1) + len(self.here(b - 1, False, True))
        return self.before - self.n_out + b * self.n

    def at(self, key, b, first, last):
        return self.start(b) + self.here(b, first, last).index(key)

    def bank(self, key, b, first, last):
        b = b if isinstance(b, int) else 2
        return self.at(key, b, first, last) % 2


def attention_phase(nc, name, n_batch, x_in, x_out, consts, wq, wk, wv, wo,
                    d_head, causal, rotary, ctx=None, bq=None, bk=None, bv=None, bo=None, rope=None):
    HD = H * d_head
    CH = HD // 512
    HPT = P // d_head
    NT = H // HPT
    SCALE = 1.0 / float(np.sqrt(d_head))
    T_LAG, V_LAG, Z_LAG = 3, 5, 6
    KQ = [P * (t + 1) if causal else S for t in range(T)]
    SOFF = [sum(KQ[:t]) for t in range(T)]
    SW = sum(KQ)
    QK = [P * k if causal else 0 for k in range(T)]
    TOFF = [sum(S - QK[j] for j in range(k)) for k in range(T)]
    NP = 4
    NPT = 2 if rotary else 4
    N_LN = KD // 2
    PLAN = [[] for _ in range(H)]
    if rotary:
        for g in range(1, NT):
            PLAN[2 * g - 2].append(("Q", g))
        for i, key in ((0, (0, 1, 0)), (1, (0, 1, 1)), (2, (1, 1, 0)), (3, (1, 1, 1))):
            PLAN[i].append(("P",) + key)
        PLAN[5] += [("V", 1, 0), ("V", 1, 1)]
        PLAN[6] += [("O", 0), ("O", 1)]
        PLAN[9] += [("+", "X", 0), ("+", "X", 1)]
        for i, key in ((10, (0, 0, 0)), (11, (0, 0, 1)), (11, (1, 0, 0)), (12, (1, 0, 1))):
            PLAN[i].append(("+", "P") + key)
        PLAN[13] += [("+", "V", 0, 0), ("+", "V", 0, 1)]
        PLAN[14].append(("+", "Q", 0))
        BEFORE = [("X", 0), ("X", 1), ("P", 0, 0, 0), ("P", 0, 0, 1), ("P", 1, 0, 0), ("P", 1, 0, 1),
                  ("V", 0, 0), ("V", 0, 1), ("Q", 0)]
        STATS_AT, APPLY_AT = 4, 7
        LATE_V = {H // 2: ("V", 1, 1)}
    else:
        PLAN[1] += [("Q", 1)]
        PLAN[5] += [("V", 0, 0), ("V", 0, 1)]
        PLAN[6] += [("Q", 2)]
        PLAN[7] += [("O", 0), ("O", 1)]
        PLAN[9] += [("Q", 3)]
        PLAN[11] += [("+", "X", 0), ("+", "X", 1)]
        PLAN[12] += [("+", "C", 0), ("+", "C", 1)]
        PLAN[14] += [("+", "Q", 0)]
        BEFORE = [("X", 0), ("X", 1), ("C", 0), ("C", 1), ("Q", 0)]
        STATS_AT, APPLY_AT = 6, 9
        LATE_V = {0: ("V", 0, 1)}
    N_W = 0 if rotary else 4 * KD
    uses = Uses(PLAN, N_W + len(BEFORE), n_batch)
    with_act = [k for k in uses.keys if k[k[0] == "+"] in "QXC"]
    before_act = [k for k in BEFORE if k[0] in "QXC"]
    P_PER = 4 * CH
    P_BEFORE = 4

    def hi_at(key, b, last):
        here = [k for k in with_act if not (last and k[0] == "+")]
        return N_W + len(before_act) + b * len(with_act) + here.index(key)

    with Phase(nc, name) as ph:
        A = [ph.bank(f"A{i}") for i in range(2)]
        SC = [ph.bank(f"S{i}") for i in range(2)]
        TP = [ph.bank(f"T{i}") for i in range(2)]
        Z = [ph.bank(f"Z{i}") for i in range(2)]

        ident = ph.sb("ident", [P, P])
        ident_b = ph.sb("ident_b", [P, P], BF16)
        mask_b = ph.sb("mask_b", [P, P], BF16)
        x_t = ph.sb("x_t", [P, T, D])
        res = ph.sb("res", [P, T, D])
        stats = ph.sb("stats", [P, T, 6])
        mv = ph.sb("mv", [P, T, 2])
        rstd = ph.sb("rstd", [P, T])
        wait_slot = ph.sb("wait_slot", [P, 1])
        minus_half = ph.sb("minus_half", [P, T])
        xT = [ph.sb(f"xT{i}", [P, KD, S], F32R) for i in "hl"]
        V = ph.sb("V", [P, T, HD])
        n_qt = 4
        n_kt = n_qt * HPT
        QT = ph.sb("QT", [P, n_qt, S])
        KT = ph.sb("KT", [P, n_kt, S])
        neg_max = ph.sb("neg_max", [P, H, T])
        sums = ph.sb("sums", [P, H, T])
        rsum = ph.sb("rsum", [P, H, T])
        prob = ph.sb("prob", [P, NP, SW])
        probT = ph.sb("probT", [P, NPT, SW])
        wvs = [ph.sb(f"wv{i}", [P, KD, HD], F32R) for i in "hl"]
        wqs = [ph.sb(f"wq{i}", [P, KD, HD], F32R) for i in "hl"]
        wks = [ph.sb(f"wk{i}", [P, KD, HD], F32R) for i in "hl"]
        if rotary:
            q_t = ph.sb("q_t", [P, T, HD])
            k_t = ph.sb("k_t", [P, T, HD])
            turn = ph.sb("turn", [P, 2, 512])
            cos = ph.sb("cos", [P, T, d_head])
            sin = ph.sb("sin", [P, T, d_head])
            rb = ph.sb("rb", [P, 2, T, HD])
            wo_f = ph.sb("wo_f", [P, NT, D])
            zT = ph.sb("zT", [P, NT, S])
            stage = [q_t, k_t, V]
        else:
            c_t = ph.sb("c_t", [P, T, D])
            cT = [ph.sb(f"cT{i}", [P, KD, S], F32R) for i in "hl"]
            wos = [ph.sb(f"wo{i}", [P, KD, D], F32R) for i in "hl"]
            zTs = [ph.sb(f"zT{i}", [P, NT, S], F32R) for i in "hl"]
            w_stage = ph.sb("w_stage", [P, 4, KD, D])
        if bq is not None and not rotary:
            bq_c = ph.sb("bq_c", [P, NT])
            bk_c = ph.sb("bk_c", [P, NT])
        if bv is not None:
            bv_c = ph.sb("bv_c", [P, NT])
        if bo is not None:
            bo_r = ph.sb("bo_r", [P, D])

        const_in = ph.sem("const_in")
        w_in = [ph.sem(f"w_in{i}") for i in range(3)]
        wo_in = ph.sem("wo_in")
        w_hi = ph.sem("w_hi")
        w_lo = ph.sem("w_lo")
        x_ok = ph.sem("x_ok")
        c_ok = ph.sem("c_ok")
        res_in = ph.sem("res_in")
        res_b = ph.sem("res_b")
        stored = ph.sem("stored")
        ln = ph.sem("ln")
        ln_pow = ph.sem("ln_pow")
        a_full = ph.sem("a_full")
        a_hi = ph.sem("a_hi")
        a_free = ph.sem("a_free")
        rot = ph.sem("rot")
        rb_ok = ph.sem("rb_ok")
        zeroed = ph.sem("zeroed")
        s_full = ph.sem("s_full")
        max_ok = ph.sem("max_ok")
        exp_ok = ph.sem("exp_ok")
        rsum_ok = ph.sem("rsum_ok")
        norm_ok = ph.sem("norm_ok")
        t_full = ph.sem("t_full")
        pt_even = ph.sem("pt_even")
        pt_odd = ph.sem("pt_odd")
        pv_ok = ph.sem("pv_ok")
        pool_const = ph.sem("pool_const")
        z_hi = ph.sem("z_hi")
        z_ok = ph.sem("z_ok")

        N_CONST = 3 + (2 if rotary else 0) + sum(v is not None for v in (bv, bo)) \
            + (0 if bq is None else 4 if rotary else 2)
        N_STAGE = 3 * 2 if rotary else 4

        block = ph.ctx.enter_context(nc.Block())

        @block.sync
        def _(sp):
            sp.dma_start(ident[:, :], consts["ident"]).then_inc(const_in, 16)
            sp.dma_start(ident_b[:, :], consts["ident_b"]).then_inc(const_in, 16)
            sp.dma_start(mask_b[:, :], consts["mask_b"]).then_inc(const_in, 16)
            sp.dma_start(x_t[:, :, :], x_in[0].rearrange("(t p) d -> p t d", p=P)).then_inc(x_ok, 16)
            if rotary:
                for i in range(N_STAGE):
                    w = (wq, wk, wv)[i // 2]
                    if i >= 3:
                        sp.wait_ge(w_lo, i - 2)
                    hh = i % 2
                    for k in range(KD):
                        sp.dma_start(
                            stage[i % 3][:, :, :].rearrange("p t n -> p (t n)")[:, k * 512:(k + 1) * 512].rearrange("p (h e) -> p h e", e=d_head),
                            w[hh * H // 2:(hh + 1) * H // 2, k * P:(k + 1) * P, :].rearrange("h p e -> p h e"),
                        ).then_inc(w_in[i % 3], 16)
                    if i == 2:
                        sp.dma_start(cos[:, :, :], rope[0]).then_inc(const_in, 16)
                        sp.dma_start(sin[:, :, :], rope[1]).then_inc(const_in, 16)
                        for j, b_ in enumerate((bq, bk)):
                            for t in range(T):
                                sp.dma_start(rb[:, j, t, :], b_.rearrange("h k -> (h k)").partition_broadcast(P)).then_inc(const_in, 16)
                        sp.dma_start(bv_c[:, :], bv.rearrange("h k -> (h k)").rearrange("(t p) -> p t", p=P),
                                     allow_slow_non_contiguous=True).then_inc(const_in, 16)
                        sp.dma_start(bo_r[:, :], bo.partition_broadcast(P)).then_inc(const_in, 16)
                sp.dma_start(wo_f[:, :, :], wo.rearrange("h e m -> (h e) m").rearrange("(k p) m -> p k m", p=P)).then_inc(wo_in, 16)
            else:
                for v, col in ((bq, "bq_c"), (bk, "bk_c"), (bv, "bv_c")):
                    if v is not None:
                        to = {"bq_c": bq_c, "bk_c": bk_c, "bv_c": bv_c}[col]
                        sp.dma_start(to[:, :], v.rearrange("(t p) -> p t", p=P), allow_slow_non_contiguous=True).then_inc(const_in, 16)
                if bo is not None:
                    sp.dma_start(bo_r[:, :], bo.partition_broadcast(P)).then_inc(const_in, 16)
                for i, w in enumerate((wq, wk, wv, wo)):
                    sp.dma_start(w_stage[:, i, :, :], w.rearrange("(j p) d -> p j d", p=P)).then_inc(w_in[0], 16)
                sp.dma_start(c_t[:, :, :], ctx[0].rearrange("(t p) d -> p t d", p=P)).then_inc(c_ok, 16)

            def store(b, first, last):
                sp.wait_ge(a_free, uses.at(("O", 1), b, first, last) + 1)
                sp.dma_start(x_out[b - 1].rearrange("(t p) d -> p t d", p=P), res[:, :, :]).then_inc(stored, 16)
                sp.wait_ge(stored, b * 16)

            def body(b, first, last):
                if not last:
                    sp.wait_ge(a_full, uses.start(b))
                    sp.dma_start(x_t[:, :, :], x_in[b + 1].rearrange("(t p) d -> p t d", p=P)).then_inc(x_ok, 16)
                    if not rotary:
                        sp.dma_start(c_t[:, :, :], ctx[b + 1].rearrange("(t p) d -> p t d", p=P)).then_inc(c_ok, 16)
                if not first:
                    store(b, first, last)
                sp.dma_start(res[:, :, :], x_in[b].rearrange("(t p) d -> p t d", p=P)).then_inc(res_in, 16)

            over_rotated(sp, n_batch, body, lambda b: store(b, False, False))

        @block.gpsimd
        def _(pool):
            def rstds(n):
                pool.wait_ge(ln, 7 * n + 5)
                pool.tensor_tensor(rstd[:, :], rstd[:, :], minus_half[:, :], ALU.pow).then_inc(ln_pow, 1)

            pool.memset(minus_half[:, :], -0.5).then_inc(pool_const, 1)
            pool.wait_ge(pool_const, 1)
            rstds(0)
            pool.wait_ge(const_in, 16 * N_CONST)
            if rotary:
                pool.wait_ge(rb_ok, 3 * 2 * T * CH)

            def turned(key, u, seq):
                _, which, c, t = key
                dst = (q_t, k_t)[which][:, t, c * 512:(c + 1) * 512]
                pool.wait_ge(a_free, u + 1)
                pool.tensor_tensor(dst, dst, turn[:, t % 2, :], ALU.add).then_inc(rot, 1)
                pool.wait_ge(rot, 2 * seq + 1)
                pool.tensor_tensor(dst, dst, rb[:, which, t, c * 512:(c + 1) * 512], ALU.add).then_inc(rot, 1)

            for key in BEFORE:
                if key[0] == "P":
                    turned(key, N_W + BEFORE.index(key), [k for k in BEFORE if k[0] == "P"].index(key))

            def body(b, first, last):
                seq = 0
                for i in range(H):
                    for key in PLAN[i]:
                        ahead = key[0] == "+"
                        if key[ahead] == "P" and not (ahead and last):
                            turned(key[ahead:], uses.at(key, b, first, last), P_BEFORE + b * P_PER + seq)
                            seq += 1
                    if i == STATS_AT and not last:
                        rstds(b + 1)
                    pool.wait_ge(rsum_ok, b * H + i + 1)
                    for t in range(T):
                        pr = prob[:, i % NP, SOFF[t]:SOFF[t] + KQ[t]]
                        ins = pool.tensor_tensor(pr, pr, rsum[:, i, t:t + 1].to_broadcast([P, KQ[t]]), ALU.mult)
                    ins.then_inc(norm_ok, 1)
                if bo is not None:
                    pool.wait_ge(res_in, b * 16 + 16)
                    for t in range(T):
                        pool.tensor_tensor(res[:, t, :], res[:, t, :], bo_r[:, :], ALU.add).then_inc(res_b, 1)
            over_rotated(pool, n_batch, body, lambda b: None)

        @block.tensor
        def _(pe):
            pe.wait_ge(const_in, 16 * N_CONST)

            def bank_for(u):
                after(pe, a_free, u - 1)

            def proj_tokens(u, bank, src, w, t, c):
                bank_for(u)
                split_products(pe, A[bank][:, :], [
                    ((src[0][:, k, t * P:(t + 1) * P], src[1][:, k, t * P:(t + 1) * P]),
                     (w[0][:, k, c * 512:(c + 1) * 512], w[1][:, k, c * 512:(c + 1) * 512])) for k in range(KD)
                ]).then_inc(a_full, 1)

            def extra(key, u, bank, n):
                kind = key[0]
                if kind in "XC":
                    if kind == "X":
                        pe.wait_ge(ln, n * 7 + 7)
                    else:
                        pe.wait_ge(c_ok, n * 16 + 16)
                    bank_for(u)
                    src = x_t if kind == "X" else c_t
                    for kk in range(2):
                        for t in range(T):
                            k = 2 * key[1] + kk
                            mm = pe.transpose(A[bank][:, (kk * T + t) * P:(kk * T + t + 1) * P], src[:, t, k * P:(k + 1) * P], ident[:, :])
                    mm.then_inc(a_full, 1)
                elif kind == "P":
                    proj_tokens(u, bank, xT, (wqs, wks)[key[1]], key[3], key[2])
                elif kind == "V":
                    proj_tokens(u, bank, xT if rotary else cT, wvs, key[2], key[1])
                elif kind == "Q" and rotary:
                    g = key[1]
                    pe.wait_ge(rot, 2 * (P_BEFORE + n * P_PER + (P_PER // CH) * (g // (NT // CH))))
                    bank_for(u)
                    for j, src in enumerate((q_t, k_t)):
                        for t in range(T):
                            mm = pe.transpose(A[bank][:, (j * T + t) * P:(j * T + t + 1) * P], src[:, t, g * P:(g + 1) * P], ident[:, :])
                    mm.then_inc(a_full, 1)
                elif kind == "Q":
                    g = key[1]
                    bank_for(u)
                    for j, (w, src) in enumerate(((wqs, xT), (wks, cT))):
                        mm = split_products(pe, A[bank][:, j * S:(j + 1) * S], [
                            ((w[0][:, k, g * P:(g + 1) * P], w[1][:, k, g * P:(g + 1) * P]),
                             (src[0][:, k, :], src[1][:, k, :])) for k in range(KD)])
                    mm.then_inc(a_full, 1)
                elif kind == "O":
                    t = key[1]
                    pe.wait_ge(z_ok, n * NT + NT)
                    bank_for(u)
                    if rotary:
                        for k in range(NT):
                            mm = pe.matmul(A[bank][:, :], zT[:, k, t * P:(t + 1) * P], wo_f[:, k, :], start=(k == 0), stop=(k == NT - 1))
                        mm.then_inc(a_full, 1)
                    else:
                        split_products(pe, A[bank][:, :], [
                            ((zTs[0][:, k, t * P:(t + 1) * P], zTs[1][:, k, t * P:(t + 1) * P]),
                             (wos[0][:, k, :], wos[1][:, k, :])) for k in range(KD)]).then_inc(a_full, 1)

            if not rotary:
                pe.wait_ge(w_in[0], 16 * 4)
                for u in range(N_W):
                    i, k = u // KD, u % KD
                    bank_for(u)
                    for j in range(4):
                        mm = pe.transpose(A[u % 2][:, j * P:(j + 1) * P], w_stage[:, i, j, k * P:(k + 1) * P], ident[:, :])
                    mm.then_inc(a_full, 1)
            n_x = sum(k[0] in "XC" for k in BEFORE)
            for j, key in enumerate(BEFORE):
                u = N_W + j
                if j == n_x:
                    pe.wait_ge(a_free, u)
                    if rotary:
                        pe.wait_ge(w_lo, N_STAGE)
                        pe.wait_ge(wo_in, 16)
                extra(key, u, u % 2, 0)
            pe.wait_ge(zeroed, 1)

            def scores(b, h, first, last):
                g = h // HPT
                if h == 0:
                    pe.wait_ge(a_free, uses.start(b))
                elif h % HPT == 0:
                    pe.wait_ge(a_free, uses.at(("Q", g), b, first, last) + 1)
                after(pe, exp_ok, b * H + h - 1)
                for t in range(T):
                    out = SC[h % 2][:, SOFF[t]:SOFF[t] + KQ[t]]
                    mm = pe.matmul(out, QT[:, g % n_qt, t * P:(t + 1) * P], KT[:, h % n_kt, 0:KQ[t]], start=True, stop=True, skip_group_check=causal)
                    if causal:
                        mm = pe.matmul(SC[h % 2][:, SOFF[t] + t * P:SOFF[t] + (t + 1) * P], ident_b[:, :], mask_b[:, :],
                                       start=False, stop=True, skip_group_check=True)
                mm.then_inc(s_full, 1)

            def prob_transposes(b, h):
                pe.wait_ge(norm_ok, b * H + h + 1)
                after(pe, (pt_even, pt_odd)[h % 2], b * (H // 2) + h // 2)
                for k in range(T):
                    for t in range(T):
                        if k * P < KQ[t]:
                            o = TOFF[k] + t * P - QK[k]
                            mm = pe.transpose(TP[h % 2][:, o:o + P], prob[:, h % NP, SOFF[t] + k * P:SOFF[t] + (k + 1) * P], ident[:, :])
                mm.then_inc(t_full, 1)

            def times_v(b, h, first, last):
                hh = h % H
                g, j = hh // HPT, hh % HPT
                pe.wait_ge((pt_even, pt_odd)[h % 2], b * (H // 2) + h // 2 + 1)
                if h in LATE_V:
                    pe.wait_ge(a_free, uses.at(LATE_V[h], b, first, last) + 1)
                if j == 0:
                    after(pe, z_ok, b * NT + h // HPT - 1)
                for k in range(T):
                    mm = pe.matmul(Z[g % 2][j * d_head:(j + 1) * d_head, QK[k]:S], V[:, k, hh * d_head:(hh + 1) * d_head],
                                   probT[:, h % NPT, TOFF[k]:TOFF[k] + S - QK[k]], start=(k == 0), stop=(k == T - 1),
                                   tile_position=(0, j * d_head))
                mm.then_inc(pv_ok, 1)

            def body(b, first, last):
                for i in range(H):
                    for key in PLAN[i]:
                        ahead = key[0] == "+"
                        if (ahead and last) or (first and key[0] == "O"):
                            continue
                        u = uses.at(key, b, first, last)
                        if key in (("+", "P", 0, 0, 0), ("+", "Q", 0)):
                            pe.wait_ge(a_free, u)
                        extra(key[ahead:], u, uses.bank(key, b, first, last), b + 1 if ahead else b - 1 if key[0] == "O" else b)
                    scores(b, i, first, last)
                    if not (first and i < T_LAG):
                        prob_transposes(b, i - T_LAG)
                    if not (first and i < V_LAG):
                        times_v(b, i - V_LAG, first, last)

            def tail(b):
                for i in range(V_LAG):
                    if i < T_LAG:
                        prob_transposes(b, i - T_LAG)
                    times_v(b, i - V_LAG, False, False)
                for t in range(T):
                    extra(("O", t), uses.at(("O", t), b, False, False), uses.bank(("O", t), b, False, False), b - 1)

            over_rotated(pe, n_batch, body, tail)

        @block.scalar
        def _(act):
            if rotary:
                for i in range(N_STAGE):
                    w = (wqs, wks, wvs)[i // 2]
                    act.wait_ge(w_in[i % 3], 16 * KD * (i // 3 + 1))
                    act.activation(w[0][:, :, (i % 2) * 512:(i % 2 + 1) * 512],
                                   stage[i % 3][:, :, :].rearrange("p t n -> p (t n)").rearrange("p (k n) -> p k n", k=KD), ACT.Copy).then_inc(w_hi, 1)
            else:
                for u in range(N_W):
                    act.wait_ge(a_full, u + 1)
                    act.activation((wqs, wks, wvs, wos)[u // KD][0][:, u % KD, :], A[u % 2][:, :], ACT.Copy).then_inc(a_hi, 1)
            if not rotary and bq is not None:
                act.wait_ge(zeroed, 2)
            act.wait_ge(const_in, 16 * N_CONST)

            def extra(key, u, bank, n):
                if key[0] in "XC":
                    act.wait_ge(a_full, u + 1)
                    j = key[1]
                    act.activation((xT if key[0] == "X" else cT)[0][:, 2 * j:2 * j + 2, :].rearrange("p k n -> p (k n)"),
                                   A[bank][:, :], ACT.Copy).then_inc(a_hi, 1)
                elif key[0] == "Q":
                    g = key[1]
                    act.wait_ge(a_full, u + 1)
                    after(act, s_full, n * H + HPT * (g + 1 - n_qt))
                    if rotary or bq is None:
                        act.activation(QT[:, g % n_qt, :], A[bank][:, 0:S], ACT.Copy, scale=SCALE).then_inc(a_hi, 1)
                    else:
                        act.activation(QT[:, g % n_qt, :], A[bank][:, 0:S], ACT.Identity, bias=bq_c[:, g:g + 1], scale=SCALE).then_inc(a_hi, 1)

            for j, key in enumerate(BEFORE):
                extra(key, N_W + j, (N_W + j) % 2, 0)

            def exps(b, h):
                act.wait_ge(max_ok, b * H + h + 1)
                after(act, t_full, b * H + h - NP + 1)
                for t in range(T):
                    ins = act.activation(prob[:, h % NP, SOFF[t]:SOFF[t] + KQ[t]], SC[h % 2][:, SOFF[t]:SOFF[t] + KQ[t]], ACT.Exp,
                                         bias=neg_max[:, h, t:t + 1], scale=1.0, accum_out=sums[:, h, t:t + 1])
                ins.then_inc(exp_ok, 1)

            def probs_odd(b, h):
                if h % 2:
                    act.wait_ge(t_full, b * H + h + 1)
                    after(act, pv_ok, b * H + h - NPT + 1)
                    act.activation(probT[:, h % NPT, :], TP[1][:, 0:SW], ACT.Copy).then_inc(pt_odd, 1)

            def heads_hi(b, h):
                if not rotary and h % HPT == HPT - 1:
                    g = (h % H) // HPT
                    act.wait_ge(pv_ok, b * H + h + 1)
                    if bv is None:
                        act.activation(zTs[0][:, g, :], Z[g % 2][:, 0:S], ACT.Copy).then_inc(z_hi, 1)
                    else:
                        act.activation(zTs[0][:, g, :], Z[g % 2][:, 0:S], ACT.Identity, bias=bv_c[:, g:g + 1]).then_inc(z_hi, 1)

            def body(b, first, last):
                for i in range(H):
                    if not (first and i < Z_LAG):
                        heads_hi(b, i - Z_LAG)
                    for key in PLAN[i]:
                        ahead = key[0] == "+"
                        if not (ahead and last) and key[ahead] in "QXC":
                            extra(key[ahead:], uses.at(key, b, first, last), uses.bank(key, b, first, last), b + 1 if ahead else b)
                    exps(b, i)
                    if not (first and i < T_LAG):
                        probs_odd(b, i - T_LAG)

            def tail(b):
                for i in range(Z_LAG):
                    heads_hi(b, i - Z_LAG)
                    if i < T_LAG:
                        probs_odd(b, i - T_LAG)

            over_rotated(act, n_batch, body, tail)

        @block.vector
        def _(dve):
            dve.memset(KT[:, :, :], 0.0).then_inc(zeroed, 1)
            if rotary:
                for i in range(N_STAGE):
                    w = (wqs, wks, wvs)[i // 2]
                    cs = slice((i % 2) * 512, (i % 2 + 1) * 512)
                    dve.wait_ge(w_hi, i + 1)
                    dve.tensor_tensor(w[1][:, :, cs], stage[i % 3][:, :, :].rearrange("p t n -> p (t n)").rearrange("p (k n) -> p k n", k=KD),
                                      w[0][:, :, cs], ALU.subtract).then_inc(w_lo, 1)
                dve.wait_ge(const_in, 16 * N_CONST)
                n = 0
                for j in range(2):
                    for t in range(T):
                        for c in range(CH):
                            flat = rb[:, j, t, c * 512:(c + 1) * 512]
                            by_half = [v.rearrange("p (h a e) -> p h a e", a=2, e=d_head // 2) for v in (flat, turn[:, 0, :], turn[:, 1, :])]
                            turn_halves(dve, by_half[0], by_half[1], by_half[2], cos[:, t, :], sin[:, t, :], 512 // d_head, d_head)[1].then_inc(rb_ok, 2)
                            n += 2
                            dve.wait_ge(rb_ok, n)
                            dve.tensor_tensor(flat, turn[:, 0, :], turn[:, 1, :], ALU.add).then_inc(rb_ok, 1)
                            n += 1
                            dve.wait_ge(rb_ok, n)
            else:
                dve.wait_ge(const_in, 16 * N_CONST)
                if bq is not None:
                    dve.wait_ge(zeroed, 1)
                    dve.tensor_scalar(bq_c[:, :], bq_c[:, :], SCALE, None, ALU.mult).then_inc(zeroed, 1)
                for u in range(N_W):
                    dve.wait_ge(a_hi, u + 1)
                    w = (wqs, wks, wvs, wos)[u // KD]
                    dve.tensor_tensor(w[1][:, u % KD, :], A[u % 2][:, :], w[0][:, u % KD, :], ALU.subtract).then_inc(a_free, 1)

            def norm_stats(n):
                dve.wait_ge(x_ok, 16 * n + 16)
                for t in range(T):
                    dve.bn_stats(stats[:, t, :], x_t[:, t, :]).then_inc(ln, 1)
                dve.wait_ge(ln, 7 * n + 2)
                dve.memset(wait_slot[:, :], 0.0)
                for t in range(T):
                    dve.bn_aggr(mv[:, t, :], stats[:, t, :]).then_inc(ln, 1)
                dve.wait_ge(ln, 7 * n + 4)
                dve.tensor_scalar(rstd[:, :], mv[:, :, 1], EPS, None, ALU.add).then_inc(ln, 1)

            def apply_norm(n):
                dve.wait_ge(ln_pow, n + 1)
                for t in range(T):
                    dve.tensor_scalar(x_t[:, t, :], x_t[:, t, :], mv[:, t, 0:1], rstd[:, t:t + 1], ALU.subtract, ALU.mult).then_inc(ln, 1)

            def extra(key, u, bank, n, hi, seq):
                kind = key[0]
                if kind in "XC":
                    dst, j = xT if kind == "X" else cT, key[1]
                    dve.wait_ge(a_hi, hi + 1)
                    dve.tensor_tensor(dst[1][:, 2 * j:2 * j + 2, :].rearrange("p k n -> p (k n)"), A[bank][:, :],
                                      dst[0][:, 2 * j:2 * j + 2, :].rearrange("p k n -> p (k n)"), ALU.subtract).then_inc(a_free, 1)
                elif kind == "P":
                    _, which, c, t = key
                    dve.wait_ge(a_full, u + 1)
                    after(dve, rot, 2 * (seq - 1))
                    by_half = [v.rearrange("p (h a e) -> p h a e", a=2, e=d_head // 2)
                               for v in (A[bank][:, :], (q_t, k_t)[which][:, t, c * 512:(c + 1) * 512], turn[:, t % 2, :])]
                    turn_halves(dve, by_half[0], by_half[1], by_half[2], cos[:, t, :], sin[:, t, :], 512 // d_head, d_head)[1].then_inc(a_free, 1)
                elif kind == "V":
                    dve.wait_ge(a_full, u + 1)
                    dve.tensor_copy(V[:, key[2], key[1] * 512:(key[1] + 1) * 512], A[bank][:, :]).then_inc(a_free, 1)
                elif kind == "Q":
                    g = key[1]
                    dve.wait_ge(a_hi, hi + 1)
                    for j in range(HPT):
                        rows = slice(j * d_head, (j + 1) * d_head)
                        if rotary or bk is None:
                            ins = dve.tensor_copy(KT[rows, (g * HPT + j) % n_kt, :], A[bank][rows, S:2 * S])
                        else:
                            ins = dve.tensor_scalar(KT[rows, (g * HPT + j) % n_kt, :], A[bank][rows, S:2 * S], bk_c[rows, g:g + 1], None, ALU.add)
                    ins.then_inc(a_free, 1)
                elif kind == "O":
                    t = key[1]
                    dve.wait_ge(res_in, n * 16 + 16)
                    if bo is not None:
                        dve.wait_ge(res_b, (n + 1) * T)
                    dve.wait_ge(a_full, u + 1)
                    dve.tensor_tensor(res[:, t, :], A[bank][:, :], res[:, t, :], ALU.add).then_inc(a_free, 1)

            norm_stats(0)
            apply_norm(0)
            for j, key in enumerate(BEFORE):
                hi = N_W + before_act.index(key) if key in before_act else None
                seq = [k for k in BEFORE if k[0] == "P"].index(key) if key[0] == "P" else None
                extra(key, N_W + j, (N_W + j) % 2, 0, hi, seq)

            def maxima(b, h):
                dve.wait_ge(s_full, b * H + h + 1)
                if causal:
                    for t in range(T):
                        ins = dve.tensor_reduce(neg_max[:, h, t:t + 1], SC[h % 2][:, SOFF[t]:SOFF[t] + KQ[t]], AX.X, ALU.max, negate=True)
                else:
                    ins = dve.tensor_reduce(neg_max[:, h, :], SC[h % 2][:, :].rearrange("p (t k) -> p t k", t=T), AX.X, ALU.max, negate=True)
                ins.then_inc(max_ok, 1)

            def sums_inverse(b, h):
                dve.wait_ge(exp_ok, b * H + h + 1)
                dve.reciprocal(rsum[:, h % H, :], sums[:, h % H, :]).then_inc(rsum_ok, 1)

            def probs_even(b, h):
                if h % 2 == 0:
                    dve.wait_ge(t_full, b * H + h + 1)
                    after(dve, pv_ok, b * H + h - NPT + 1)
                    dve.tensor_copy(probT[:, h % NPT, :], TP[0][:, 0:SW]).then_inc(pt_even, 1)

            def heads_done(b, h):
                if h % HPT == HPT - 1:
                    g = (h % H) // HPT
                    if rotary:
                        dve.wait_ge(pv_ok, b * H + h + 1)
                        dve.tensor_scalar(zT[:, g, :], Z[g % 2][:, 0:S], bv_c[:, g:g + 1], None, ALU.add).then_inc(z_ok, 1)
                    else:
                        dve.wait_ge(z_hi, b * NT + h // HPT + 1)
                        if bv is None:
                            dve.tensor_tensor(zTs[1][:, g, :], Z[g % 2][:, 0:S], zTs[0][:, g, :], ALU.subtract).then_inc(z_ok, 1)
                        else:
                            dve.scalar_tensor_tensor(zTs[1][:, g, :], Z[g % 2][:, 0:S], bv_c[:, g:g + 1], zTs[0][:, g, :],
                                                     ALU.add, ALU.subtract).then_inc(z_ok, 1)

            def body(b, first, last):
                seq = 0
                for i in range(H):
                    if not (first and i < Z_LAG):
                        heads_done(b, i - Z_LAG)
                    for key in PLAN[i]:
                        ahead = key[0] == "+"
                        if (ahead and last) or (first and key[0] == "O"):
                            continue
                        kind = key[ahead]
                        extra(key[ahead:], uses.at(key, b, first, last), uses.bank(key, b, first, last),
                              b - 1 if kind == "O" else b, hi_at(key, b, last) if kind in "QXC" else None, P_BEFORE + b * P_PER + seq)
                        seq += kind == "P"
                    maxima(b, i)
                    if not (first and i < 1):
                        sums_inverse(b, i - 1)
                    if i == STATS_AT and not last:
                        norm_stats(b + 1)
                    if i == APPLY_AT and not last:
                        apply_norm(b + 1)
                    if not (first and i < T_LAG):
                        probs_even(b, i - T_LAG)

            def tail(b):
                for i in range(Z_LAG):
                    heads_done(b, i - Z_LAG)
                    if i < 1:
                        sums_inverse(b, i - 1)
                    if i < T_LAG:
                        probs_even(b, i - T_LAG)
                for t in range(T):
                    extra(("O", t), uses.at(("O", t), b, False, False), uses.bank(("O", t), b, False, False), b - 1, None, None)

            over_rotated(dve, n_batch, body, tail)


def turn_halves(dve, src, to_cos, to_sin, cos, sin, heads, d_head):
    half = d_head // 2
    c = cos.rearrange("p (o a e) -> p o a e", o=1, a=2).to_broadcast([P, heads, 2, half])
    s = sin.rearrange("p (o a e) -> p o a e", o=1, a=2).to_broadcast([P, heads, 2, half])
    return (dve.tensor_tensor(to_cos, src, c, ALU.mult),
            dve.tensor_tensor(to_sin, src[:, :, ::-1, :], s, ALU.mult))


def expert_phase(nc, n_batch, x_in, x_norm, consts, gate_w, gate_b, w1, w2, logits_d, sel_d, selT_d, out_d):
    E = gate_w.shape[0]
    HID = w1.shape[2]
    Q = HID // 512
    G = P // E
    NG = n_batch // G
    K8 = 8
    with Phase(nc, "moe") as ph:
        ident = ph.sb("ident", [P, P])
        merged = ph.sb("merged", [P, E, KD, n_batch])
        const_in = ph.sem("const_in")

        with Phase(nc, "route") as r:
            xT_bank = [r.bank(f"X{i}") for i in range(2)]
            L = r.bank("L")
            gate = r.sb("gate", [E, D])
            gateT = r.sb("gateT", [P, KD, E])
            gb = r.sb("gb", [E, 1])
            x_t = r.sb("x_t", [P, 2, T, D])
            xT = r.sb("xT", [P, KD, S])
            lg = r.sb("lg", [E, 2, S])
            stats = r.sb("stats", [P, T, 6])
            mv = r.sb("mv", [P, T, 2])
            rstd = r.sb("rstd", [P, T])
            minus_half = r.sb("minus_half", [P, T])
            wait_slot = r.sb("wait_slot", [P, 1])
            x_ok = [r.sem(f"x_ok{i}") for i in range(2)]
            ln = r.sem("ln")
            ln_pow = r.sem("ln_pow")
            pool_const = r.sem("pool_const")
            stored = [r.sem(f"stored{i}") for i in range(2)]
            g_full = r.sem("g_full")
            g_ok = r.sem("g_ok")
            t_full = r.sem("t_full")
            t_ok = r.sem("t_ok")
            l_full = r.sem("l_full")
            l_ok = r.sem("l_ok")
            block = r.ctx.enter_context(nc.Block())

            @block.sync
            def _(sp):
                sp.dma_start(ident[:, :], consts["ident"]).then_inc(const_in, 16)
                sp.dma_start(gate[:, :], gate_w).then_inc(const_in, 16)
                sp.dma_start(gb[:, :], gate_b.rearrange("(e o) -> e o", o=1)).then_inc(const_in, 16)
                for s in range(2):
                    sp.sem_inc(stored[s], 16)
                with sp.Fori(0, n_batch // 2) as i:
                    for s in range(2):
                        b = 2 * i + s
                        sp.wait_ge(stored[s], 16 + 32 * i)
                        sp.dma_start(x_t[:, s, :, :], x_in[b].rearrange("(t p) d -> p t d", p=P)).then_inc(x_ok[s], 16)
                for s in range(2):
                    sp.wait_ge(stored[s], 16 + 16 * n_batch)

            @block.gpsimd
            def _(pool):
                pool.memset(minus_half[:, :], -0.5).then_inc(pool_const, 1)
                pool.wait_ge(pool_const, 1)
                with pool.Fori(0, n_batch) as b:
                    pool.wait_ge(ln, 7 * b + 5)
                    pool.tensor_tensor(rstd[:, :], rstd[:, :], minus_half[:, :], ALU.pow).then_inc(ln_pow, 1)

            @block.vector
            def _(dve):
                dve.sem_inc(l_ok, 1)
                dve.wait_ge(g_full, 1)
                dve.tensor_copy(gateT[:, :, :].rearrange("p k e -> p (k e)"), L[:, 0:KD * E]).then_inc(g_ok, 1)
                with dve.Fori(0, n_batch // 2) as i:
                    for s in range(2):
                        n = 2 * i + s
                        dve.wait_ge(x_ok[s], 16 * i + 16)
                        for t in range(T):
                            dve.bn_stats(stats[:, t, :], x_t[:, s, t, :]).then_inc(ln, 1)
                        dve.wait_ge(ln, 7 * n + 2)
                        dve.memset(wait_slot[:, :], 0.0)
                        for t in range(T):
                            dve.bn_aggr(mv[:, t, :], stats[:, t, :]).then_inc(ln, 1)
                        dve.wait_ge(ln, 7 * n + 4)
                        dve.tensor_scalar(rstd[:, :], mv[:, :, 1], EPS, None, ALU.add).then_inc(ln, 1)
                        dve.wait_ge(ln_pow, n + 1)
                        for t in range(T):
                            dve.tensor_scalar(x_t[:, s, t, :], x_t[:, s, t, :], mv[:, t, 0:1], rstd[:, t:t + 1], ALU.subtract, ALU.mult).then_inc(ln, 1)
                        dve.wait_ge(l_full, n + 1)
                        dve.wait_ge(stored[s], 16 + 32 * i)
                        dve.tensor_scalar(lg[:, s, :], L[0:E, 0:S], gb[:, 0:1], None, ALU.add).then_inc(l_ok, 1)

            @block.tensor
            def _(pe):
                pe.wait_ge(const_in, 48)
                pe.sem_inc(t_full, 1)
                for k in range(KD):
                    mm = pe.transpose(L[:, k * E:(k + 1) * E], gate[:, k * P:(k + 1) * P], ident[0:E, 0:E])
                mm.then_inc(g_full, 1)
                pe.wait_ge(g_ok, 1)
                with pe.Fori(0, n_batch // 2) as i:
                    for s in range(2):
                        n = 2 * i + s
                        pe.wait_ge(ln, 7 * n + 7)
                        pe.wait_ge(t_ok, 1 + 2 * n)
                        for j in range(2):
                            for kk in range(2):
                                for t in range(T):
                                    k = 2 * j + kk
                                    mm = pe.transpose(xT_bank[j][:, (kk * T + t) * P:(kk * T + t + 1) * P], x_t[:, s, t, k * P:(k + 1) * P], ident[:, :])
                            mm.then_inc(t_full, 1)
                        pe.wait_ge(t_ok, 1 + 2 * n + 2)
                        pe.wait_ge(l_ok, 1 + n)
                        for k in range(KD):
                            mm = pe.matmul(L[0:E, 0:S], gateT[:, k, :], xT[:, k, :], start=(k == 0), stop=(k == KD - 1))
                        mm.then_inc(l_full, 1)

            @block.scalar
            def _(act):
                act.sem_inc(t_ok, 1)
                with act.Fori(0, n_batch // 2) as i:
                    for s in range(2):
                        n = 2 * i + s
                        act.wait_ge(ln, 7 * n + 7)
                        act.dma_start(x_norm[n].rearrange("(t p) d -> p t d", p=P), x_t[:, s, :, :]).then_inc(stored[s], 16)
                        for j in range(2):
                            act.wait_ge(t_full, 1 + 2 * n + j + 1)
                            act.activation(xT[:, 2 * j:2 * j + 2, :].rearrange("p k n -> p (k n)"), xT_bank[j][:, :], ACT.Copy).then_inc(t_ok, 1)
                        act.wait_ge(l_ok, 1 + n + 1)
                        act.dma_start(logits_d[n], lg[:, s, :]).then_inc(stored[s], 16)

        with Phase(nc, "top") as r:
            TB = [r.bank(f"T{i}") for i in range(2)]
            pr = r.sb("pr", [P, NG, S])
            rest = r.sb("rest", [P, NG, S])
            nm = r.sb("nm", [P, NG])
            sm = r.sb("sm", [P, NG])
            top = r.sb("top", [P, NG, K8])
            selT = r.sb("selT", [P, T, NG, P])
            landed, mx, ex, step, full, got, done = (r.sem(n) for n in ("landed", "mx", "ex", "step", "full", "got", "done"))
            block = r.ctx.enter_context(nc.Block())
            NDONE = 1 + NG * G * T

            @block.sync
            def _(sp):
                sp.dma_start(pr[:, :, :], logits_d.rearrange("(g b) e s -> (b e) g s", b=G)).then_inc(landed, 16)
                sp.wait_ge(step, 5 * NG)
                sp.dma_start(sel_d.rearrange("(g b) e s -> (b e) g s", b=G), pr[:, :, :]).then_inc(done, 16)
                for g in range(NG):
                    sp.wait_ge(got, g + 1)
                    for b in range(G):
                        for t in range(T):
                            sp.dma_start(selT_d[g * G + b, t], selT[:, t, g, b * E:(b + 1) * E]).then_inc(done, 16)
                sp.wait_ge(done, 16 * NDONE)

            @block.vector
            def _(dve):
                dve.wait_ge(landed, 16)
                for g in range(NG):
                    dve.tensor_reduce(nm[:, g:g + 1], pr[:, g, :], AX.X, ALU.max, negate=True).then_inc(mx, 1)
                for g in range(NG):
                    dve.wait_ge(ex, g + 1)
                    dve.reciprocal(sm[:, g:g + 1], sm[:, g:g + 1]).then_inc(step, 1)
                    dve.wait_ge(step, 5 * g + 1)
                    dve.tensor_scalar(pr[:, g, :], pr[:, g, :], sm[:, g:g + 1], None, ALU.mult).then_inc(step, 1)
                    dve.wait_ge(step, 5 * g + 2)
                    dve.max(top[:, g, :], pr[:, g, :]).then_inc(step, 1)
                    dve.wait_ge(step, 5 * g + 3)
                    dve.match_replace(rest[:, g, :], top[:, g, :], pr[:, g, :], 0.0).then_inc(step, 1)
                    dve.wait_ge(step, 5 * g + 4)
                    dve.tensor_tensor(pr[:, g, :], pr[:, g, :], rest[:, g, :], ALU.subtract).then_inc(step, 1)
                for g in range(NG):
                    dve.wait_ge(full, g + 1)
                    dve.tensor_copy(selT[:, :, g, :], TB[g % 2][:, 0:T * P].rearrange("p (t e) -> p t e", t=T)).then_inc(got, 1)

            @block.scalar
            def _(act):
                for g in range(NG):
                    act.wait_ge(mx, g + 1)
                    act.activation(pr[:, g, :], pr[:, g, :], ACT.Exp, bias=nm[:, g:g + 1], accum_out=sm[:, g:g + 1]).then_inc(ex, 1)

            @block.tensor
            def _(pe):
                for g in range(NG):
                    pe.wait_ge(step, 5 * g + 5)
                    if g >= 2:
                        pe.wait_ge(got, g - 1)
                    for t in range(T):
                        mm = pe.transpose(TB[g % 2][:, t * P:(t + 1) * P], pr[:, g, t * P:(t + 1) * P], ident[:, :])
                    mm.then_inc(full, 1)

        with Phase(nc, "merge") as r:
            M = [r.bank(f"M{i}") for i in range(2)]
            xn = r.sb("xn", [P, 2, T, D])
            sel = r.sb("sel", [P, 2, T, E])
            landed = [r.sem(f"landed{i}") for i in range(2)]
            full, got = r.sem("full"), r.sem("got")
            block = r.ctx.enter_context(nc.Block())

            @block.sync
            def _(sp):
                with sp.Fori(0, n_batch // 2) as i:
                    for s in range(2):
                        b = 2 * i + s
                        sp.wait_ge(full, 2 * i + s + 1)
                        sp.dma_start(xn[:, s, :, :], x_norm[b].rearrange("(t p) d -> p t d", p=P)).then_inc(landed[s], 16)
                        sp.dma_start(sel[:, s, :, :], selT_d[b].rearrange("t p e -> p t e")).then_inc(landed[s], 16)

            @block.tensor
            def _(pe):
                pe.sem_inc(full, 2)
                with pe.Fori(0, n_batch // 2) as i:
                    for s in range(2):
                        pe.wait_ge(landed[s], 32 * i + 32)
                        pe.wait_ge(got, 2 * i + s + 1)
                        for k in range(KD):
                            for t in range(T):
                                mm = pe.matmul(M[s][:, k * E:(k + 1) * E], xn[:, s, t, k::KD], sel[:, s, t, :], start=(t == 0), stop=(t == T - 1))
                        mm.then_inc(full, 1)

            @block.vector
            def _(dve):
                dve.sem_inc(got, 2)
                with dve.Fori(0, n_batch // 2) as i:
                    for s in range(2):
                        dve.wait_ge(full, 2 + 2 * i + s + 1)
                        dve.tensor_copy(merged[:, :, :, bass.ds(2 * i + s, 1)].rearrange("p e k o -> p k e o"),
                                        M[s][:, 0:KD * E].rearrange("p (k e o) -> p k e o", k=KD, o=1)).then_inc(got, 1)

        with Phase(nc, "experts") as r:
            HP = [r.bank(f"H{i}") for i in range(2)]
            TP = [r.bank(f"T{i}") for i in range(2)]
            OP = [r.bank(f"O{i}") for i in range(2)]
            w1_s = [r.sb(f"w1_{i}", [P, KD, HID]) for i in range(2)]
            w2_s = [r.sb(f"w2_{i}", [P, Q, HID // (P * Q), D]) for i in range(2)]
            NQ = HID // (P * Q)
            b1_s = [r.sb(f"b1_{i}", [1, HID]) for i in range(2)]
            tok = r.sb("tok", [P, 2, KD, 32])
            ones = r.sb("ones", [1, 32])
            hid = r.sb("hid", [P, 2, 512])
            hidT = r.sb("hidT", [P, 2, NQ, P])
            o_sb = r.sb("o_sb", [P, 2, D])
            w1_in = [r.sem(f"w1_in{i}") for i in range(2)]
            w2_in = [r.sem(f"w2_in{i}") for i in range(2)]
            stored = [r.sem(f"stored{i}") for i in range(2)]
            zeroed, tok_ok, h_full, act_ok, ht_full, ht_ok, o_full, o_ok = (
                r.sem(n) for n in ("zeroed", "tok_ok", "h_full", "act_ok", "ht_full", "ht_ok", "o_full", "o_ok"))
            block = r.ctx.enter_context(nc.Block())

            @block.sync
            def _(sp):
                with sp.Fori(0, E // 2) as i:
                    for s in range(2):
                        e = 2 * i + s
                        sp.wait_ge(h_full, e + 1)
                        sp.dma_start(w1_s[s][:, :, :], w1[e, 0:D].rearrange("(p k) j -> p k j", k=KD)).then_inc(w1_in[s], 16)
                        sp.dma_start(b1_s[s][:, :], w1[e, D:D + 1]).then_inc(w1_in[s], 16)
                        sp.wait_ge(o_full, e + 1)
                        sp.dma_start(w2_s[s][:, :, :, :], w2[e, 0:HID].rearrange("(n p q) m -> p n q m", n=Q, q=NQ)).then_inc(w2_in[s], 16)

            @block.gpsimd
            def _(pool):
                pool.memset(tok[:, :, :, :], 0.0).then_inc(zeroed, 1)
                pool.memset(ones[:, :], 1.0).then_inc(zeroed, 1)

            @block.tensor
            def _(pe):
                pe.sem_inc(h_full, 2)
                pe.sem_inc(o_full, 2)
                pe.sem_inc(ht_full, 2)
                pe.wait_ge(zeroed, 2)

                def hidden(e, i, s):
                    pe.wait_ge(w1_in[s], 32 * i + 32)
                    pe.wait_ge(tok_ok, e + 1)
                    pe.wait_ge(act_ok, e + 1)
                    for k in range(KD):
                        for n in range(Q):
                            pe.matmul(HP[s][32 * n:32 * n + 32, :], tok[:, s, k, :], w1_s[s][:, k, n * 512:(n + 1) * 512],
                                      start=(k == 0), stop=False, tile_position=(0, 32 * n))
                    for n in range(Q):
                        mm = pe.matmul(HP[s][32 * n:32 * n + 32, :], ones[:, :], b1_s[s][:, n * 512:(n + 1) * 512],
                                       start=False, stop=True, tile_position=(0, 32 * n))
                    mm.then_inc(h_full, 1)

                def output(e, i, s):
                    pe.wait_ge(act_ok, e + 3)
                    pe.wait_ge(ht_ok, e + 1)
                    for q in range(NQ):
                        mm = pe.transpose(TP[s][:, q * P:(q + 1) * P], hid[:, s, q::NQ], ident[:, :])
                    mm.then_inc(ht_full, 1)
                    pe.wait_ge(w2_in[s], 16 * i + 16)
                    pe.wait_ge(ht_ok, e + 3)
                    pe.wait_ge(o_ok, e + 1)
                    for q in range(NQ):
                        for n in range(Q):
                            mm = pe.matmul(OP[s][32 * n:32 * n + 32, :], hidT[:, s, q, 32 * n:32 * n + 32], w2_s[s][:, n, q, :],
                                           start=(q == 0), stop=(q == NQ - 1), tile_position=(0, 32 * n))
                    mm.then_inc(o_full, 1)

                with pe.Fori(0, E // 2) as i:
                    for s in range(2):
                        hidden(2 * i + s, i, s)
                        output(2 * i + s, i, s)

            @block.scalar
            def _(act):
                act.sem_inc(act_ok, 2)
                for s in range(2):
                    act.sem_inc(stored[s], 16)
                with act.Fori(0, E // 2) as i:
                    for s in range(2):
                        e = 2 * i + s
                        act.wait_ge(h_full, 2 + e + 1)
                        act.wait_ge(ht_full, e + 1)
                        act.activation(hid[:, s, :], HP[s][:, :], ACT.Gelu).then_inc(act_ok, 1)
                        act.wait_ge(o_ok, 2 + e + 1)
                        for n in range(Q):
                            act.dma_start(out_d[:, n, bass.ds(e, 1), :].rearrange("b o d -> b (o d)"),
                                          o_sb[32 * n:32 * n + n_batch, s, :]).then_inc(stored[s], 16)
                for s in range(2):
                    act.wait_ge(stored[s], 16 + 16 * Q * E // 2)

            @block.vector
            def _(dve):
                for count in (ht_ok, o_ok):
                    dve.sem_inc(count, 2)
                dve.wait_ge(zeroed, 2)

                def tokens(e, s):
                    dve.tensor_copy(tok[:, s, :, 0:n_batch], merged[:, bass.ds(e, 1), :, :].rearrange("p o k b -> p (o k) b")).then_inc(tok_ok, 1)

                with dve.Fori(0, E // 2) as i:
                    for s in range(2):
                        e = 2 * i + s
                        dve.wait_ge(h_full, e + 1)
                        tokens(e, s)
                        dve.wait_ge(ht_full, 2 + e + 1)
                        dve.tensor_copy(hidT[:, s, :, :].rearrange("p q n -> p (q n)"), TP[s][:, :]).then_inc(ht_ok, 1)
                        dve.wait_ge(o_full, 2 + e + 1)
                        dve.wait_ge(stored[s], 16 + 16 * Q * i)
                        dve.tensor_copy(o_sb[:, s, :], OP[s][:, :]).then_inc(o_ok, 1)


def over_pairs(eng, n, body):
    if n > 2:
        with eng.Fori(0, n // 2 - 1) as i:
            for s in range(2):
                body(2 * i + s, i, s, False)
    for s in range(2):
        body(n - 2 + s, n // 2 - 1, s, s == 1)


def norm_attention_phase(nc, n_batch, x_in, x_out, consts, sel_d, out_d, w2, wq, bq, wk, bk, wv, bv):
    E, Q = out_d.shape[2], out_d.shape[1]
    HID = w2.shape[1] - 1
    NU = 3 * T
    ORDER = [("k", 0), ("v", 0), ("k", 1), ("v", 1), ("q", 0), ("q", 1)]
    NL = 9
    with Phase(nc, "norm") as ph:
        A = [ph.bank(f"A{i}") for i in range(2)]
        B = [ph.bank(f"B{i}") for i in range(2)]
        C = [ph.bank(f"C{i}") for i in range(3)]
        KV = ph.bank("KV")
        ident = ph.sb("ident", [P, P])
        w_stage = ph.sb("w_stage", [P, 3, KD, D])
        w = {n: [ph.sb(f"w{n}{i}", [P, KD, D], F32R) for i in "hl"] for n in "qkv"}
        bias = {n: ph.sb(f"b{n}", [P, D]) for n in "qkv"}
        b2 = ph.sb("b2", [E, D])
        x_ld = ph.sb("x_ld", [P, T, D])
        x3 = ph.sb("x3", [P, 2, T, D])
        xn = ph.sb("xn", [P, T, D])
        sel4 = ph.sb("sel4", [P, S])
        ob = ph.sb("ob", [P, D])
        stats = ph.sb("stats", [P, T, 6])
        mv = ph.sb("mv", [P, T, 2])
        rstd = ph.sb("rstd", [P, T])
        minus_half = ph.sb("minus_half", [P, T])
        wait_slot = ph.sb("wait_slot", [P, 1])
        xT = [ph.sb(f"xT{i}", [P, KD, S], F32R) for i in "hl"]
        t_sb = {n: ph.sb(f"{n}_sb", [P, T, D]) for n in "qkv"}
        prod = ph.sb("prod", [P, T, D])
        squares = ph.sb("squares", [P, D])
        ssq = ph.sb("ssq", [P, 2 * T])
        rn = ph.sb("rn", [P, 2 * T])
        names = ("const_in w_in w_full w_hi w_lo f_in ob_ok sc_full ln ln_pow xT_full hi_ok lo_ok p_full c_ok "
                 "sq_ok prod_ok rn_ok kv_full fin pool_const")
        (const_in, w_in, w_full, w_hi, w_lo, f_in, ob_ok, sc_full, ln, ln_pow, xT_full, hi_ok, lo_ok, p_full, c_ok,
         sq_ok, prod_ok, rn_ok, kv_full, fin, pool_const) = (ph.sem(n) for n in names.split())
        stored = [ph.sem(f"stored{i}") for i in range(2)]
        NW = 3 * KD
        block = ph.ctx.enter_context(nc.Block())

        @block.sync
        def _(sp):
            sp.dma_start(ident[:, :], consts["ident"]).then_inc(const_in, 16)
            for i, src in enumerate((wq, wk, wv)):
                sp.dma_start(w_stage[:, i, :, :], src.rearrange("(j p) d -> p j d", p=P)).then_inc(w_in, 16)
            for n, src in zip("qkv", (bq, bk, bv)):
                sp.dma_start(bias[n][:, :], src.partition_broadcast(P)).then_inc(const_in, 16)
            sp.dma_start(b2[:, :], w2[:, HID, :]).then_inc(const_in, 16)

            def load(n):
                sp.dma_start(x_ld[:, :, :], x_in[n].rearrange("(t p) d -> p t d", p=P)).then_inc(f_in, 16)
                sp.dma_start(ob[:, :], out_d[n].rearrange("n e d -> (n e) d")).then_inc(f_in, 16)
                for j in range(Q):
                    sp.dma_start(sel4[j * E:(j + 1) * E, :], sel_d[n]).then_inc(f_in, 16)

            load(0)

            def body(n, i, s, last):
                if not last:
                    sp.wait_ge(ln, NL * n + 2)
                    load(n + 1)
                sp.wait_ge(fin, 4 * n + 4)
                sp.dma_start(x_out[n].rearrange("(t p) d -> p t d", p=P), x3[:, s, :, :]).then_inc(stored[s], 16)
            over_pairs(sp, n_batch, body)
            for s in range(2):
                sp.wait_ge(stored[s], 16 + 8 * n_batch)

        @block.gpsimd
        def _(pool):
            pool.memset(minus_half[:, :], -0.5).then_inc(pool_const, 1)
            pool.wait_ge(pool_const, 1)

            def rstds(n):
                pool.wait_ge(ln, NL * n + 7)
                pool.tensor_tensor(rstd[:, :], rstd[:, :], minus_half[:, :], ALU.pow).then_inc(ln_pow, 1)

            rstds(0)

            def body(n, i, s, last):
                for t in range(T):
                    pool.wait_ge(c_ok, 3 + NU * n + 2 * t + 2)
                    pool.tensor_tensor(prod[:, t, :], t_sb["k"][:, t, :], t_sb["v"][:, t, :], ALU.mult).then_inc(prod_ok, 1)
                for j in range(2):
                    pool.wait_ge(sq_ok, 1 + 4 * n + 2 * j + 2)
                    pool.tensor_tensor(rn[:, 2 * j:2 * j + 2], ssq[:, 2 * j:2 * j + 2], minus_half[:, :], ALU.pow).then_inc(rn_ok, 1)
                if not last:
                    rstds(n + 1)
            over_pairs(pool, n_batch, body)

        @block.tensor
        def _(pe):
            pe.wait_ge(const_in, 16 * 5)
            pe.wait_ge(w_in, 48)
            for i in range(3):
                for k in range(KD):
                    u = i * KD + k
                    if u >= 2:
                        pe.wait_ge(w_lo, u - 1)
                    for j in range(4):
                        mm = pe.transpose(B[u % 2][:, j * P:(j + 1) * P], w_stage[:, i, j, k * P:(k + 1) * P], ident[:, :])
                    mm.then_inc(w_full, 1)
            pe.wait_ge(w_lo, NW)

            def spread(n):
                pe.wait_ge(ob_ok, n + 1)
                for t in range(T):
                    mm = pe.matmul(A[t][:, :], sel4[:, t * P:(t + 1) * P], ob[:, :], start=True, stop=True)
                mm.then_inc(sc_full, 1)

            def transposes(n):
                pe.wait_ge(ln, NL * n + NL)
                for j in range(2):
                    for kk in range(2):
                        for t in range(T):
                            k = 2 * j + kk
                            mm = pe.transpose(B[j][:, (kk * T + t) * P:(kk * T + t + 1) * P], xn[:, t, k * P:(k + 1) * P], ident[:, :])
                    mm.then_inc(xT_full, 1)

            spread(0)
            transposes(0)

            def body(n, i, s, last):
                pe.wait_ge(lo_ok, 2 * n + 2)
                for u, (which, t) in enumerate(ORDER):
                    pe.wait_ge(c_ok, NU * n + u + 1)
                    split_products(pe, C[u % 3][:, :], [
                        ((xT[0][:, k, t * P:(t + 1) * P], xT[1][:, k, t * P:(t + 1) * P]),
                         (w[which][0][:, k, :], w[which][1][:, k, :])) for k in range(KD)]).then_inc(p_full, 1)
                if not last:
                    spread(n + 1)
                pe.wait_ge(prod_ok, 2 * n + 2)
                pe.wait_ge(rn_ok, 2 * n + 1)
                for t in range(T):
                    mm = pe.matmul(KV[:, :], rn[:, t:t + 1].to_broadcast([P, P]), prod[:, t, :], start=(t == 0), stop=(t == T - 1))
                mm.then_inc(kv_full, 1)
                if not last:
                    transposes(n + 1)
            over_pairs(pe, n_batch, body)

        @block.scalar
        def _(act):
            act.sem_inc(sq_ok, 1)
            for u in range(NW):
                act.wait_ge(w_full, u + 1)
                act.activation(w["qkv"[u // KD]][0][:, u % KD, :], B[u % 2][:, :], ACT.Copy).then_inc(w_hi, 1)

            def take_hi(n):
                for j in range(2):
                    act.wait_ge(xT_full, 2 * n + j + 1)
                    act.activation(xT[0][:, 2 * j:2 * j + 2, :].rearrange("p k n -> p (k n)"), B[j][:, :], ACT.Copy).then_inc(hi_ok, 1)

            take_hi(0)

            def body(n, i, s, last):
                for j, (which, t, u) in enumerate((("k", 0, 0), ("k", 1, 2), ("q", 0, 4), ("q", 1, 5))):
                    act.wait_ge(c_ok, 3 + NU * n + u + 1)
                    act.wait_ge(sq_ok, 1 + 4 * n + j)
                    act.activation(squares[:, :], t_sb[which][:, t, :], ACT.Square, accum_out=ssq[:, j:j + 1]).then_inc(sq_ok, 1)
                if not last:
                    take_hi(n + 1)
            over_pairs(act, n_batch, body)

        @block.vector
        def _(dve):
            dve.sem_inc(c_ok, 3)
            for s in range(2):
                dve.sem_inc(stored[s], 16)
            for u in range(NW):
                parts = w["qkv"[u // KD]]
                dve.wait_ge(w_hi, u + 1)
                dve.tensor_tensor(parts[1][:, u % KD, :], B[u % 2][:, :], parts[0][:, u % KD, :], ALU.subtract).then_inc(w_lo, 1)
            dve.wait_ge(const_in, 16 * 5)

            def residual_and_stats(n, i, s):
                dve.wait_ge(f_in, 16 * (2 + Q) * (n + 1))
                dve.tensor_tensor(ob[0:E, :], ob[0:E, :], b2[:, :], ALU.add).then_inc(ob_ok, 1)
                dve.wait_ge(sc_full, n + 1)
                dve.wait_ge(stored[s], 16 + 16 * i)
                for t in range(T):
                    dve.tensor_tensor(x3[:, s, t, :], A[t][:, :], x_ld[:, t, :], ALU.add).then_inc(ln, 1)
                dve.wait_ge(ln, NL * n + 2)
                for t in range(T):
                    dve.bn_stats(stats[:, t, :], x3[:, s, t, :]).then_inc(ln, 1)
                dve.wait_ge(ln, NL * n + 4)
                dve.memset(wait_slot[:, :], 0.0)
                for t in range(T):
                    dve.bn_aggr(mv[:, t, :], stats[:, t, :]).then_inc(ln, 1)
                dve.wait_ge(ln, NL * n + 6)
                dve.tensor_scalar(rstd[:, :], mv[:, :, 1], EPS, None, ALU.add).then_inc(ln, 1)

            def apply_norm(n, s):
                dve.wait_ge(ln_pow, n + 1)
                for t in range(T):
                    dve.tensor_scalar(xn[:, t, :], x3[:, s, t, :], mv[:, t, 0:1], rstd[:, t:t + 1], ALU.subtract, ALU.mult).then_inc(ln, 1)

            def take_lo(n):
                for j in range(2):
                    dve.wait_ge(hi_ok, 2 * n + j + 1)
                    dve.tensor_tensor(xT[1][:, 2 * j:2 * j + 2, :].rearrange("p k n -> p (k n)"), B[j][:, :],
                                      xT[0][:, 2 * j:2 * j + 2, :].rearrange("p k n -> p (k n)"), ALU.subtract).then_inc(lo_ok, 1)

            residual_and_stats(0, 0, 0)
            apply_norm(0, 0)
            take_lo(0)

            def body(n, i, s, last):
                for u, (which, t) in enumerate(ORDER):
                    dve.wait_ge(p_full, NU * n + u + 1)
                    dve.tensor_tensor(t_sb[which][:, t, :], C[u % 3][:, :], bias[which][:, :], ALU.add).then_inc(c_ok, 1)
                if not last:
                    residual_and_stats(n + 1, i + s, 1 - s)
                dve.wait_ge(kv_full, n + 1)
                dve.wait_ge(rn_ok, 2 * n + 2)
                for t in range(T):
                    dve.tensor_tensor(t_sb["q"][:, t, :], KV[:, :], t_sb["q"][:, t, :], ALU.mult).then_inc(fin, 1)
                dve.wait_ge(fin, 4 * n + 2)
                for t in range(T):
                    dve.scalar_tensor_tensor(x3[:, s, t, :], t_sb["q"][:, t, :], rn[:, T + t:T + t + 1], x3[:, s, t, :], ALU.mult, ALU.add).then_inc(fin, 1)
                if not last:
                    apply_norm(n + 1, 1 - s)
                    take_lo(n + 1)
            over_pairs(dve, n_batch, body)


def fp8_linear_phase(nc, n_batch, x_in, x_out, consts, weight, bias):
    NL = 9
    with Phase(nc, "fp8") as ph:
        B = [ph.bank(f"B{i}", BF16) for i in range(2)]
        O = [ph.bank(f"O{i}") for i in range(4)]
        ident_b = ph.sb("ident_b", [P, P], BF16)
        w_f = ph.sb("w_f", [P, KD, D])
        small = ph.sb("small", [P, KD, D])
        large = ph.sb("large", [P, KD, D])
        w8 = ph.sb("w8", [P, KD, D], FP8)
        wb = ph.sb("wb", [P, KD, D], BF16)
        wT = ph.sb("wT", [P, KD, D], BF16)
        bias_r = ph.sb("bias_r", [P, D])
        x_t = ph.sb("x_t", [P, 2, T, D])
        x8 = ph.sb("x8", [P, 2, T, D], FP8)
        xb = ph.sb("xb", [P, 2, T, D], BF16)
        xT = ph.sb("xT", [P, 2, KD, S], BF16)
        y16 = ph.sb("y16", [P, 2, T, D], F16)
        stats = ph.sb("stats", [P, T, 6])
        mv = ph.sb("mv", [P, T, 2])
        rstd = ph.sb("rstd", [P, T])
        minus_half = ph.sb("minus_half", [P, T])
        wait_slot = ph.sb("wait_slot", [P, 1])
        (const_in, w_step, wT_full, wT_ok, ln, ln_pow, xT_full, xT_ok, o_full, y_ok, fin, pool_const) = (
            ph.sem(n) for n in "const_in w_step wT_full wT_ok ln ln_pow xT_full xT_ok o_full y_ok fin pool_const".split())
        x_ok = [ph.sem(f"x_ok{i}") for i in range(2)]
        stored = [ph.sem(f"stored{i}") for i in range(2)]
        block = ph.ctx.enter_context(nc.Block())

        @block.sync
        def _(sp):
            sp.dma_start(ident_b[:, :], consts["ident_b"]).then_inc(const_in, 16)
            sp.dma_start(w_f[:, :, :], weight.rearrange("(j p) d -> p j d", p=P)).then_inc(const_in, 16)
            sp.dma_start(bias_r[:, :], bias.partition_broadcast(P)).then_inc(const_in, 16)
            for s in range(2):
                sp.sem_inc(stored[s], 16)
            with sp.Fori(0, n_batch // 2) as i:
                for s in range(2):
                    sp.wait_ge(stored[s], 16 + 16 * i)
                    sp.dma_start(x_t[:, s, :, :], x_in[2 * i + s].rearrange("(t p) d -> p t d", p=P)).then_inc(x_ok[s], 16)
            for s in range(2):
                sp.wait_ge(stored[s], 16 + 8 * n_batch)

        @block.gpsimd
        def _(pool):
            pool.sem_inc(fin, 4)
            pool.memset(minus_half[:, :], -0.5).then_inc(pool_const, 1)
            pool.wait_ge(pool_const, 1)
            pool.wait_ge(const_in, 48)

            def rstds(n):
                pool.wait_ge(ln, NL * n + 5)
                pool.tensor_tensor(rstd[:, :], rstd[:, :], minus_half[:, :], ALU.pow).then_inc(ln_pow, 1)

            rstds(0)

            def body(n, i, s, last):
                if not last:
                    rstds(n + 1)
                for t in range(T):
                    pool.wait_ge(y_ok, 2 * T + T * n + t + 1)
                    pool.tensor_tensor(x_t[:, s, t, :], x_t[:, s, t, :], y16[:, s, t, :], ALU.add).then_inc(fin, 1)
            over_pairs(pool, n_batch, body)

        @block.tensor
        def _(pe):
            pe.wait_ge(const_in, 48)
            pe.wait_ge(w_step, 9)
            for k in range(KD):
                if k >= 2:
                    pe.wait_ge(wT_ok, k - 1)
                for j in range(4):
                    mm = pe.transpose(B[k % 2][:, j * P:(j + 1) * P], wb[:, j, k * P:(k + 1) * P], ident_b[:, :])
                mm.then_inc(wT_full, 1)
            pe.wait_ge(wT_ok, KD)
            pe.sem_inc(xT_full, 2)
            with pe.Fori(0, n_batch // 2) as i:
                for s in range(2):
                    n = 2 * i + s
                    pe.wait_ge(ln, NL * n + 9)
                    pe.wait_ge(xT_ok, n + 1)
                    for k in range(KD):
                        for t in range(T):
                            mm = pe.transpose(B[s][:, (k * T + t) * P:(k * T + t + 1) * P], xb[:, s, t, k * P:(k + 1) * P], ident_b[:, :])
                    mm.then_inc(xT_full, 1)
                    pe.wait_ge(xT_ok, n + 3)
                    pe.wait_ge(y_ok, T * n + T)
                    for t in range(T):
                        for k in range(KD):
                            mm = pe.matmul(O[2 * s + t][:, :], xT[:, s, k, t * P:(t + 1) * P], wT[:, k, :], start=(k == 0), stop=(k == KD - 1))
                    mm.then_inc(o_full, 1)

        @block.scalar
        def _(act):
            act.sem_inc(xT_ok, 2)
            for k in range(KD):
                act.wait_ge(wT_full, k + 1)
                act.activation(wT[:, k, :], B[k % 2][:, 0:D], ACT.Copy).then_inc(wT_ok, 1)
            with act.Fori(0, n_batch // 2) as i:
                for s in range(2):
                    n = 2 * i + s
                    act.wait_ge(xT_full, 2 + n + 1)
                    act.activation(xT[:, s, :, :].rearrange("p k n -> p (k n)"), B[s][:, :], ACT.Copy).then_inc(xT_ok, 1)
                    act.wait_ge(fin, 4 + T * n + T)
                    act.dma_start(x_out[n].rearrange("(t p) d -> p t d", p=P), x_t[:, s, :, :]).then_inc(stored[s], 16)

        @block.vector
        def _(dve):
            dve.wait_ge(const_in, 48)
            steps = [
                lambda: dve.tensor_scalar(small[:, :, :], w_f[:, :, :], 240.0, -240.0, ALU.min, ALU.max),
                lambda: dve.tensor_copy(w8[:, :, :], small[:, :, :], saturate=False),
                lambda: dve.tensor_copy(small[:, :, :], w8[:, :, :]),
                lambda: dve.tensor_scalar(large[:, :, :], w_f[:, :, :], 448.0, -448.0, ALU.min, ALU.max),
            ]
            n = 0
            for step in steps:
                n += 1
                step().then_inc(w_step, 1)
                dve.wait_ge(w_step, n)
            dve.tensor_scalar(w8[:, :, :], large[:, :, :], 0.5, None, ALU.mult, saturate=False).then_inc(w_step, 1)
            dve.wait_ge(w_step, 5)
            dve.scalar_tensor_tensor(large[:, :, :], w8[:, :, :], 2.0, small[:, :, :], ALU.mult, ALU.subtract).then_inc(w_step, 1)
            dve.tensor_tensor(w_f[:, :, :], w_f[:, :, :], w_f[:, :, :], ALU.mult).then_inc(w_step, 1)
            dve.wait_ge(w_step, 7)
            dve.tensor_scalar(w_f[:, :, :], w_f[:, :, :], 256.0, None, ALU.is_ge).then_inc(w_step, 1)
            dve.wait_ge(w_step, 8)
            dve.tensor_tensor(large[:, :, :], large[:, :, :], w_f[:, :, :], ALU.mult).then_inc(pool_const, 1)
            dve.wait_ge(pool_const, 2)
            dve.tensor_tensor(wb[:, :, :], large[:, :, :], small[:, :, :], ALU.add).then_inc(w_step, 1)
            dve.sem_inc(y_ok, 2 * T)

            def norm(n, i, s):
                dve.wait_ge(x_ok[s], 16 * i + 16)
                for t in range(T):
                    dve.bn_stats(stats[:, t, :], x_t[:, s, t, :]).then_inc(ln, 1)
                dve.wait_ge(ln, NL * n + 2)
                dve.memset(wait_slot[:, :], 0.0)
                for t in range(T):
                    dve.bn_aggr(mv[:, t, :], stats[:, t, :]).then_inc(ln, 1)
                dve.wait_ge(ln, NL * n + 4)
                dve.tensor_scalar(rstd[:, :], mv[:, :, 1], EPS, None, ALU.add).then_inc(ln, 1)
                dve.wait_ge(ln_pow, n + 1)
                dve.memset(wait_slot[:, :], 0.0)
                for t in range(T):
                    dve.tensor_scalar(x8[:, s, t, :], x_t[:, s, t, :], mv[:, t, 0:1], rstd[:, t:t + 1], ALU.subtract, ALU.mult, saturate=False).then_inc(ln, 1)
                dve.wait_ge(ln, NL * n + 7)
                dve.memset(wait_slot[:, :], 0.0)
                for t in range(T):
                    dve.tensor_copy(xb[:, s, t, :], x8[:, s, t, :]).then_inc(ln, 1)

            norm(0, 0, 0)

            def body(n, i, s, last):
                if not last:
                    norm(n + 1, i + s, 1 - s)
                for t in range(T):
                    dve.tensor_tensor(x_t[:, s, t, :], x_t[:, s, t, :], bias_r[:, :], ALU.add)
                dve.wait_ge(o_full, n + 1)
                dve.wait_ge(fin, T * n + T)
                for t in range(T):
                    dve.tensor_copy(y16[:, s, t, :], O[2 * s + t][:, :]).then_inc(y_ok, 1)
            over_pairs(dve, n_batch, body)


def constants():
    bf16 = np.dtype("bfloat16")
    pos = np.arange(S, dtype=np.float32)
    half = 32
    freq = np.power(np.float32(ROPE_BASE), np.arange(half, dtype=np.float32) / np.float32(half)).astype(np.float32)
    angles = pos[:, None] / np.concatenate([freq, freq])[None, :]
    sign = np.concatenate([-np.ones(half), np.ones(half)]).astype(np.float32)

    def rows(a):
        return np.ascontiguousarray(a.reshape(T, P, -1).transpose(1, 0, 2))
    return {
        "ident": np.eye(P, dtype=np.float32),
        "ident_b": np.eye(P).astype(bf16),
        "mask_b": np.triu(np.full((P, P), -1e9), 1).astype(bf16),
        "cos": rows(np.cos(angles).astype(np.float32)),
        "sin": rows((np.sin(angles) * sign).astype(np.float32)),
    }


def decoder(nc, a, c, out, n_batch):
    def scratch(name, shape):
        return nc.dram_tensor(name, shape, F32, kind="Internal").ap()
    def self0(x, y):
        attention_phase(nc, "self0", n_batch, x, y, c, a["L0_attn_W_Q"], a["L0_attn_W_K"], a["L0_attn_W_V"], a["L0_attn_W_O"],
                        64, True, True, bq=a["L0_attn_b_Q"], bk=a["L0_attn_b_K"], bv=a["L0_attn_b_V"], bo=a["L0_attn_b_O"],
                        rope=(c["cos"], c["sin"]))

    def cross0(x, y):
        attention_phase(nc, "cross0", n_batch, x, y, c, a["L0_xattn_Wq"], a["L0_xattn_Wk"], a["L0_xattn_Wv"], a["L0_xattn_Wo"],
                        32, True, False, ctx=a["ctx_1024"])

    def cross1(x, y):
        attention_phase(nc, "cross1", n_batch, x, y, c, a["L1_xattn_Wq"], a["L1_xattn_Wk"], a["L1_xattn_Wv"], a["L1_xattn_Wo"],
                        32, False, False, ctx=a["ctx_1024"], bq=a["L1_xattn_bq"], bk=a["L1_xattn_bk"], bv=a["L1_xattn_bv"],
                        bo=a["L1_xattn_bo"])

    E, HID = a["L0_ffn_w1"].shape[0], a["L0_ffn_w1"].shape[2]
    logits_d, sel_d = scratch("logits", (n_batch, E, S)), scratch("sel", (n_batch, E, S))
    selT_d = scratch("selT", (n_batch, T, P, E))
    out_d = scratch("experts_out", (n_batch, HID // 512, E, D))
    x_norm = scratch("x_norm", (n_batch, S, D))

    def experts(x):
        expert_phase(nc, n_batch, x, x_norm, c, a["L0_ffn_gate_w"], a["L0_ffn_gate_b"], a["L0_ffn_w1"], a["L0_ffn_w2"],
                     logits_d, sel_d, selT_d, out_d)

    def norm1(x, y):
        norm_attention_phase(nc, n_batch, x, y, c, sel_d, out_d, a["L0_ffn_w2"], a["L1_attn_Wq"], a["L1_attn_bq"],
                             a["L1_attn_Wk"], a["L1_attn_bk"], a["L1_attn_Wv"], a["L1_attn_bv"])

    def fp8(x, y):
        fp8_linear_phase(nc, n_batch, x, y, c, a["L1_ffn_weight"], a["L1_ffn_bias"])

    x1, x2, x4, x5 = (scratch(f"x{i}", (n_batch, S, D)) for i in (1, 2, 4, 5))
    self0(a["x"], x1)
    cross0(x1, x2)
    experts(x2)
    norm1(x2, x4)
    cross1(x4, x5)
    fp8(x5, out)

def kernel(**inputs):
    import concourse.bacc as bacc
    from concourse.bass_utils import run_bass_kernel_spmd

    nc = bacc.Bacc("TRN2", target_bir_lowering=False, num_devices=1)
    arrays, a, c = {}, {}, {}
    for group, made in ((a, inputs), (c, constants())):
        for name, value in made.items():
            value = np.ascontiguousarray(value)
            arrays[f"in_{name}"] = value
            group[name] = nc.dram_tensor(f"in_{name}", value.shape, mybir.dt.from_np(value.dtype), kind="ExternalInput").ap()
    n_batch = a["x"].shape[0]
    out = nc.dram_tensor("out_x", (n_batch, S, D), F32, kind="ExternalOutput").ap()
    decoder(nc, a, c, out, n_batch)
    r = run_bass_kernel_spmd(nc, [arrays], core_ids=[0])
    return r.results[0]["out_x"]
```

```python
from contextlib import ExitStack

import numpy as np

import concourse.bass as bass
from concourse import mybir

F32 = mybir.dt.float32
F32R = mybir.dt.float32r
BF16 = mybir.dt.bfloat16
F16 = mybir.dt.float16
FP8 = mybir.dt.float8e4
ALU = mybir.AluOpType
ACT = mybir.ActivationFunctionType
AX = mybir.AxisListType

P = 128
D = 512
KD = D // P
S = 256
T = S // P
H = 16
EPS = 1e-5
ROPE_BASE = 10000.0


class Phase:

    def __init__(self, nc, name):
        self.nc, self.name, self.ctx, self.sems = nc, name, ExitStack(), []

    def __enter__(self):
        self.ctx.__enter__()
        self.ctx.callback(self.clear)
        return self

    def __exit__(self, *a):
        return self.ctx.__exit__(*a)

    def clear(self):
        self.nc.clear_and_free_semaphores(self.sems)
        self.nc.all_engine_barrier()

    def sb(self, name, shape, dt=F32):
        return self.ctx.enter_context(self.nc.sbuf_tensor(f"{self.name}_{name}", shape, dt))

    def bank(self, name, dt=F32):
        return self.ctx.enter_context(self.nc.psum_tensor(f"{self.name}_{name}", [P, 2048 // (2 if dt == BF16 else 4)], dt))

    def sem(self, name):
        self.sems.append(self.nc.alloc_semaphore(name=f"{self.name}_{name}"))
        return self.sems[-1]


def split_products(pe, out, pairs):
    for i, ((ah, al), (bh, bl)) in enumerate(pairs):
        first, last = i == 0, i == len(pairs) - 1
        pe.matmul(out, ah, bh, start=first, stop=False)
        pe.matmul(out, ah, bl, start=False, stop=False)
        mm = pe.matmul(out, al, bh, start=False, stop=last)
    return mm


def after(eng, sem, value):
    if not isinstance(value, int) or value > 0:
        eng.wait_ge(sem, value)


def over_rotated(eng, n, body, tail):
    body(0, True, False)
    if n > 2:
        with eng.Fori(1, n - 1) as b:
            body(b, False, False)
    body(n - 1, False, True)
    tail(n)


class Uses:

    def __init__(self, plan, before, n_batch):
        self.keys = [k for step in plan for k in step]
        self.before, self.n, self.n_batch = before, len(self.keys), n_batch
        self.n_out = sum(k[0] == "O" for k in self.keys)
        assert self.n % 2 == 0 and self.n_out % 2 == 0

    def here(self, b, first, last):
        if isinstance(b, int) and b == self.n_batch:
            return [k for k in self.keys if k[0] == "O"]
        return [k for k in self.keys if not (first and k[0] == "O") and not (last and k[0] == "+")]

    def start(self, b):
        if isinstance(b, int) and b == 0:
            return self.before
        if isinstance(b, int) and b == self.n_batch:
            return self.start(b - 1) + len(self.here(b - 1, False, True))
        return self.before - self.n_out + b * self.n

    def at(self, key, b, first, last):
        return self.start(b) + self.here(b, first, last).index(key)

    def bank(self, key, b, first, last):
        b = b if isinstance(b, int) else 2
        return self.at(key, b, first, last) % 2


def attention_phase(nc, name, n_batch, x_in, x_out, consts, wq, wk, wv, wo,
                    d_head, causal, rotary, ctx=None, bq=None, bk=None, bv=None, bo=None, rope=None):
    HD = H * d_head
    CH = HD // 512
    HPT = P // d_head
    NT = H // HPT
    SCALE = 1.0 / float(np.sqrt(d_head))
    T_LAG, V_LAG, Z_LAG = 3, 5, 6
    KQ = [P * (t + 1) if causal else S for t in range(T)]
    SOFF = [sum(KQ[:t]) for t in range(T)]
    SW = sum(KQ)
    QK = [P * k if causal else 0 for k in range(T)]
    TOFF = [sum(S - QK[j] for j in range(k)) for k in range(T)]
    NP = 4
    NPT = 2 if rotary else 4
    N_LN = KD // 2
    PLAN = [[] for _ in range(H)]
    if rotary:
        for g in range(1, NT):
            PLAN[2 * g - 2].append(("Q", g))
        for i, key in ((0, (0, 1, 0)), (1, (0, 1, 1)), (2, (1, 1, 0)), (3, (1, 1, 1))):
            PLAN[i].append(("P",) + key)
        PLAN[5] += [("V", 1, 0), ("V", 1, 1)]
        PLAN[6] += [("O", 0), ("O", 1)]
        PLAN[8] += [("+", "X", 0)]
        PLAN[9] += [("+", "X", 1)]
        for i, key in ((11, (0, 0, 0)), (11, (0, 0, 1)), (12, (1, 0, 0)), (12, (1, 0, 1))):
            PLAN[i].append(("+", "P") + key)
        PLAN[13] += [("+", "V", 0, 0), ("+", "V", 0, 1)]
        PLAN[14].append(("+", "Q", 0))
        BEFORE = [("X", 0), ("X", 1), ("P", 0, 0, 0), ("P", 0, 0, 1), ("P", 1, 0, 0), ("P", 1, 0, 1),
                  ("V", 0, 0), ("V", 0, 1), ("Q", 0)]
        STATS_AT, APPLY_AT = 4, 7
        LATE_V = {H // 2: ("V", 1, 1)}
    else:
        PLAN[1] += [("Q", 1)]
        PLAN[5] += [("V", 0, 0), ("V", 0, 1)]
        PLAN[4] += [("Q", 2)]
        PLAN[6] += [("O", 0), ("O", 1)]
        PLAN[7] += [("Q", 3)]
        PLAN[8] += [("+", "X", 0)]
        PLAN[9] += [("+", "X", 1)]
        PLAN[10] += [("+", "C", 0)]
        PLAN[11] += [("+", "C", 1)]
        PLAN[13] += [("+", "Q", 0)]
        BEFORE = [("X", 0), ("X", 1), ("C", 0), ("C", 1), ("Q", 0)]
        STATS_AT, APPLY_AT = 4, 6
        LATE_V = {0: ("V", 0, 1)}
    N_W = 0 if rotary else 4 * KD
    uses = Uses(PLAN, N_W + len(BEFORE), n_batch)
    with_act = [k for k in uses.keys if k[k[0] == "+"] in "QXC"]
    before_act = [k for k in BEFORE if k[0] in "QXC"]
    P_PER = 4 * CH
    P_BEFORE = 4

    def hi_at(key, b, last):
        here = [k for k in with_act if not (last and k[0] == "+")]
        return N_W + len(before_act) + b * len(with_act) + here.index(key)

    with Phase(nc, name) as ph:
        A = [ph.bank(f"A{i}") for i in range(2)]
        SC = [ph.bank(f"S{i}") for i in range(2)]
        TP = [ph.bank(f"T{i}") for i in range(2)]
        Z = [ph.bank(f"Z{i}") for i in range(2)]

        ident = ph.sb("ident", [P, P])
        ident_b = ph.sb("ident_b", [P, P], BF16)
        mask_b = ph.sb("mask_b", [P, P], BF16)
        x_t = ph.sb("x_t", [P, T, D])
        res = ph.sb("res", [P, T, D])
        stats = ph.sb("stats", [P, T, 6])
        mv = ph.sb("mv", [P, T, 2])
        rstd = ph.sb("rstd", [P, T])
        wait_slot = ph.sb("wait_slot", [P, 1])
        minus_half = ph.sb("minus_half", [P, T])
        xT = [ph.sb(f"xT{i}", [P, KD, S], F32R) for i in "hl"]
        V = ph.sb("V", [P, T, HD])
        n_qt = 4
        n_kt = n_qt * HPT
        QT = ph.sb("QT", [P, n_qt, S])
        KT = ph.sb("KT", [P, n_kt, S])
        neg_max = ph.sb("neg_max", [P, H, T])
        sums = ph.sb("sums", [P, H, T])
        rsum = ph.sb("rsum", [P, H, T])
        prob = ph.sb("prob", [P, NP, SW])
        probT = ph.sb("probT", [P, NPT, SW])
        wvs = [ph.sb(f"wv{i}", [P, KD, HD], F32R) for i in "hl"]
        wqs = [ph.sb(f"wq{i}", [P, KD, HD], F32R) for i in "hl"]
        wks = [ph.sb(f"wk{i}", [P, KD, HD], F32R) for i in "hl"]
        if rotary:
            q_t = ph.sb("q_t", [P, T, HD])
            k_t = ph.sb("k_t", [P, T, HD])
            turn = ph.sb("turn", [P, 2, 512])
            cos = ph.sb("cos", [P, T, d_head])
            sin = ph.sb("sin", [P, T, d_head])
            rb = ph.sb("rb", [P, 2, T, HD])
            wo_f = ph.sb("wo_f", [P, NT, D])
            zT = ph.sb("zT", [P, NT, S])
            stage = [q_t, k_t, V]
        else:
            c_t = ph.sb("c_t", [P, T, D])
            cT = [ph.sb(f"cT{i}", [P, KD, S], F32R) for i in "hl"]
            wos = [ph.sb(f"wo{i}", [P, KD, D], F32R) for i in "hl"]
            zTs = [ph.sb(f"zT{i}", [P, NT, S], F32R) for i in "hl"]
            w_stage = ph.sb("w_stage", [P, 4, KD, D])
        if bq is not None and not rotary:
            bq_c = ph.sb("bq_c", [P, NT])
            bk_c = ph.sb("bk_c", [P, NT])
        if bv is not None:
            bv_c = ph.sb("bv_c", [P, NT])
        if bo is not None:
            bo_r = ph.sb("bo_r", [P, D])

        const_in = ph.sem("const_in")
        w_in = [ph.sem(f"w_in{i}") for i in range(4)]
        wo_in = ph.sem("wo_in")
        w_hi = ph.sem("w_hi")
        w_lo = ph.sem("w_lo")
        x_ok = ph.sem("x_ok")
        c_ok = ph.sem("c_ok")
        res_in = ph.sem("res_in")
        res_b = ph.sem("res_b")
        stored = ph.sem("stored")
        ln = ph.sem("ln")
        ln_pow = ph.sem("ln_pow")
        a_full = ph.sem("a_full")
        a_hi = ph.sem("a_hi")
        a_free = ph.sem("a_free")
        rot = ph.sem("rot")
        rb_ok = ph.sem("rb_ok")
        zeroed = ph.sem("zeroed")
        s_full = ph.sem("s_full")
        max_ok = ph.sem("max_ok")
        exp_ok = ph.sem("exp_ok")
        rsum_ok = ph.sem("rsum_ok")
        norm_ok = ph.sem("norm_ok")
        t_full = ph.sem("t_full")
        pt_even = ph.sem("pt_even")
        pt_odd = ph.sem("pt_odd")
        pv_ok = ph.sem("pv_ok")
        pool_const = ph.sem("pool_const")
        z_hi = ph.sem("z_hi")
        z_ok = ph.sem("z_ok")

        N_CONST = 3 + (2 if rotary else 0) + sum(v is not None for v in (bv, bo)) \
            + (0 if bq is None else 4 if rotary else 2)
        N_STAGE = 3 * 2 if rotary else 4

        block = ph.ctx.enter_context(nc.Block())

        @block.sync
        def _(sp):
            sp.dma_start(ident[:, :], consts["ident"]).then_inc(const_in, 16)
            sp.dma_start(ident_b[:, :], consts["ident_b"]).then_inc(const_in, 16)
            sp.dma_start(mask_b[:, :], consts["mask_b"]).then_inc(const_in, 16)
            sp.dma_start(x_t[:, :, :], x_in[0].rearrange("(t p) d -> p t d", p=P)).then_inc(x_ok, 16)
            if rotary:
                sp.dma_start(cos[:, :, :], rope[0]).then_inc(const_in, 16)
                sp.dma_start(sin[:, :, :], rope[1]).then_inc(const_in, 16)
                for j, b_ in enumerate((bq, bk)):
                    for t in range(T):
                        sp.dma_start(rb[:, j, t, :], b_.rearrange("h k -> (h k)").partition_broadcast(P)).then_inc(const_in, 16)
                sp.dma_start(bv_c[:, :], bv.rearrange("h k -> (h k)").rearrange("(t p) -> p t", p=P),
                             allow_slow_non_contiguous=True).then_inc(const_in, 16)
                sp.dma_start(bo_r[:, :], bo.partition_broadcast(P)).then_inc(const_in, 16)
                for i in range(N_STAGE):
                    w = (wq, wk, wv)[i // 2]
                    if i >= 3:
                        sp.wait_ge(w_lo, i - 2)
                    hh = i % 2
                    for k in range(KD):
                        sp.dma_start(
                            stage[i % 3][:, :, :].rearrange("p t n -> p (t n)")[:, k * 512:(k + 1) * 512].rearrange("p (h e) -> p h e", e=d_head),
                            w[hh * H // 2:(hh + 1) * H // 2, k * P:(k + 1) * P, :].rearrange("h p e -> p h e"),
                        ).then_inc(w_in[i % 3], 16)
                sp.dma_start(wo_f[:, :, :], wo.rearrange("h e m -> (h e) m").rearrange("(k p) m -> p k m", p=P)).then_inc(wo_in, 16)
            else:
                for v, col in ((bq, "bq_c"), (bk, "bk_c"), (bv, "bv_c")):
                    if v is not None:
                        to = {"bq_c": bq_c, "bk_c": bk_c, "bv_c": bv_c}[col]
                        sp.dma_start(to[:, :], v.rearrange("(t p) -> p t", p=P), allow_slow_non_contiguous=True).then_inc(const_in, 16)
                if bo is not None:
                    sp.dma_start(bo_r[:, :], bo.partition_broadcast(P)).then_inc(const_in, 16)
                for i, w in enumerate((wq, wk, wv, wo)):
                    sp.dma_start(w_stage[:, i, :, :], w.rearrange("(j p) d -> p j d", p=P)).then_inc(w_in[i], 16)
                sp.dma_start(c_t[:, :, :], ctx[0].rearrange("(t p) d -> p t d", p=P)).then_inc(c_ok, 16)

            def store(b, first, last):
                sp.wait_ge(a_free, uses.at(("O", 1), b, first, last) + 1)
                sp.dma_start(x_out[b - 1].rearrange("(t p) d -> p t d", p=P), res[:, :, :]).then_inc(stored, 16)
                sp.wait_ge(stored, b * 16)

            def body(b, first, last):
                if not last:
                    sp.wait_ge(a_full, uses.start(b))
                    sp.dma_start(x_t[:, :, :], x_in[b + 1].rearrange("(t p) d -> p t d", p=P)).then_inc(x_ok, 16)
                    if not rotary:
                        sp.dma_start(c_t[:, :, :], ctx[b + 1].rearrange("(t p) d -> p t d", p=P)).then_inc(c_ok, 16)
                if not first:
                    store(b, first, last)
                sp.dma_start(res[:, :, :], x_in[b].rearrange("(t p) d -> p t d", p=P)).then_inc(res_in, 16)

            over_rotated(sp, n_batch, body, lambda b: store(b, False, False))

        @block.gpsimd
        def _(pool):
            def rstds(n):
                pool.wait_ge(ln, 7 * n + 5)
                pool.tensor_tensor(rstd[:, :], rstd[:, :], minus_half[:, :], ALU.pow).then_inc(ln_pow, 1)

            pool.memset(minus_half[:, :], -0.5).then_inc(pool_const, 1)
            pool.wait_ge(pool_const, 1)
            rstds(0)
            pool.wait_ge(const_in, 16 * N_CONST)
            if rotary:
                pool.wait_ge(rb_ok, 3 * 2 * T * CH)

            def turned(key, u, seq):
                _, which, c, t = key
                dst = (q_t, k_t)[which][:, t, c * 512:(c + 1) * 512]
                pool.wait_ge(a_free, u + 1)
                pool.tensor_tensor(dst, dst, turn[:, t % 2, :], ALU.add).then_inc(rot, 1)
                pool.wait_ge(rot, 2 * seq + 1)
                pool.tensor_tensor(dst, dst, rb[:, which, t, c * 512:(c + 1) * 512], ALU.add).then_inc(rot, 1)

            for key in BEFORE:
                if key[0] == "P":
                    turned(key, N_W + BEFORE.index(key), [k for k in BEFORE if k[0] == "P"].index(key))

            def body(b, first, last):
                seq = 0
                for i in range(H):
                    for key in PLAN[i]:
                        ahead = key[0] == "+"
                        if key[ahead] == "P" and not (ahead and last):
                            turned(key[ahead:], uses.at(key, b, first, last), P_BEFORE + b * P_PER + seq)
                            seq += 1
                    if i == STATS_AT and not last:
                        rstds(b + 1)
                    pool.wait_ge(rsum_ok, b * H + i + 1)
                    for t in range(T):
                        pr = prob[:, i % NP, SOFF[t]:SOFF[t] + KQ[t]]
                        ins = pool.tensor_tensor(pr, pr, rsum[:, i, t:t + 1].to_broadcast([P, KQ[t]]), ALU.mult)
                    ins.then_inc(norm_ok, 1)
                if bo is not None:
                    pool.wait_ge(res_in, b * 16 + 16)
                    for t in range(T):
                        pool.tensor_tensor(res[:, t, :], res[:, t, :], bo_r[:, :], ALU.add).then_inc(res_b, 1)
            over_rotated(pool, n_batch, body, lambda b: None)

        @block.tensor
        def _(pe):
            pe.wait_ge(const_in, 16 * N_CONST)

            def bank_for(u):
                after(pe, a_free, u - 1)

            def proj_tokens(u, bank, src, w, t, c):
                bank_for(u)
                split_products(pe, A[bank][:, :], [
                    ((src[0][:, k, t * P:(t + 1) * P], src[1][:, k, t * P:(t + 1) * P]),
                     (w[0][:, k, c * 512:(c + 1) * 512], w[1][:, k, c * 512:(c + 1) * 512])) for k in range(KD)
                ]).then_inc(a_full, 1)

            def extra(key, u, bank, n):
                kind = key[0]
                if kind in "XC":
                    if kind == "X":
                        pe.wait_ge(ln, n * 7 + 7)
                    else:
                        pe.wait_ge(c_ok, n * 16 + 16)
                    bank_for(u)
                    src = x_t if kind == "X" else c_t
                    for kk in range(2):
                        for t in range(T):
                            k = 2 * key[1] + kk
                            mm = pe.transpose(A[bank][:, (kk * T + t) * P:(kk * T + t + 1) * P], src[:, t, k * P:(k + 1) * P], ident[:, :])
                    mm.then_inc(a_full, 1)
                elif kind == "P":
                    proj_tokens(u, bank, xT, (wqs, wks)[key[1]], key[3], key[2])
                elif kind == "V":
                    proj_tokens(u, bank, xT if rotary else cT, wvs, key[2], key[1])
                elif kind == "Q" and rotary:
                    g = key[1]
                    pe.wait_ge(rot, 2 * (P_BEFORE + n * P_PER + (P_PER // CH) * (g // (NT // CH))))
                    bank_for(u)
                    for j, src in enumerate((q_t, k_t)):
                        for t in range(T):
                            mm = pe.transpose(A[bank][:, (j * T + t) * P:(j * T + t + 1) * P], src[:, t, g * P:(g + 1) * P], ident[:, :])
                    mm.then_inc(a_full, 1)
                elif kind == "Q":
                    g = key[1]
                    bank_for(u)
                    for j, (w, src) in enumerate(((wqs, xT), (wks, cT))):
                        mm = split_products(pe, A[bank][:, j * S:(j + 1) * S], [
                            ((w[0][:, k, g * P:(g + 1) * P], w[1][:, k, g * P:(g + 1) * P]),
                             (src[0][:, k, :], src[1][:, k, :])) for k in range(KD)])
                    mm.then_inc(a_full, 1)
                elif kind == "O":
                    t = key[1]
                    pe.wait_ge(z_ok, n * NT + NT)
                    bank_for(u)
                    if rotary:
                        for k in range(NT):
                            mm = pe.matmul(A[bank][:, :], zT[:, k, t * P:(t + 1) * P], wo_f[:, k, :], start=(k == 0), stop=(k == NT - 1))
                        mm.then_inc(a_full, 1)
                    else:
                        split_products(pe, A[bank][:, :], [
                            ((zTs[0][:, k, t * P:(t + 1) * P], zTs[1][:, k, t * P:(t + 1) * P]),
                             (wos[0][:, k, :], wos[1][:, k, :])) for k in range(KD)]).then_inc(a_full, 1)

            if not rotary:
                for u in range(N_W):
                    i, k = u // KD, u % KD
                    if k == 0:
                        pe.wait_ge(w_in[i], 16)
                    bank_for(u)
                    for j in range(4):
                        mm = pe.transpose(A[u % 2][:, j * P:(j + 1) * P], w_stage[:, i, j, k * P:(k + 1) * P], ident[:, :])
                    mm.then_inc(a_full, 1)
            n_x = sum(k[0] in "XC" for k in BEFORE)
            for j, key in enumerate(BEFORE):
                u = N_W + j
                if j == n_x:
                    pe.wait_ge(a_free, u)
                if rotary and key[0] in "PV":
                    pe.wait_ge(w_lo, 2 * key[1] + 1 if key[0] == "P" else 6)
                    if key[0] == "V":
                        pe.wait_ge(wo_in, 16)
                extra(key, u, u % 2, 0)
            pe.wait_ge(zeroed, 1)

            def scores(b, h, first, last):
                g = h // HPT
                if h == 0:
                    pe.wait_ge(a_free, uses.start(b))
                elif h % HPT == 0:
                    pe.wait_ge(a_free, uses.at(("Q", g), b, first, last) + 1)
                after(pe, exp_ok, b * H + h - 1)
                for t in range(T):
                    out = SC[h % 2][:, SOFF[t]:SOFF[t] + KQ[t]]
                    mm = pe.matmul(out, QT[:, g % n_qt, t * P:(t + 1) * P], KT[:, h % n_kt, 0:KQ[t]], start=True, stop=True, skip_group_check=causal)
                    if causal:
                        mm = pe.matmul(SC[h % 2][:, SOFF[t] + t * P:SOFF[t] + (t + 1) * P], ident_b[:, :], mask_b[:, :],
                                       start=False, stop=True, skip_group_check=True)
                mm.then_inc(s_full, 1)

            def prob_transposes(b, h):
                pe.wait_ge(norm_ok, b * H + h + 1)
                after(pe, (pt_even, pt_odd)[h % 2], b * (H // 2) + h // 2)
                for k in range(T):
                    for t in range(T):
                        if k * P < KQ[t]:
                            o = TOFF[k] + t * P - QK[k]
                            mm = pe.transpose(TP[h % 2][:, o:o + P], prob[:, h % NP, SOFF[t] + k * P:SOFF[t] + (k + 1) * P], ident[:, :])
                mm.then_inc(t_full, 1)

            def times_v(b, h, first, last):
                hh = h % H
                g, j = hh // HPT, hh % HPT
                pe.wait_ge((pt_even, pt_odd)[h % 2], b * (H // 2) + h // 2 + 1)
                if h in LATE_V:
                    pe.wait_ge(a_free, uses.at(LATE_V[h], b, first, last) + 1)
                if j == 0:
                    after(pe, z_ok, b * NT + h // HPT - 1)
                for k in range(T):
                    mm = pe.matmul(Z[g % 2][j * d_head:(j + 1) * d_head, QK[k]:S], V[:, k, hh * d_head:(hh + 1) * d_head],
                                   probT[:, h % NPT, TOFF[k]:TOFF[k] + S - QK[k]], start=(k == 0), stop=(k == T - 1),
                                   tile_position=(0, j * d_head))
                mm.then_inc(pv_ok, 1)

            def body(b, first, last):
                for i in range(H):
                    for key in PLAN[i]:
                        ahead = key[0] == "+"
                        if (ahead and last) or (first and key[0] == "O"):
                            continue
                        u = uses.at(key, b, first, last)
                        if key in (("+", "P", 0, 0, 0), ("+", "Q", 0)):
                            pe.wait_ge(a_free, u)
                        extra(key[ahead:], u, uses.bank(key, b, first, last), b + 1 if ahead else b - 1 if key[0] == "O" else b)
                    scores(b, i, first, last)
                    if not (first and i < T_LAG):
                        prob_transposes(b, i - T_LAG)
                    if not (first and i < V_LAG):
                        times_v(b, i - V_LAG, first, last)

            def tail(b):
                for i in range(V_LAG):
                    if i < T_LAG:
                        prob_transposes(b, i - T_LAG)
                    times_v(b, i - V_LAG, False, False)
                for t in range(T):
                    extra(("O", t), uses.at(("O", t), b, False, False), uses.bank(("O", t), b, False, False), b - 1)

            over_rotated(pe, n_batch, body, tail)

        @block.scalar
        def _(act):
            if rotary:
                for i in range(N_STAGE):
                    w = (wqs, wks, wvs)[i // 2]
                    act.wait_ge(w_in[i % 3], 16 * KD * (i // 3 + 1))
                    act.activation(w[0][:, :, (i % 2) * 512:(i % 2 + 1) * 512],
                                   stage[i % 3][:, :, :].rearrange("p t n -> p (t n)").rearrange("p (k n) -> p k n", k=KD), ACT.Copy).then_inc(w_hi, 1)
            else:
                for u in range(N_W):
                    act.wait_ge(a_full, u + 1)
                    act.activation((wqs, wks, wvs, wos)[u // KD][0][:, u % KD, :], A[u % 2][:, :], ACT.Copy).then_inc(a_hi, 1)
            if not rotary and bq is not None:
                act.wait_ge(zeroed, 2)
            act.wait_ge(const_in, 16 * N_CONST)

            def extra(key, u, bank, n):
                if key[0] in "XC":
                    act.wait_ge(a_full, u + 1)
                    j = key[1]
                    act.activation((xT if key[0] == "X" else cT)[0][:, 2 * j:2 * j + 2, :].rearrange("p k n -> p (k n)"),
                                   A[bank][:, :], ACT.Copy).then_inc(a_hi, 1)
                elif key[0] == "Q":
                    g = key[1]
                    act.wait_ge(a_full, u + 1)
                    after(act, s_full, n * H + HPT * (g + 1 - n_qt))
                    if rotary or bq is None:
                        act.activation(QT[:, g % n_qt, :], A[bank][:, 0:S], ACT.Copy, scale=SCALE).then_inc(a_hi, 1)
                    else:
                        act.activation(QT[:, g % n_qt, :], A[bank][:, 0:S], ACT.Identity, bias=bq_c[:, g:g + 1], scale=SCALE).then_inc(a_hi, 1)

            for j, key in enumerate(BEFORE):
                extra(key, N_W + j, (N_W + j) % 2, 0)

            def exps(b, h):
                act.wait_ge(max_ok, b * H + h + 1)
                after(act, t_full, b * H + h - NP + 1)
                for t in range(T):
                    ins = act.activation(prob[:, h % NP, SOFF[t]:SOFF[t] + KQ[t]], SC[h % 2][:, SOFF[t]:SOFF[t] + KQ[t]], ACT.Exp,
                                         bias=neg_max[:, h, t:t + 1], scale=1.0, accum_out=sums[:, h, t:t + 1])
                ins.then_inc(exp_ok, 1)

            def probs_odd(b, h):
                if h % 2:
                    act.wait_ge(t_full, b * H + h + 1)
                    after(act, pv_ok, b * H + h - NPT + 1)
                    act.activation(probT[:, h % NPT, :], TP[1][:, 0:SW], ACT.Copy).then_inc(pt_odd, 1)

            def heads_hi(b, h):
                if not rotary and h % HPT == HPT - 1:
                    g = (h % H) // HPT
                    act.wait_ge(pv_ok, b * H + h + 1)
                    if bv is None:
                        act.activation(zTs[0][:, g, :], Z[g % 2][:, 0:S], ACT.Copy).then_inc(z_hi, 1)
                    else:
                        act.activation(zTs[0][:, g, :], Z[g % 2][:, 0:S], ACT.Identity, bias=bv_c[:, g:g + 1]).then_inc(z_hi, 1)

            def body(b, first, last):
                for i in range(H):
                    if not (first and i < Z_LAG):
                        heads_hi(b, i - Z_LAG)
                    for key in PLAN[i]:
                        ahead = key[0] == "+"
                        if not (ahead and last) and key[ahead] in "QXC":
                            extra(key[ahead:], uses.at(key, b, first, last), uses.bank(key, b, first, last), b + 1 if ahead else b)
                    exps(b, i)
                    if not (first and i < T_LAG):
                        probs_odd(b, i - T_LAG)

            def tail(b):
                for i in range(Z_LAG):
                    heads_hi(b, i - Z_LAG)
                    if i < T_LAG:
                        probs_odd(b, i - T_LAG)

            over_rotated(act, n_batch, body, tail)

        @block.vector
        def _(dve):
            dve.memset(KT[:, :, :], 0.0).then_inc(zeroed, 1)
            def norm_stats(n):
                dve.wait_ge(x_ok, 16 * n + 16)
                for t in range(T):
                    dve.bn_stats(stats[:, t, :], x_t[:, t, :]).then_inc(ln, 1)
                dve.wait_ge(ln, 7 * n + 2)
                dve.memset(wait_slot[:, :], 0.0)
                for t in range(T):
                    dve.bn_aggr(mv[:, t, :], stats[:, t, :]).then_inc(ln, 1)
                dve.wait_ge(ln, 7 * n + 4)
                dve.tensor_scalar(rstd[:, :], mv[:, :, 1], EPS, None, ALU.add).then_inc(ln, 1)

            def apply_norm(n):
                dve.wait_ge(ln_pow, n + 1)
                for t in range(T):
                    dve.tensor_scalar(x_t[:, t, :], x_t[:, t, :], mv[:, t, 0:1], rstd[:, t:t + 1], ALU.subtract, ALU.mult).then_inc(ln, 1)

            def extra(key, u, bank, n, hi, seq):
                kind = key[0]
                if kind in "XC":
                    dst, j = xT if kind == "X" else cT, key[1]
                    dve.wait_ge(a_hi, hi + 1)
                    dve.tensor_tensor(dst[1][:, 2 * j:2 * j + 2, :].rearrange("p k n -> p (k n)"), A[bank][:, :],
                                      dst[0][:, 2 * j:2 * j + 2, :].rearrange("p k n -> p (k n)"), ALU.subtract).then_inc(a_free, 1)
                elif kind == "P":
                    _, which, c, t = key
                    dve.wait_ge(a_full, u + 1)
                    after(dve, rot, 2 * (seq - 1))
                    by_half = [v.rearrange("p (h a e) -> p h a e", a=2, e=d_head // 2)
                               for v in (A[bank][:, :], (q_t, k_t)[which][:, t, c * 512:(c + 1) * 512], turn[:, t % 2, :])]
                    turn_halves(dve, by_half[0], by_half[1], by_half[2], cos[:, t, :], sin[:, t, :], 512 // d_head, d_head)[1].then_inc(a_free, 1)
                elif kind == "V":
                    dve.wait_ge(a_full, u + 1)
                    dve.tensor_copy(V[:, key[2], key[1] * 512:(key[1] + 1) * 512], A[bank][:, :]).then_inc(a_free, 1)
                elif kind == "Q":
                    g = key[1]
                    dve.wait_ge(a_hi, hi + 1)
                    for j in range(HPT):
                        rows = slice(j * d_head, (j + 1) * d_head)
                        if rotary or bk is None:
                            ins = dve.tensor_copy(KT[rows, (g * HPT + j) % n_kt, :], A[bank][rows, S:2 * S])
                        else:
                            ins = dve.tensor_scalar(KT[rows, (g * HPT + j) % n_kt, :], A[bank][rows, S:2 * S], bk_c[rows, g:g + 1], None, ALU.add)
                    ins.then_inc(a_free, 1)
                elif kind == "O":
                    t = key[1]
                    dve.wait_ge(res_in, n * 16 + 16)
                    if bo is not None:
                        dve.wait_ge(res_b, (n + 1) * T)
                    dve.wait_ge(a_full, u + 1)
                    dve.tensor_tensor(res[:, t, :], A[bank][:, :], res[:, t, :], ALU.add).then_inc(a_free, 1)

            norm_stats(0)
            apply_norm(0)
            if rotary:
                dve.wait_ge(const_in, 16 * N_CONST)

                def turned_bias(n):
                    j, t, c = n // (T * CH), n // CH % T, n % CH
                    flat = rb[:, j, t, c * 512:(c + 1) * 512]
                    by_half = [v.rearrange("p (h a e) -> p h a e", a=2, e=d_head // 2) for v in (flat, turn[:, 0, :], turn[:, 1, :])]
                    turn_halves(dve, by_half[0], by_half[1], by_half[2], cos[:, t, :], sin[:, t, :], 512 // d_head, d_head)[1].then_inc(rb_ok, 2)
                    dve.wait_ge(rb_ok, 3 * n + 2)
                    dve.tensor_tensor(flat, turn[:, 0, :], turn[:, 1, :], ALU.add).then_inc(rb_ok, 1)
                    dve.wait_ge(rb_ok, 3 * n + 3)

                for i in range(N_STAGE):
                    w = (wqs, wks, wvs)[i // 2]
                    cs = slice((i % 2) * 512, (i % 2 + 1) * 512)
                    dve.wait_ge(w_hi, i + 1)
                    dve.tensor_tensor(w[1][:, :, cs], stage[i % 3][:, :, :].rearrange("p t n -> p (t n)").rearrange("p (k n) -> p k n", k=KD),
                                      w[0][:, :, cs], ALU.subtract).then_inc(w_lo, 1)
                    if i < 4:
                        for n in range(i * T * CH // 2, (i + 1) * T * CH // 2):
                            turned_bias(n)
            else:
                if bq is not None:
                    dve.wait_ge(const_in, 16 * N_CONST)
                    dve.wait_ge(zeroed, 1)
                    dve.tensor_scalar(bq_c[:, :], bq_c[:, :], SCALE, None, ALU.mult).then_inc(zeroed, 1)
                for u in range(N_W):
                    dve.wait_ge(a_hi, u + 1)
                    w = (wqs, wks, wvs, wos)[u // KD]
                    dve.tensor_tensor(w[1][:, u % KD, :], A[u % 2][:, :], w[0][:, u % KD, :], ALU.subtract).then_inc(a_free, 1)
                dve.wait_ge(const_in, 16 * N_CONST)
            for j, key in enumerate(BEFORE):
                hi = N_W + before_act.index(key) if key in before_act else None
                seq = [k for k in BEFORE if k[0] == "P"].index(key) if key[0] == "P" else None
                extra(key, N_W + j, (N_W + j) % 2, 0, hi, seq)

            def maxima(b, h):
                dve.wait_ge(s_full, b * H + h + 1)
                if causal:
                    for t in range(T):
                        ins = dve.tensor_reduce(neg_max[:, h, t:t + 1], SC[h % 2][:, SOFF[t]:SOFF[t] + KQ[t]], AX.X, ALU.max, negate=True)
                else:
                    ins = dve.tensor_reduce(neg_max[:, h, :], SC[h % 2][:, :].rearrange("p (t k) -> p t k", t=T), AX.X, ALU.max, negate=True)
                ins.then_inc(max_ok, 1)

            def sums_inverse(b, h):
                dve.wait_ge(exp_ok, b * H + h + 1)
                dve.reciprocal(rsum[:, h % H, :], sums[:, h % H, :]).then_inc(rsum_ok, 1)

            def probs_even(b, h):
                if h % 2 == 0:
                    dve.wait_ge(t_full, b * H + h + 1)
                    after(dve, pv_ok, b * H + h - NPT + 1)
                    dve.tensor_copy(probT[:, h % NPT, :], TP[0][:, 0:SW]).then_inc(pt_even, 1)

            def heads_done(b, h):
                if h % HPT == HPT - 1:
                    g = (h % H) // HPT
                    if rotary:
                        dve.wait_ge(pv_ok, b * H + h + 1)
                        dve.tensor_scalar(zT[:, g, :], Z[g % 2][:, 0:S], bv_c[:, g:g + 1], None, ALU.add).then_inc(z_ok, 1)
                    else:
                        dve.wait_ge(z_hi, b * NT + h // HPT + 1)
                        if bv is None:
                            dve.tensor_tensor(zTs[1][:, g, :], Z[g % 2][:, 0:S], zTs[0][:, g, :], ALU.subtract).then_inc(z_ok, 1)
                        else:
                            dve.scalar_tensor_tensor(zTs[1][:, g, :], Z[g % 2][:, 0:S], bv_c[:, g:g + 1], zTs[0][:, g, :],
                                                     ALU.add, ALU.subtract).then_inc(z_ok, 1)

            def body(b, first, last):
                seq = 0
                for i in range(H):
                    if not (first and i < Z_LAG):
                        heads_done(b, i - Z_LAG)
                    for key in PLAN[i]:
                        ahead = key[0] == "+"
                        if (ahead and last) or (first and key[0] == "O"):
                            continue
                        kind = key[ahead]
                        extra(key[ahead:], uses.at(key, b, first, last), uses.bank(key, b, first, last),
                              b - 1 if kind == "O" else b, hi_at(key, b, last) if kind in "QXC" else None, P_BEFORE + b * P_PER + seq)
                        seq += kind == "P"
                    maxima(b, i)
                    if not (first and i < 1):
                        sums_inverse(b, i - 1)
                    if i == STATS_AT and not last:
                        norm_stats(b + 1)
                    if i == APPLY_AT and not last:
                        apply_norm(b + 1)
                    if not (first and i < T_LAG):
                        probs_even(b, i - T_LAG)

            def tail(b):
                for i in range(Z_LAG):
                    heads_done(b, i - Z_LAG)
                    if i < 1:
                        sums_inverse(b, i - 1)
                    if i < T_LAG:
                        probs_even(b, i - T_LAG)
                for t in range(T):
                    extra(("O", t), uses.at(("O", t), b, False, False), uses.bank(("O", t), b, False, False), b - 1, None, None)

            over_rotated(dve, n_batch, body, tail)


def turn_halves(dve, src, to_cos, to_sin, cos, sin, heads, d_head):
    half = d_head // 2
    c = cos.rearrange("p (o a e) -> p o a e", o=1, a=2).to_broadcast([P, heads, 2, half])
    s = sin.rearrange("p (o a e) -> p o a e", o=1, a=2).to_broadcast([P, heads, 2, half])
    return (dve.tensor_tensor(to_cos, src, c, ALU.mult),
            dve.tensor_tensor(to_sin, src[:, :, ::-1, :], s, ALU.mult))


def over_pairs(eng, n, body):
    if n > 2:
        with eng.Fori(0, n // 2 - 1) as i:
            for s in range(2):
                body(2 * i + s, i, s, False)
    for s in range(2):
        body(n - 2 + s, n // 2 - 1, s, s == 1)


def over_ring(eng, n, r, body):
    if n > r:
        with eng.Fori(0, n // r - 1) as i:
            for s in range(r):
                body(r * i + s, i, s, False)
    for s in range(r):
        body(n - r + s, n // r - 1, s, s == r - 1)


def expert_phase(nc, n_batch, x_in, x_norm, consts, gate_w, gate_b, w1, w2, logits_d, sel_d, selT_d, out_d):
    E = gate_w.shape[0]
    HID = w1.shape[2]
    Q = HID // 512
    G = P // E
    NG = n_batch // G
    K8 = 8
    R = 4
    NQ = HID // (P * Q)
    with Phase(nc, "moe") as ph:
        ident = ph.sb("ident", [P, P])
        merged = ph.sb("merged", [P, E, KD, n_batch])
        const_in = ph.sem("const_in")
        w1_s = [ph.sb(f"w1_{i}", [P, KD, HID]) for i in range(2)]
        w2_s = [ph.sb(f"w2_{i}", [P, Q, NQ, D]) for i in range(2)]
        b1_s = [ph.sb(f"b1_{i}", [1, HID]) for i in range(2)]
        w1_in = [ph.sem(f"w1_in{i}") for i in range(2)]
        w2_in = [ph.sem(f"w2_in{i}") for i in range(2)]

        def load_w1(sp, e, s):
            sp.dma_start(w1_s[s][:, :, :], w1[e, 0:D].rearrange("(p k) j -> p k j", k=KD)).then_inc(w1_in[s], 16)
            sp.dma_start(b1_s[s][:, :], w1[e, D:D + 1]).then_inc(w1_in[s], 16)

        def load_w2(sp, e, s):
            sp.dma_start(w2_s[s][:, :, :, :], w2[e, 0:HID].rearrange("(n p q) m -> p n q m", n=Q, q=NQ)).then_inc(w2_in[s], 16)

        with Phase(nc, "route") as r:
            xT_bank = [r.bank(f"X{i}") for i in range(2)]
            L = [r.bank(f"L{i}") for i in range(2)]
            gate = r.sb("gate", [E, D])
            gateT = r.sb("gateT", [P, KD, E])
            gb = r.sb("gb", [E, 1])
            x_t = r.sb("x_t", [P, R, T, D])
            xT = r.sb("xT", [P, 2, KD, S])
            lg = r.sb("lg", [E, 2, S])
            stats = r.sb("stats", [P, T, 6])
            mv = r.sb("mv", [P, T, 2])
            rstd = r.sb("rstd", [P, T])
            minus_half = r.sb("minus_half", [P, T])
            wait_slot = r.sb("wait_slot", [P, 1])
            x_ok = [r.sem(f"x_ok{i}") for i in range(R)]
            ln = r.sem("ln")
            ln_pow = r.sem("ln_pow")
            pool_const = r.sem("pool_const")
            stored = [r.sem(f"stored{i}") for i in range(R)]
            l_stored = [r.sem(f"l_stored{i}") for i in range(2)]
            g_full = r.sem("g_full")
            g_ok = r.sem("g_ok")
            t_full = r.sem("t_full")
            t_ok = r.sem("t_ok")
            l_full = r.sem("l_full")
            l_ok = r.sem("l_ok")
            block = r.ctx.enter_context(nc.Block())

            @block.sync
            def _(sp):
                sp.dma_start(ident[:, :], consts["ident"]).then_inc(const_in, 16)
                sp.dma_start(gate[:, :], gate_w).then_inc(const_in, 16)
                sp.dma_start(gb[:, :], gate_b.rearrange("(e o) -> e o", o=1)).then_inc(const_in, 16)

                def load(n, s):
                    sp.dma_start(x_t[:, s, :, :], x_in[n].rearrange("(t p) d -> p t d", p=P)).then_inc(x_ok[s], 16)

                for s in range(2, R):
                    sp.sem_inc(stored[s], 16)
                for s in range(2):
                    load(s, s)

                def body(n, i, s, last):
                    if not isinstance(n, int) or n + 2 < n_batch:
                        u = (s + 2) % R
                        sp.wait_ge(stored[u], 16 + 16 * i)
                        sp.wait_ge(t_full, 1 + 2 * n)
                        load(n + 2, u)
                    sp.wait_ge(l_ok, 1 + n + 1)
                    sp.dma_start(logits_d[n], lg[:, s % 2, :]).then_inc(l_stored[s % 2], 16)
                over_ring(sp, n_batch, R, body)
                for s in range(R):
                    sp.wait_ge(stored[s], (16 if s >= 2 else 0) + 16 * n_batch // R)
                for s in range(2):
                    sp.wait_ge(l_stored[s], 16 + 16 * n_batch // 2)

            @block.gpsimd
            def _(pool):
                pool.memset(minus_half[:, :], -0.5).then_inc(pool_const, 1)
                pool.wait_ge(pool_const, 1)
                with pool.Fori(0, n_batch) as b:
                    pool.wait_ge(ln, 7 * b + 5)
                    pool.tensor_tensor(rstd[:, :], rstd[:, :], minus_half[:, :], ALU.pow).then_inc(ln_pow, 1)

            @block.vector
            def _(dve):
                dve.sem_inc(l_ok, 1)
                for s in range(2):
                    dve.sem_inc(l_stored[s], 16)
                dve.wait_ge(g_full, 1)
                dve.tensor_copy(gateT[:, :, :].rearrange("p k e -> p (k e)"), L[0][:, 0:KD * E]).then_inc(g_ok, 1)

                def norm(n, i, s):
                    dve.wait_ge(x_ok[s], 16 * i + 16)
                    for t in range(T):
                        dve.bn_stats(stats[:, t, :], x_t[:, s, t, :]).then_inc(ln, 1)
                    dve.wait_ge(ln, 7 * n + 2)
                    dve.memset(wait_slot[:, :], 0.0)
                    for t in range(T):
                        dve.bn_aggr(mv[:, t, :], stats[:, t, :]).then_inc(ln, 1)
                    dve.wait_ge(ln, 7 * n + 4)
                    dve.tensor_scalar(rstd[:, :], mv[:, :, 1], EPS, None, ALU.add).then_inc(ln, 1)
                    dve.wait_ge(ln_pow, n + 1)
                    for t in range(T):
                        dve.tensor_scalar(x_t[:, s, t, :], x_t[:, s, t, :], mv[:, t, 0:1], rstd[:, t:t + 1], ALU.subtract, ALU.mult).then_inc(ln, 1)

                norm(0, 0, 0)

                def body(n, i, s, last):
                    if not last:
                        norm(n + 1, i + (s + 1) // R, (s + 1) % R)
                    dve.wait_ge(l_full, n + 1)
                    dve.wait_ge(l_stored[s % 2], 16 + 16 * (2 * i + s // 2))
                    dve.tensor_scalar(lg[:, s % 2, :], L[s % 2][0:E, 0:S], gb[:, 0:1], None, ALU.add).then_inc(l_ok, 1)
                over_ring(dve, n_batch, R, body)

            @block.tensor
            def _(pe):
                pe.wait_ge(const_in, 48)
                pe.sem_inc(t_full, 1)
                for k in range(KD):
                    mm = pe.transpose(L[0][:, k * E:(k + 1) * E], gate[:, k * P:(k + 1) * P], ident[0:E, 0:E])
                mm.then_inc(g_full, 1)
                pe.wait_ge(g_ok, 1)

                def transposes(n, s):
                    pe.wait_ge(ln, 7 * n + 7)
                    pe.wait_ge(t_ok, 1 + 2 * n)
                    for j in range(2):
                        for kk in range(2):
                            for t in range(T):
                                k = 2 * j + kk
                                mm = pe.transpose(xT_bank[j][:, (kk * T + t) * P:(kk * T + t + 1) * P], x_t[:, s, t, k * P:(k + 1) * P], ident[:, :])
                        mm.then_inc(t_full, 1)

                transposes(0, 0)

                def body(n, i, s, last):
                    pe.wait_ge(t_ok, 1 + 2 * n + 2)
                    pe.wait_ge(l_ok, 1 + n)
                    for k in range(KD):
                        mm = pe.matmul(L[s % 2][0:E, 0:S], gateT[:, k, :], xT[:, s % 2, k, :], start=(k == 0), stop=(k == KD - 1))
                    mm.then_inc(l_full, 1)
                    if not last:
                        transposes(n + 1, (s + 1) % R)
                over_ring(pe, n_batch, R, body)

            @block.scalar
            def _(act):
                act.sem_inc(t_ok, 1)

                def body(n, i, s, last):
                    act.wait_ge(ln, 7 * n + 7)
                    act.dma_start(x_norm[n].rearrange("(t p) d -> p t d", p=P), x_t[:, s, :, :]).then_inc(stored[s], 16)
                    for j in range(2):
                        act.wait_ge(t_full, 1 + 2 * n + j + 1)
                        act.activation(xT[:, s % 2, 2 * j:2 * j + 2, :].rearrange("p k n -> p (k n)"), xT_bank[j][:, :], ACT.Copy).then_inc(t_ok, 1)
                over_ring(act, n_batch, R, body)

        with Phase(nc, "top") as r:
            TB = [r.bank(f"T{i}") for i in range(2)]
            pr = r.sb("pr", [P, NG, S])
            rest = r.sb("rest", [P, NG, S])
            nm = r.sb("nm", [P, NG])
            sm = r.sb("sm", [P, NG])
            top = r.sb("top", [P, NG, K8])
            selT = r.sb("selT", [P, T, NG, P])
            landed, mx, ex, step, full, got, done = (r.sem(n) for n in ("landed", "mx", "ex", "step", "full", "got", "done"))
            block = r.ctx.enter_context(nc.Block())
            NDONE = 1 + NG * G * T

            @block.sync
            def _(sp):
                sp.dma_start(pr[:, :, :], logits_d.rearrange("(g b) e s -> (b e) g s", b=G)).then_inc(landed, 16)
                load_w1(sp, 0, 0)
                sp.wait_ge(step, 5 * NG)
                sp.dma_start(sel_d.rearrange("(g b) e s -> (b e) g s", b=G), pr[:, :, :]).then_inc(done, 16)
                for g in range(NG):
                    sp.wait_ge(got, g + 1)
                    for b in range(G):
                        for t in range(T):
                            sp.dma_start(selT_d[g * G + b, t], selT[:, t, g, b * E:(b + 1) * E]).then_inc(done, 16)
                sp.wait_ge(done, 16 * NDONE)

            @block.vector
            def _(dve):
                dve.wait_ge(landed, 16)
                for g in range(NG):
                    dve.tensor_reduce(nm[:, g:g + 1], pr[:, g, :], AX.X, ALU.max, negate=True).then_inc(mx, 1)
                for g in range(NG):
                    dve.wait_ge(ex, g + 1)
                    dve.reciprocal(sm[:, g:g + 1], sm[:, g:g + 1]).then_inc(step, 1)
                    dve.wait_ge(step, 5 * g + 1)
                    dve.tensor_scalar(pr[:, g, :], pr[:, g, :], sm[:, g:g + 1], None, ALU.mult).then_inc(step, 1)
                    dve.wait_ge(step, 5 * g + 2)
                    dve.max(top[:, g, :], pr[:, g, :]).then_inc(step, 1)
                    dve.wait_ge(step, 5 * g + 3)
                    dve.match_replace(rest[:, g, :], top[:, g, :], pr[:, g, :], 0.0).then_inc(step, 1)
                    dve.wait_ge(step, 5 * g + 4)
                    dve.tensor_tensor(pr[:, g, :], pr[:, g, :], rest[:, g, :], ALU.subtract).then_inc(step, 1)
                for g in range(NG):
                    dve.wait_ge(full, g + 1)
                    dve.tensor_copy(selT[:, :, g, :], TB[g % 2][:, 0:T * P].rearrange("p (t e) -> p t e", t=T)).then_inc(got, 1)

            @block.scalar
            def _(act):
                for g in range(NG):
                    act.wait_ge(mx, g + 1)
                    act.activation(pr[:, g, :], pr[:, g, :], ACT.Exp, bias=nm[:, g:g + 1], accum_out=sm[:, g:g + 1]).then_inc(ex, 1)

            @block.tensor
            def _(pe):
                for g in range(NG):
                    pe.wait_ge(step, 5 * g + 5)
                    if g >= 2:
                        pe.wait_ge(got, g - 1)
                    for t in range(T):
                        mm = pe.transpose(TB[g % 2][:, t * P:(t + 1) * P], pr[:, g, t * P:(t + 1) * P], ident[:, :])
                    mm.then_inc(full, 1)

        with Phase(nc, "merge") as r:
            M = [r.bank(f"M{i}") for i in range(2)]
            xn = r.sb("xn", [P, R, T, D])
            sel = r.sb("sel", [P, R, T, E])
            landed = [r.sem(f"landed{i}") for i in range(R)]
            full, got = r.sem("full"), r.sem("got")
            block = r.ctx.enter_context(nc.Block())

            @block.sync
            def _(sp):
                with sp.Fori(0, n_batch // R) as i:
                    for s in range(R):
                        n = R * i + s
                        sp.wait_ge(full, n + 1)
                        sp.dma_start(xn[:, s, :, :], x_norm[n].rearrange("(t p) d -> p t d", p=P)).then_inc(landed[s], 16)
                        sp.dma_start(sel[:, s, :, :], selT_d[n].rearrange("t p e -> p t e")).then_inc(landed[s], 16)
                load_w2(sp, 0, 0)
                load_w1(sp, 1, 1)
                load_w2(sp, 1, 1)

            @block.tensor
            def _(pe):
                pe.sem_inc(full, R)
                with pe.Fori(0, n_batch // R) as i:
                    for s in range(R):
                        pe.wait_ge(landed[s], 32 * i + 32)
                        pe.wait_ge(got, R * i + s + 1)
                        for k in range(KD):
                            for t in range(T):
                                mm = pe.matmul(M[s % 2][:, k * E:(k + 1) * E], xn[:, s, t, k::KD], sel[:, s, t, :], start=(t == 0), stop=(t == T - 1))
                        mm.then_inc(full, 1)

            @block.vector
            def _(dve):
                dve.sem_inc(got, 2)
                with dve.Fori(0, n_batch // R) as i:
                    for s in range(R):
                        dve.wait_ge(full, R + R * i + s + 1)
                        dve.tensor_copy(merged[:, :, :, bass.ds(R * i + s, 1)].rearrange("p e k o -> p k e o"),
                                        M[s % 2][:, 0:KD * E].rearrange("p (k e o) -> p k e o", k=KD, o=1)).then_inc(got, 1)

        with Phase(nc, "experts") as r:
            HP = [r.bank(f"H{i}") for i in range(2)]
            TP = [r.bank(f"T{i}") for i in range(2)]
            OP = [r.bank(f"O{i}") for i in range(2)]
            tok = r.sb("tok", [P, 2, KD, 32])
            ones = r.sb("ones", [1, 32])
            hid = r.sb("hid", [P, 2, 512])
            hidT = r.sb("hidT", [P, 2, NQ, P])
            o_sb = r.sb("o_sb", [P, 2, D])
            stored = [r.sem(f"stored{i}") for i in range(2)]
            zeroed, tok_ok, h_full, act_ok, ht_full, ht_ok, o_full, o_ok = (
                r.sem(n) for n in ("zeroed", "tok_ok", "h_full", "act_ok", "ht_full", "ht_ok", "o_full", "o_ok"))
            block = r.ctx.enter_context(nc.Block())

            @block.sync
            def _(sp):
                with sp.Fori(1, E // 2) as i:
                    for s in range(2):
                        e = 2 * i + s
                        sp.wait_ge(h_full, e + 1)
                        load_w1(sp, e, s)
                        sp.wait_ge(o_full, e + 1)
                        load_w2(sp, e, s)

            @block.gpsimd
            def _(pool):
                pool.memset(tok[:, :, :, :], 0.0).then_inc(zeroed, 1)
                pool.memset(ones[:, :], 1.0).then_inc(zeroed, 1)

            @block.tensor
            def _(pe):
                pe.sem_inc(h_full, 2)
                pe.sem_inc(o_full, 2)
                pe.sem_inc(ht_full, 2)
                pe.wait_ge(zeroed, 2)

                def hidden(e, i, s):
                    pe.wait_ge(w1_in[s], 32 * i + 32)
                    pe.wait_ge(tok_ok, e + 1)
                    pe.wait_ge(act_ok, e + 1)
                    for k in range(KD):
                        for n in range(Q):
                            pe.matmul(HP[s][32 * n:32 * n + 32, :], tok[:, s, k, :], w1_s[s][:, k, n * 512:(n + 1) * 512],
                                      start=(k == 0), stop=False, tile_position=(0, 32 * n))
                    for n in range(Q):
                        mm = pe.matmul(HP[s][32 * n:32 * n + 32, :], ones[:, :], b1_s[s][:, n * 512:(n + 1) * 512],
                                       start=False, stop=True, tile_position=(0, 32 * n))
                    mm.then_inc(h_full, 1)

                def output(e, i, s):
                    pe.wait_ge(act_ok, e + 3)
                    pe.wait_ge(ht_ok, e + 1)
                    for q in range(NQ):
                        mm = pe.transpose(TP[s][:, q * P:(q + 1) * P], hid[:, s, q::NQ], ident[:, :])
                    mm.then_inc(ht_full, 1)
                    pe.wait_ge(w2_in[s], 16 * i + 16)
                    pe.wait_ge(ht_ok, e + 3)
                    pe.wait_ge(o_ok, e + 1)
                    for q in range(NQ):
                        for n in range(Q):
                            mm = pe.matmul(OP[s][32 * n:32 * n + 32, :], hidT[:, s, q, 32 * n:32 * n + 32], w2_s[s][:, n, q, :],
                                           start=(q == 0), stop=(q == NQ - 1), tile_position=(0, 32 * n))
                    mm.then_inc(o_full, 1)

                with pe.Fori(0, E // 2) as i:
                    for s in range(2):
                        hidden(2 * i + s, i, s)
                        output(2 * i + s, i, s)

            @block.scalar
            def _(act):
                act.sem_inc(act_ok, 2)
                for s in range(2):
                    act.sem_inc(stored[s], 16)
                with act.Fori(0, E // 2) as i:
                    for s in range(2):
                        e = 2 * i + s
                        act.wait_ge(h_full, 2 + e + 1)
                        act.wait_ge(ht_full, e + 1)
                        act.activation(hid[:, s, :], HP[s][:, :], ACT.Gelu).then_inc(act_ok, 1)
                        act.wait_ge(o_ok, 2 + e + 1)
                        for n in range(Q):
                            act.dma_start(out_d[:, n, bass.ds(e, 1), :].rearrange("b o d -> b (o d)"),
                                          o_sb[32 * n:32 * n + n_batch, s, :]).then_inc(stored[s], 16)
                for s in range(2):
                    act.wait_ge(stored[s], 16 + 16 * Q * E // 2)

            @block.vector
            def _(dve):
                for count in (ht_ok, o_ok):
                    dve.sem_inc(count, 2)
                dve.wait_ge(zeroed, 2)

                def tokens(e, s):
                    dve.tensor_copy(tok[:, s, :, 0:n_batch], merged[:, bass.ds(e, 1), :, :].rearrange("p o k b -> p (o k) b")).then_inc(tok_ok, 1)

                with dve.Fori(0, E // 2) as i:
                    for s in range(2):
                        e = 2 * i + s
                        dve.wait_ge(h_full, e + 1)
                        tokens(e, s)
                        dve.wait_ge(ht_full, 2 + e + 1)
                        dve.tensor_copy(hidT[:, s, :, :].rearrange("p q n -> p (q n)"), TP[s][:, :]).then_inc(ht_ok, 1)
                        dve.wait_ge(o_full, 2 + e + 1)
                        dve.wait_ge(stored[s], 16 + 16 * Q * i)
                        dve.tensor_copy(o_sb[:, s, :], OP[s][:, :]).then_inc(o_ok, 1)


def norm_attention_phase(nc, n_batch, x_in, x_out, consts, sel_d, out_d, w2, wq, bq, wk, bk, wv, bv):
    E, Q = out_d.shape[2], out_d.shape[1]
    HID = w2.shape[1] - 1
    NU = 3 * T
    ORDER = [("k", 0), ("v", 0), ("k", 1), ("v", 1), ("q", 0), ("q", 1)]
    NL = 9
    with Phase(nc, "norm") as ph:
        A = [ph.bank(f"A{i}") for i in range(2)]
        B = [ph.bank(f"B{i}") for i in range(2)]
        C = [ph.bank(f"C{i}") for i in range(3)]
        KV = ph.bank("KV")
        ident = ph.sb("ident", [P, P])
        w_stage = ph.sb("w_stage", [P, 3, KD, D])
        w = {n: [ph.sb(f"w{n}{i}", [P, KD, D], F32R) for i in "hl"] for n in "qkv"}
        bias = {n: ph.sb(f"b{n}", [P, D]) for n in "qkv"}
        b2 = ph.sb("b2", [E, D])
        x_ld = ph.sb("x_ld", [P, T, D])
        x3 = ph.sb("x3", [P, 2, T, D])
        xn = ph.sb("xn", [P, T, D])
        sel4 = ph.sb("sel4", [P, S])
        ob = ph.sb("ob", [P, D])
        stats = ph.sb("stats", [P, T, 6])
        mv = ph.sb("mv", [P, T, 2])
        rstd = ph.sb("rstd", [P, T])
        minus_half = ph.sb("minus_half", [P, T])
        wait_slot = ph.sb("wait_slot", [P, 1])
        xT = [ph.sb(f"xT{i}", [P, 2, KD, S], F32R) for i in "hl"]
        t_sb = {n: ph.sb(f"{n}_sb", [P, T, D]) for n in "qkv"}
        prod = ph.sb("prod", [P, T, D])
        squares = ph.sb("squares", [P, D])
        ssq = ph.sb("ssq", [P, 2 * T])
        rn = ph.sb("rn", [P, 2 * T])
        names = ("const_in w_full w_hi w_lo f_in ob_ok sc_full ln ln_pow xT_full hi_ok lo_ok p_full c_ok "
                 "sq_ok prod_ok rn_ok kv_full fin pool_const")
        (const_in, w_full, w_hi, w_lo, f_in, ob_ok, sc_full, ln, ln_pow, xT_full, hi_ok, lo_ok, p_full, c_ok,
         sq_ok, prod_ok, rn_ok, kv_full, fin, pool_const) = (ph.sem(n) for n in names.split())
        w_in = [ph.sem(f"w_in{i}") for i in range(3)]
        stored = [ph.sem(f"stored{i}") for i in range(2)]
        NW = 3 * KD
        block = ph.ctx.enter_context(nc.Block())

        @block.sync
        def _(sp):
            sp.dma_start(ident[:, :], consts["ident"]).then_inc(const_in, 16)
            for n, src in zip("qkv", (bq, bk, bv)):
                sp.dma_start(bias[n][:, :], src.partition_broadcast(P)).then_inc(const_in, 16)
            sp.dma_start(b2[:, :], w2[:, HID, :]).then_inc(const_in, 16)

            def load(n):
                sp.dma_start(x_ld[:, :, :], x_in[n].rearrange("(t p) d -> p t d", p=P)).then_inc(f_in, 16)
                sp.dma_start(ob[:, :], out_d[n].rearrange("n e d -> (n e) d")).then_inc(f_in, 16)
                for j in range(Q):
                    sp.dma_start(sel4[j * E:(j + 1) * E, :], sel_d[n]).then_inc(f_in, 16)

            load(0)
            for i, src in enumerate((wq, wk, wv)):
                sp.dma_start(w_stage[:, i, :, :], src.rearrange("(j p) d -> p j d", p=P)).then_inc(w_in[i], 16)
            sp.wait_ge(ln, 2)
            load(1)

            def body(n, i, s, last):
                if not isinstance(n, int) or n + 2 < n_batch:
                    sp.wait_ge(ln, NL * n + NL + 2)
                    load(n + 2)
                sp.wait_ge(fin, 4 * n + 4)
                sp.dma_start(x_out[n].rearrange("(t p) d -> p t d", p=P), x3[:, s, :, :]).then_inc(stored[s], 16)
            over_pairs(sp, n_batch, body)
            for s in range(2):
                sp.wait_ge(stored[s], 16 + 8 * n_batch)

        @block.gpsimd
        def _(pool):
            pool.memset(minus_half[:, :], -0.5).then_inc(pool_const, 1)
            pool.wait_ge(pool_const, 1)

            def rstds(n):
                pool.wait_ge(ln, NL * n + 7)
                pool.tensor_tensor(rstd[:, :], rstd[:, :], minus_half[:, :], ALU.pow).then_inc(ln_pow, 1)

            rstds(0)

            def body(n, i, s, last):
                for t in range(T):
                    if t == 1 and not last:
                        rstds(n + 1)
                    pool.wait_ge(c_ok, 3 + NU * n + 2 * t + 2)
                    pool.tensor_tensor(prod[:, t, :], t_sb["k"][:, t, :], t_sb["v"][:, t, :], ALU.mult).then_inc(prod_ok, 1)
                for j in range(2):
                    pool.wait_ge(sq_ok, 1 + 4 * n + 2 * j + 2)
                    pool.tensor_tensor(rn[:, 2 * j:2 * j + 2], ssq[:, 2 * j:2 * j + 2], minus_half[:, :], ALU.pow).then_inc(rn_ok, 1)
            over_pairs(pool, n_batch, body)

        @block.tensor
        def _(pe):
            pe.wait_ge(const_in, 16 * 5)

            def spread(n):
                pe.wait_ge(ob_ok, n + 1)
                for t in range(T):
                    mm = pe.matmul(A[t][:, :], sel4[:, t * P:(t + 1) * P], ob[:, :], start=True, stop=True)
                mm.then_inc(sc_full, 1)

            def transposes(n):
                pe.wait_ge(ln, NL * n + NL)
                for j in range(2):
                    for kk in range(2):
                        for t in range(T):
                            k = 2 * j + kk
                            mm = pe.transpose(B[j][:, (kk * T + t) * P:(kk * T + t + 1) * P], xn[:, t, k * P:(k + 1) * P], ident[:, :])
                    mm.then_inc(xT_full, 1)

            spread(0)
            for i in range(3):
                pe.wait_ge(w_in[i], 16)
                for k in range(KD):
                    u = i * KD + k
                    if u >= 2:
                        pe.wait_ge(w_lo, u - 1)
                    for j in range(4):
                        mm = pe.transpose(B[u % 2][:, j * P:(j + 1) * P], w_stage[:, i, j, k * P:(k + 1) * P], ident[:, :])
                    mm.then_inc(w_full, 1)
            pe.wait_ge(w_lo, NW)
            transposes(0)

            def body(n, i, s, last):
                pe.wait_ge(lo_ok, 2 * n + 2)
                for u, (which, t) in enumerate(ORDER):
                    if u == 3 and not last:
                        spread(n + 1)
                    if u == 5 and not last:
                        transposes(n + 1)
                    pe.wait_ge(c_ok, NU * n + u + 1)
                    split_products(pe, C[u % 3][:, :], [
                        ((xT[0][:, s, k, t * P:(t + 1) * P], xT[1][:, s, k, t * P:(t + 1) * P]),
                         (w[which][0][:, k, :], w[which][1][:, k, :])) for k in range(KD)]).then_inc(p_full, 1)
                pe.wait_ge(prod_ok, 2 * n + 2)
                pe.wait_ge(rn_ok, 2 * n + 1)
                for t in range(T):
                    mm = pe.matmul(KV[:, :], rn[:, t:t + 1].to_broadcast([P, P]), prod[:, t, :], start=(t == 0), stop=(t == T - 1))
                mm.then_inc(kv_full, 1)
            over_pairs(pe, n_batch, body)

        @block.scalar
        def _(act):
            act.sem_inc(sq_ok, 1)
            for u in range(NW):
                act.wait_ge(w_full, u + 1)
                act.activation(w["qkv"[u // KD]][0][:, u % KD, :], B[u % 2][:, :], ACT.Copy).then_inc(w_hi, 1)

            def take_hi(n, s):
                for j in range(2):
                    act.wait_ge(xT_full, 2 * n + j + 1)
                    act.activation(xT[0][:, s, 2 * j:2 * j + 2, :].rearrange("p k n -> p (k n)"), B[j][:, :], ACT.Copy).then_inc(hi_ok, 1)

            take_hi(0, 0)

            def body(n, i, s, last):
                for j, (which, t, u) in enumerate((("k", 0, 0), ("k", 1, 2), ("q", 0, 4), ("q", 1, 5))):
                    act.wait_ge(c_ok, 3 + NU * n + u + 1)
                    act.wait_ge(sq_ok, 1 + 4 * n + j)
                    act.activation(squares[:, :], t_sb[which][:, t, :], ACT.Square, accum_out=ssq[:, j:j + 1]).then_inc(sq_ok, 1)
                    if j == 2 and not last:
                        take_hi(n + 1, 1 - s)
            over_pairs(act, n_batch, body)

        @block.vector
        def _(dve):
            dve.sem_inc(c_ok, 3)
            for s in range(2):
                dve.sem_inc(stored[s], 16)
            dve.wait_ge(const_in, 16 * 5)

            def output_bias(n):
                dve.wait_ge(f_in, 16 * (2 + Q) * (n + 1))
                dve.tensor_tensor(ob[0:E, :], ob[0:E, :], b2[:, :], ALU.add).then_inc(ob_ok, 1)

            def residual_and_stats(n, i, s):
                dve.wait_ge(sc_full, n + 1)
                dve.wait_ge(stored[s], 16 + 16 * i)
                for t in range(T):
                    dve.tensor_tensor(x3[:, s, t, :], A[t][:, :], x_ld[:, t, :], ALU.add).then_inc(ln, 1)
                dve.wait_ge(ln, NL * n + 2)
                for t in range(T):
                    dve.bn_stats(stats[:, t, :], x3[:, s, t, :]).then_inc(ln, 1)
                dve.wait_ge(ln, NL * n + 4)
                dve.memset(wait_slot[:, :], 0.0)
                for t in range(T):
                    dve.bn_aggr(mv[:, t, :], stats[:, t, :]).then_inc(ln, 1)
                dve.wait_ge(ln, NL * n + 6)
                dve.tensor_scalar(rstd[:, :], mv[:, :, 1], EPS, None, ALU.add).then_inc(ln, 1)

            def apply_norm(n, s):
                dve.wait_ge(ln_pow, n + 1)
                for t in range(T):
                    dve.tensor_scalar(xn[:, t, :], x3[:, s, t, :], mv[:, t, 0:1], rstd[:, t:t + 1], ALU.subtract, ALU.mult).then_inc(ln, 1)

            def take_lo(n, s):
                for j in range(2):
                    dve.wait_ge(hi_ok, 2 * n + j + 1)
                    dve.tensor_tensor(xT[1][:, s, 2 * j:2 * j + 2, :].rearrange("p k n -> p (k n)"), B[j][:, :],
                                      xT[0][:, s, 2 * j:2 * j + 2, :].rearrange("p k n -> p (k n)"), ALU.subtract).then_inc(lo_ok, 1)

            output_bias(0)
            residual_and_stats(0, 0, 0)
            apply_norm(0, 0)
            for u in range(NW):
                parts = w["qkv"[u // KD]]
                dve.wait_ge(w_hi, u + 1)
                dve.tensor_tensor(parts[1][:, u % KD, :], B[u % 2][:, :], parts[0][:, u % KD, :], ALU.subtract).then_inc(w_lo, 1)
            take_lo(0, 0)

            def body(n, i, s, last):
                for u, (which, t) in enumerate(ORDER):
                    dve.wait_ge(p_full, NU * n + u + 1)
                    dve.tensor_tensor(t_sb[which][:, t, :], C[u % 3][:, :], bias[which][:, :], ALU.add).then_inc(c_ok, 1)
                    if u == 1 and not last:
                        output_bias(n + 1)
                    if u == 2 and not last:
                        residual_and_stats(n + 1, i + s, 1 - s)
                    if u == 3 and not last:
                        apply_norm(n + 1, 1 - s)
                    if u == 4 and not last:
                        take_lo(n + 1, 1 - s)
                dve.wait_ge(kv_full, n + 1)
                dve.wait_ge(rn_ok, 2 * n + 2)
                for t in range(T):
                    dve.tensor_tensor(t_sb["q"][:, t, :], KV[:, :], t_sb["q"][:, t, :], ALU.mult).then_inc(fin, 1)
                dve.wait_ge(fin, 4 * n + 2)
                for t in range(T):
                    dve.scalar_tensor_tensor(x3[:, s, t, :], t_sb["q"][:, t, :], rn[:, T + t:T + t + 1], x3[:, s, t, :], ALU.mult, ALU.add).then_inc(fin, 1)
            over_pairs(dve, n_batch, body)


def fp8_linear_phase(nc, n_batch, x_in, x_out, consts, weight, bias):
    NL = 9
    R = 4
    with Phase(nc, "fp8") as ph:
        B = [ph.bank(f"B{i}", BF16) for i in range(2)]
        O = [ph.bank(f"O{i}") for i in range(4)]
        ident_b = ph.sb("ident_b", [P, P], BF16)
        w_f = ph.sb("w_f", [P, KD, D])
        small = ph.sb("small", [P, KD, D])
        large = ph.sb("large", [P, KD, D])
        w8 = ph.sb("w8", [P, KD, D], FP8)
        wb = ph.sb("wb", [P, KD, D], BF16)
        wT = ph.sb("wT", [P, KD, D], BF16)
        bias_r = ph.sb("bias_r", [P, D])
        x_t = ph.sb("x_t", [P, R, T, D])
        x8 = ph.sb("x8", [P, 2, T, D], FP8)
        xb = ph.sb("xb", [P, 2, T, D], BF16)
        xT = ph.sb("xT", [P, 2, KD, S], BF16)
        y16 = ph.sb("y16", [P, 2, T, D], F16)
        stats = ph.sb("stats", [P, T, 6])
        mv = ph.sb("mv", [P, T, 2])
        rstd = ph.sb("rstd", [P, T])
        minus_half = ph.sb("minus_half", [P, T])
        wait_slot = ph.sb("wait_slot", [P, 1])
        (const_in, w_step, wT_full, wT_ok, ln, ln_pow, xT_full, xT_ok, o_full, y_ok, fin, pool_const, biased) = (
            ph.sem(n) for n in "const_in w_step wT_full wT_ok ln ln_pow xT_full xT_ok o_full y_ok fin pool_const biased".split())
        x_ok = [ph.sem(f"x_ok{i}") for i in range(R)]
        stored = [ph.sem(f"stored{i}") for i in range(R)]
        block = ph.ctx.enter_context(nc.Block())

        @block.sync
        def _(sp):
            sp.dma_start(ident_b[:, :], consts["ident_b"]).then_inc(const_in, 16)
            sp.dma_start(w_f[:, :, :], weight.rearrange("(j p) d -> p j d", p=P)).then_inc(const_in, 16)
            sp.dma_start(bias_r[:, :], bias.partition_broadcast(P)).then_inc(const_in, 16)
            for s in range(2, R):
                sp.sem_inc(stored[s], 16)

            def load(n, s):
                sp.dma_start(x_t[:, s, :, :], x_in[n].rearrange("(t p) d -> p t d", p=P)).then_inc(x_ok[s], 16)

            for s in range(2):
                load(s, s)

            def body(n, i, s, last):
                if not isinstance(n, int) or n + 2 < n_batch:
                    u = (s + 2) % R
                    sp.wait_ge(stored[u], 16 + 16 * i)
                    load(n + 2, u)
                sp.wait_ge(fin, 2 * T + T * n + T)
                sp.dma_start(x_out[n].rearrange("(t p) d -> p t d", p=P), x_t[:, s, :, :]).then_inc(stored[s], 16)
            over_ring(sp, n_batch, R, body)
            for s in range(R):
                sp.wait_ge(stored[s], (16 if s >= 2 else 0) + 16 * n_batch // R)

        @block.gpsimd
        def _(pool):
            pool.sem_inc(fin, 2 * T)
            pool.memset(minus_half[:, :], -0.5).then_inc(pool_const, 1)
            pool.wait_ge(pool_const, 1)
            pool.wait_ge(const_in, 48)

            def rstds(n):
                pool.wait_ge(ln, NL * n + 5)
                pool.tensor_tensor(rstd[:, :], rstd[:, :], minus_half[:, :], ALU.pow).then_inc(ln_pow, 1)

            rstds(0)

            def body(n, i, s, last):
                if not last:
                    rstds(n + 1)
                pool.wait_ge(ln, NL * n + 7)
                for t in range(T):
                    pool.tensor_tensor(x_t[:, s, t, :], x_t[:, s, t, :], bias_r[:, :], ALU.add).then_inc(biased, 1)
                pool.wait_ge(biased, T * n + T)
                for t in range(T):
                    pool.wait_ge(y_ok, 2 * T + T * n + t + 1)
                    pool.tensor_tensor(x_t[:, s, t, :], x_t[:, s, t, :], y16[:, s % 2, t, :], ALU.add).then_inc(fin, 1)
            over_ring(pool, n_batch, R, body)

        @block.tensor
        def _(pe):
            pe.wait_ge(const_in, 48)
            pe.wait_ge(w_step, 9)
            for k in range(KD):
                if k >= 2:
                    pe.wait_ge(wT_ok, k - 1)
                for j in range(4):
                    mm = pe.transpose(B[k % 2][:, j * P:(j + 1) * P], wb[:, j, k * P:(k + 1) * P], ident_b[:, :])
                mm.then_inc(wT_full, 1)
            pe.wait_ge(wT_ok, KD)
            pe.sem_inc(xT_full, 2)

            def transposes(n, s):
                pe.wait_ge(ln, NL * n + 9)
                pe.wait_ge(xT_ok, n + 1)
                for k in range(KD):
                    for t in range(T):
                        mm = pe.transpose(B[s][:, (k * T + t) * P:(k * T + t + 1) * P], xb[:, s, t, k * P:(k + 1) * P], ident_b[:, :])
                mm.then_inc(xT_full, 1)

            transposes(0, 0)

            def body(n, i, s, last):
                pe.wait_ge(xT_ok, n + 3)
                pe.wait_ge(y_ok, T * n + T)
                for t in range(T):
                    for k in range(KD):
                        mm = pe.matmul(O[2 * s + t][:, :], xT[:, s, k, t * P:(t + 1) * P], wT[:, k, :], start=(k == 0), stop=(k == KD - 1))
                mm.then_inc(o_full, 1)
                if not last:
                    transposes(n + 1, 1 - s)
            over_pairs(pe, n_batch, body)

        @block.scalar
        def _(act):
            act.sem_inc(xT_ok, 2)
            for k in range(KD):
                act.wait_ge(wT_full, k + 1)
                act.activation(wT[:, k, :], B[k % 2][:, 0:D], ACT.Copy).then_inc(wT_ok, 1)
            with act.Fori(0, n_batch // 2) as i:
                for s in range(2):
                    n = 2 * i + s
                    act.wait_ge(xT_full, 2 + n + 1)
                    act.activation(xT[:, s, :, :].rearrange("p k n -> p (k n)"), B[s][:, :], ACT.Copy).then_inc(xT_ok, 1)

        @block.vector
        def _(dve):
            dve.wait_ge(const_in, 48)
            steps = [
                lambda: dve.tensor_scalar(small[:, :, :], w_f[:, :, :], 240.0, -240.0, ALU.min, ALU.max),
                lambda: dve.tensor_copy(w8[:, :, :], small[:, :, :], saturate=False),
                lambda: dve.tensor_copy(small[:, :, :], w8[:, :, :]),
                lambda: dve.tensor_scalar(large[:, :, :], w_f[:, :, :], 448.0, -448.0, ALU.min, ALU.max),
            ]
            n = 0
            for step in steps:
                n += 1
                step().then_inc(w_step, 1)
                dve.wait_ge(w_step, n)
            dve.tensor_scalar(w8[:, :, :], large[:, :, :], 0.5, None, ALU.mult, saturate=False).then_inc(w_step, 1)
            dve.wait_ge(w_step, 5)
            dve.scalar_tensor_tensor(large[:, :, :], w8[:, :, :], 2.0, small[:, :, :], ALU.mult, ALU.subtract).then_inc(w_step, 1)
            dve.tensor_tensor(w_f[:, :, :], w_f[:, :, :], w_f[:, :, :], ALU.mult).then_inc(w_step, 1)
            dve.wait_ge(w_step, 7)
            dve.tensor_scalar(w_f[:, :, :], w_f[:, :, :], 256.0, None, ALU.is_ge).then_inc(w_step, 1)
            dve.wait_ge(w_step, 8)
            dve.tensor_tensor(large[:, :, :], large[:, :, :], w_f[:, :, :], ALU.mult).then_inc(pool_const, 1)
            dve.wait_ge(pool_const, 2)
            dve.tensor_tensor(wb[:, :, :], large[:, :, :], small[:, :, :], ALU.add).then_inc(w_step, 1)
            dve.sem_inc(y_ok, 2 * T)

            def norm(n, i, s):
                dve.wait_ge(x_ok[s], 16 * i + 16)
                for t in range(T):
                    dve.bn_stats(stats[:, t, :], x_t[:, s, t, :]).then_inc(ln, 1)
                dve.wait_ge(ln, NL * n + 2)
                dve.memset(wait_slot[:, :], 0.0)
                for t in range(T):
                    dve.bn_aggr(mv[:, t, :], stats[:, t, :]).then_inc(ln, 1)
                dve.wait_ge(ln, NL * n + 4)
                dve.tensor_scalar(rstd[:, :], mv[:, :, 1], EPS, None, ALU.add).then_inc(ln, 1)
                dve.wait_ge(ln_pow, n + 1)
                dve.memset(wait_slot[:, :], 0.0)
                for t in range(T):
                    dve.tensor_scalar(x8[:, s % 2, t, :], x_t[:, s, t, :], mv[:, t, 0:1], rstd[:, t:t + 1], ALU.subtract, ALU.mult, saturate=False).then_inc(ln, 1)
                dve.wait_ge(ln, NL * n + 7)
                dve.memset(wait_slot[:, :], 0.0)
                for t in range(T):
                    dve.tensor_copy(xb[:, s % 2, t, :], x8[:, s % 2, t, :]).then_inc(ln, 1)

            norm(0, 0, 0)

            def body(n, i, s, last):
                if not last:
                    norm(n + 1, i + (s + 1) // R, (s + 1) % R)
                dve.wait_ge(o_full, n + 1)
                dve.wait_ge(fin, T * n + T)
                for t in range(T):
                    dve.tensor_copy(y16[:, s % 2, t, :], O[2 * (s % 2) + t][:, :]).then_inc(y_ok, 1)
            over_ring(dve, n_batch, R, body)


def constants():
    bf16 = np.dtype("bfloat16")
    pos = np.arange(S, dtype=np.float32)
    half = 32
    freq = np.power(np.float32(ROPE_BASE), np.arange(half, dtype=np.float32) / np.float32(half)).astype(np.float32)
    angles = pos[:, None] / np.concatenate([freq, freq])[None, :]
    sign = np.concatenate([-np.ones(half), np.ones(half)]).astype(np.float32)

    def rows(a):
        return np.ascontiguousarray(a.reshape(T, P, -1).transpose(1, 0, 2))
    return {
        "ident": np.eye(P, dtype=np.float32),
        "ident_b": np.eye(P).astype(bf16),
        "mask_b": np.triu(np.full((P, P), -1e9), 1).astype(bf16),
        "cos": rows(np.cos(angles).astype(np.float32)),
        "sin": rows((np.sin(angles) * sign).astype(np.float32)),
    }


def decoder(nc, a, c, out, n_batch):
    def scratch(name, shape):
        return nc.dram_tensor(name, shape, F32, kind="Internal").ap()
    def self0(x, y):
        attention_phase(nc, "self0", n_batch, x, y, c, a["L0_attn_W_Q"], a["L0_attn_W_K"], a["L0_attn_W_V"], a["L0_attn_W_O"],
                        64, True, True, bq=a["L0_attn_b_Q"], bk=a["L0_attn_b_K"], bv=a["L0_attn_b_V"], bo=a["L0_attn_b_O"],
                        rope=(c["cos"], c["sin"]))

    def cross0(x, y):
        attention_phase(nc, "cross0", n_batch, x, y, c, a["L0_xattn_Wq"], a["L0_xattn_Wk"], a["L0_xattn_Wv"], a["L0_xattn_Wo"],
                        32, True, False, ctx=a["ctx_1024"])

    def cross1(x, y):
        attention_phase(nc, "cross1", n_batch, x, y, c, a["L1_xattn_Wq"], a["L1_xattn_Wk"], a["L1_xattn_Wv"], a["L1_xattn_Wo"],
                        32, False, False, ctx=a["ctx_1024"], bq=a["L1_xattn_bq"], bk=a["L1_xattn_bk"], bv=a["L1_xattn_bv"],
                        bo=a["L1_xattn_bo"])

    E, HID = a["L0_ffn_w1"].shape[0], a["L0_ffn_w1"].shape[2]
    logits_d, sel_d = scratch("logits", (n_batch, E, S)), scratch("sel", (n_batch, E, S))
    selT_d = scratch("selT", (n_batch, T, P, E))
    out_d = scratch("experts_out", (n_batch, HID // 512, E, D))
    x_norm = scratch("x_norm", (n_batch, S, D))

    def experts(x):
        expert_phase(nc, n_batch, x, x_norm, c, a["L0_ffn_gate_w"], a["L0_ffn_gate_b"], a["L0_ffn_w1"], a["L0_ffn_w2"],
                     logits_d, sel_d, selT_d, out_d)

    def norm1(x, y):
        norm_attention_phase(nc, n_batch, x, y, c, sel_d, out_d, a["L0_ffn_w2"], a["L1_attn_Wq"], a["L1_attn_bq"],
                             a["L1_attn_Wk"], a["L1_attn_bk"], a["L1_attn_Wv"], a["L1_attn_bv"])

    def fp8(x, y):
        fp8_linear_phase(nc, n_batch, x, y, c, a["L1_ffn_weight"], a["L1_ffn_bias"])

    x1, x2, x4, x5 = (scratch(f"x{i}", (n_batch, S, D)) for i in (1, 2, 4, 5))
    self0(a["x"], x1)
    cross0(x1, x2)
    experts(x2)
    norm1(x2, x4)
    cross1(x4, x5)
    fp8(x5, out)

def kernel(**inputs):
    import concourse.bacc as bacc
    from concourse.bass_utils import run_bass_kernel_spmd

    nc = bacc.Bacc("TRN2", target_bir_lowering=False, num_devices=1)
    arrays, a, c = {}, {}, {}
    for group, made in ((a, inputs), (c, constants())):
        for name, value in made.items():
            value = np.ascontiguousarray(value)
            arrays[f"in_{name}"] = value
            group[name] = nc.dram_tensor(f"in_{name}", value.shape, mybir.dt.from_np(value.dtype), kind="ExternalInput").ap()
    n_batch = a["x"].shape[0]
    out = nc.dram_tensor("out_x", (n_batch, S, D), F32, kind="ExternalOutput").ap()
    decoder(nc, a, c, out, n_batch)
    r = run_bass_kernel_spmd(nc, [arrays], core_ids=[0])
    return r.results[0]["out_x"]
```
